# Optimizing a Trainium2 kernel written in Bass

```python
import numpy as np
import jax
import jax.numpy as jnp

def _softmax(x, axis=-1):
    return jax.nn.softmax(x, axis=axis)

def _gelu(x):
    return jax.nn.gelu(x, approximate=True)

def _silu(x):
    return jax.nn.silu(x)

def _sigmoid(x):
    return jax.nn.sigmoid(x)

def _layernorm(x, axis=-1, eps=1e-05):
    m = jnp.mean(x, axis=axis, keepdims=True)
    v = jnp.var(x, axis=axis, keepdims=True)
    return (x - m) / jnp.sqrt(v + eps)

def _scatter_add(tgt, idx, src, axis=0):
    return tgt.at[idx].add(src)

def _segment_sum(src, seg, n):
    return jax.ops.segment_sum(src, seg, n)
kernel_name = 'mk_sandwich_d2_jaxref_r8_b5b8ac'

def setup_inputs(seed: int=0):
    np.random.seed(seed)
    _w = jnp.asarray

    def _L0_attn_setup():
        import jax, jax.numpy as jnp
        import numpy as np
        HIDDEN = 128
        HEADS = 16
        HEAD_DIM = HIDDEN // HEADS
        SCALE = HEAD_DIM ** (-0.5)
        key = jax.random.key(seed)
        ks = jax.random.split(key, 9)
        init = 1.0 / np.sqrt(HIDDEN)
        hidden_states = jax.random.normal(ks[0], (8, 128, HIDDEN), dtype=jnp.float32)

        def lin(k):
            kw, kb = jax.random.split(k)
            W = jax.random.uniform(kw, (HIDDEN, HIDDEN), jnp.float32, -init, init)
            b = jax.random.uniform(kb, (HIDDEN,), jnp.float32, -init, init)
            return (W, b)
        Wq, bq = lin(ks[1])
        Wk, bk = lin(ks[2])
        Wv, bv = lin(ks[3])
        Wo, bo = lin(ks[4])
        return {'hidden_states': hidden_states, 'Wq': Wq, 'bq': bq, 'Wk': Wk, 'bk': bk, 'Wv': Wv, 'bv': bv, 'Wo': Wo, 'bo': bo}
    _L0_attn_in = _L0_attn_setup()

    def _L0_ffn_setup():
        import jax, jax.numpy as jnp
        import numpy as np
        DIM = 128
        DEPTH = 2
        HEADS = 8
        DIM_HEAD = 64
        WINDOW = 64
        INNER = HEADS * DIM_HEAD
        HID = int(DIM * 4 * 2 / 3)
        B, N = (2, 1024)
        QK_SCALE = 8.0

        def shift_token(t):
            t1, t2 = jnp.split(t, 2, axis=-1)
            t2 = jnp.pad(t2, ((0, 0), (1, 0), (0, 0)))[:, :-1]
            return jnp.concatenate([t1, t2], axis=-1)

        def l2norm(t):
            return t / jnp.clip(jnp.linalg.norm(t, axis=-1, keepdims=True), 1e-12)

        def rotate_half(x):
            x1, x2 = jnp.split(x, 2, axis=-1)
            return jnp.concatenate([-x2, x1], axis=-1)

        def rotary_xpos(q, k):
            n = q.shape[-2]
            half_idx = jnp.arange(0, DIM_HEAD, 2, dtype=jnp.float32)
            inv_freq = 1.0 / 10000.0 ** (half_idx / DIM_HEAD)
            t = jnp.arange(n, dtype=jnp.float32)
            freqs = t[:, None] * inv_freq[None, :]
            freqs = jnp.concatenate([freqs, freqs], axis=-1)
            base = (half_idx + 0.4 * DIM_HEAD) / (1.4 * DIM_HEAD)
            power = (t - n // 2) / float(WINDOW // 2)
            scale = base[None, :] ** power[:, None]
            scale = jnp.concatenate([scale, scale], axis=-1)
            cos, sin = (jnp.cos(freqs), jnp.sin(freqs))
            q = q * cos * scale + rotate_half(q) * sin * scale
            k = k * cos / scale + rotate_half(k) * sin / scale
            return (q, k)

        def local_attention(q, k, v):
            b, h, n, d = q.shape
            w = n // WINDOW
            bq = q.reshape(b, h, w, WINDOW, d) * QK_SCALE
            bk = k.reshape(b, h, w, WINDOW, d)
            bv = v.reshape(b, h, w, WINDOW, d)

            def look_around(t):
                p = jnp.pad(t, ((0, 0), (0, 0), (1, 0), (0, 0), (0, 0)))
                return jnp.concatenate([p[:, :, :w], p[:, :, 1:]], axis=3)
            bk, bv = (look_around(bk), look_around(bv))
            bt = jnp.arange(n).reshape(w, WINDOW)
            btp = jnp.pad(bt, ((1, 0), (0, 0)), constant_values=-1)
            btk = jnp.concatenate([btp[:w], btp[1:]], axis=1)
            sim = jnp.einsum('bhwid,bhwjd->bhwij', bq, bk)
            i = bt[:, :, None]
            j = btk[:, None, :]
            mask = (i < j) | (i > j + WINDOW) | (j == -1)
            sim = jnp.where(mask, -jnp.finfo(sim.dtype).max, sim)
            attn = jax.nn.softmax(sim, axis=-1)
            out = jnp.einsum('bhwij,bhwjd->bhwid', attn, bv)
            return out.reshape(b, h, n, d)

        def _layer(x, wqkv, qs, ksc, wo, lg, lb, w1, b1, w2, b2):
            b, n, _ = x.shape
            h = shift_token(x)
            qkv = h @ wqkv
            q, k, v = jnp.split(qkv, 3, axis=-1)
            to_heads = lambda t: t.reshape(b, n, HEADS, DIM_HEAD).transpose(0, 2, 1, 3)
            q, k, v = (to_heads(q), to_heads(k), to_heads(v))
            q = l2norm(q) * qs
            k = l2norm(k) * ksc
            q, k = rotary_xpos(q, k)
            o = local_attention(q, k, v)
            o = o.transpose(0, 2, 1, 3).reshape(b, n, INNER)
            x = x + o @ wo
            h = shift_token(x)
            mu = h.mean(-1, keepdims=True)
            var = h.var(-1, keepdims=True)
            h = (h - mu) / jnp.sqrt(var + 1e-05) * lg + lb
            h = h @ w1 + b1
            a, g = jnp.split(h, 2, axis=-1)
            h = a * jax.nn.gelu(g, approximate=False)
            x = x + h @ w2 + b2
            return x
        key = jax.random.key(seed)
        ks = jax.random.split(key, 6)
        return {'x': jax.random.normal(ks[0], (B, N, DIM), jnp.float32), 'wqkv': jax.random.normal(ks[1], (DEPTH, DIM, 3 * INNER), jnp.float32) * 0.02, 'q_scale': jnp.ones((DEPTH, DIM_HEAD), jnp.float32), 'k_scale': jnp.ones((DEPTH, DIM_HEAD), jnp.float32), 'wo': jax.random.normal(ks[2], (DEPTH, INNER, DIM), jnp.float32) * 0.02, 'ln_g': jnp.ones((DEPTH, DIM), jnp.float32), 'ln_b': jnp.zeros((DEPTH, DIM), jnp.float32), 'w1': jax.random.normal(ks[3], (DEPTH, DIM, 2 * HID), jnp.float32) * 0.02, 'b1': jnp.zeros((DEPTH, 2 * HID), jnp.float32), 'w2': jax.random.normal(ks[4], (DEPTH, HID, DIM), jnp.float32) * 0.02, 'b2': jnp.zeros((DEPTH, DIM), jnp.float32)}
    _L0_ffn_in = _L0_ffn_setup()

    def _L1_attn_setup():
        import jax, jax.numpy as jnp
        import numpy as np
        CHUNK = 32

        def l2norm(x, eps=1e-06):
            return x * jax.lax.rsqrt(jnp.sum(x * x, axis=-1, keepdims=True) + eps)

        def rmsnorm(x, w, eps=1e-05):
            return x * jax.lax.rsqrt(jnp.mean(x * x, axis=-1, keepdims=True) + eps) * w

        def short_conv(x, w):
            K = w.shape[1]
            l = x.shape[1]
            xp = jnp.pad(x, ((0, 0), (K - 1, 0), (0, 0)))
            y = sum((xp[:, t:t + l, :] * w[:, t] for t in range(K)))
            return y * jax.nn.sigmoid(y)

        def build_sin_cos(l, d):
            inv_freq = 1.0 / 10000.0 ** (jnp.arange(0, d, 2, dtype=jnp.float32) / d)
            ang = jnp.arange(l, dtype=jnp.float32)[:, None] * inv_freq[None, :]
            return (jnp.sin(ang), jnp.cos(ang))

        def apply_rotary(x, sin, cos):
            s = sin[None, :, None, :]
            c = cos[None, :, None, :]
            x1, x2 = (x[..., ::2], x[..., 1::2])
            return jnp.concatenate([x1 * c - x2 * s, x1 * s + x2 * c], axis=-1)

        def delta_rule_chunkwise(q, k, v, beta, gamma, chunk=CHUNK):
            b, h, l, dk = q.shape
            dv = v.shape[-1]
            n = l // chunk
            q = l2norm(q)
            k = l2norm(k)
            v = v * beta[..., None]
            kb = k * beta[..., None]
            rs = lambda x: x.reshape(b, h, n, chunk, -1)
            q, k, v, kb = (rs(q), rs(k), rs(v), rs(kb))
            gm = gamma.reshape(b, h, n, chunk).mean(-1)
            idx = jnp.arange(chunk)
            strict_lower = (idx[:, None] > idx[None, :]).astype(q.dtype)
            A = -(kb @ jnp.swapaxes(k, -1, -2)) * strict_lower
            for i in range(1, chunk):
                A = A.at[..., i, :i].add(jnp.einsum('...j,...jc->...c', A[..., i, :i], A[..., :i, :i]))
            T = A + jnp.eye(chunk, dtype=A.dtype)
            u = T @ v
            w = T @ kb
            tril_inc = (idx[:, None] >= idx[None, :]).astype(q.dtype)

            def step(S, xs):
                qi, ki, ui, wi, g = xs
                attn = qi @ jnp.swapaxes(ki, -1, -2) * tril_inc
                u_t = ui - wi @ S
                o_i = qi @ S + attn @ u_t
                S_new = g[..., None, None] * S + jnp.einsum('bhck,bhcv->bhkv', ki, u_t)
                return (S_new, o_i)
            mv = lambda x: jnp.moveaxis(x, 2, 0)
            S0 = jnp.zeros((b, h, dk, dv), dtype=q.dtype)
            S, o = jax.lax.scan(step, S0, (mv(q), mv(k), mv(u), mv(w), mv(gm)))
            o = jnp.moveaxis(o, 0, 2).reshape(b, h, l, dv)
            return (o, S)

        def fractal_mixer(x, conv_w):
            out = 2.0 * x
            l = x.shape[1]
            for i in range(conv_w.shape[0]):
                dil = 2 ** i
                x_shift = jnp.pad(x, ((0, 0), (dil, 0), (0, 0)))[:, :l, :]
                out = out + x_shift * conv_w[i, :, 0] + x * conv_w[i, :, 1]
            return out
        key = jax.random.key(seed)
        ks = jax.random.split(key, 16)
        B, L, D, H = (2, 512, 128, 4)
        hd = D // H
        s = 0.02
        return {'hidden_states': jax.random.normal(ks[0], (B, L, D), jnp.float32), 'Wq': jax.random.normal(ks[1], (D, D), jnp.float32) * s, 'Wk': jax.random.normal(ks[2], (D, D), jnp.float32) * s, 'Wv': jax.random.normal(ks[3], (D, D), jnp.float32) * s, 'Wb': jax.random.normal(ks[4], (D, H), jnp.float32) * s, 'Wgamma': jax.random.normal(ks[5], (D, H), jnp.float32) * s, 'rot_logit': jnp.zeros((H,), jnp.float32), 'conv_q': jax.random.normal(ks[6], (D, 4), jnp.float32) * 0.1, 'conv_k': jax.random.normal(ks[7], (D, 4), jnp.float32) * 0.1, 'conv_v': jax.random.normal(ks[8], (D, 4), jnp.float32) * 0.1, 'o_norm_w': jnp.ones((hd,), jnp.float32), 'Wo': jax.random.normal(ks[9], (D, D), jnp.float32) * s, 'frac_conv_w': jax.random.normal(ks[10], (4, D, 2), jnp.float32) * 0.02, 'frac_gate_w': jax.random.normal(ks[11], (D, 1), jnp.float32) * s, 'frac_gate_b': jnp.full((1,), -1.0, jnp.float32), 'mixer_norm_w': jnp.ones((D,), jnp.float32)}
    _L1_attn_in = _L1_attn_setup()

    def _L1_ffn_setup():
        import jax, jax.numpy as jnp
        import numpy as np
        DIM = 128
        HIDDEN = 384
        SCALE = 1.0 / 127.0

        def _dequant(w_int, dtype):
            return w_int.astype(dtype) * jnp.asarray(SCALE, dtype)
        key = jax.random.key(seed)
        k_x, k_g, k_u, k_d = jax.random.split(key, 4)
        x = jax.random.normal(k_x, (4, 256, DIM), dtype=jnp.float32)
        w_gate = jax.random.randint(k_g, (HIDDEN, DIM), -127, 128, dtype=jnp.int32)
        w_up = jax.random.randint(k_u, (HIDDEN, DIM), -127, 128, dtype=jnp.int32)
        w_down = jax.random.randint(k_d, (DIM, HIDDEN), -127, 128, dtype=jnp.int32)
        return {'x': x, 'w_gate': w_gate, 'w_up': w_up, 'w_down': w_down}
    _L1_ffn_in = _L1_ffn_setup()
    _d = {'L0_attn_hidden_states': _L0_attn_in['hidden_states'], 'L0_attn_Wq': _L0_attn_in['Wq'], 'L0_attn_bq': _L0_attn_in['bq'], 'L0_attn_Wk': _L0_attn_in['Wk'], 'L0_attn_bk': _L0_attn_in['bk'], 'L0_attn_Wv': _L0_attn_in['Wv'], 'L0_attn_bv': _L0_attn_in['bv'], 'L0_attn_Wo': _L0_attn_in['Wo'], 'L0_attn_bo': _L0_attn_in['bo'], 'L0_ffn_wqkv': _L0_ffn_in['wqkv'], 'L0_ffn_q_scale': _L0_ffn_in['q_scale'], 'L0_ffn_k_scale': _L0_ffn_in['k_scale'], 'L0_ffn_wo': _L0_ffn_in['wo'], 'L0_ffn_ln_g': _L0_ffn_in['ln_g'], 'L0_ffn_ln_b': _L0_ffn_in['ln_b'], 'L0_ffn_w1': _L0_ffn_in['w1'], 'L0_ffn_b1': _L0_ffn_in['b1'], 'L0_ffn_w2': _L0_ffn_in['w2'], 'L0_ffn_b2': _L0_ffn_in['b2'], 'L1_attn_Wq': _L1_attn_in['Wq'], 'L1_attn_Wk': _L1_attn_in['Wk'], 'L1_attn_Wv': _L1_attn_in['Wv'], 'L1_attn_Wb': _L1_attn_in['Wb'], 'L1_attn_Wgamma': _L1_attn_in['Wgamma'], 'L1_attn_rot_logit': _L1_attn_in['rot_logit'], 'L1_attn_conv_q': _L1_attn_in['conv_q'], 'L1_attn_conv_k': _L1_attn_in['conv_k'], 'L1_attn_conv_v': _L1_attn_in['conv_v'], 'L1_attn_o_norm_w': _L1_attn_in['o_norm_w'], 'L1_attn_Wo': _L1_attn_in['Wo'], 'L1_attn_frac_conv_w': _L1_attn_in['frac_conv_w'], 'L1_attn_frac_gate_w': _L1_attn_in['frac_gate_w'], 'L1_attn_frac_gate_b': _L1_attn_in['frac_gate_b'], 'L1_attn_mixer_norm_w': _L1_attn_in['mixer_norm_w'], 'L1_ffn_w_gate': _L1_ffn_in['w_gate'], 'L1_ffn_w_up': _L1_ffn_in['w_up'], 'L1_ffn_w_down': _L1_ffn_in['w_down']}
    _x0 = _d['L0_attn_hidden_states']
    _d['L0_attn_hidden_states'] = jax.random.normal(jax.random.fold_in(jax.random.key(seed), 1), (8, 512, 128), dtype=_x0.dtype)
    del _x0
    return _d

def reference(L0_attn_hidden_states, L0_attn_Wq, L0_attn_bq, L0_attn_Wk, L0_attn_bk, L0_attn_Wv, L0_attn_bv, L0_attn_Wo, L0_attn_bo, L0_ffn_wqkv, L0_ffn_q_scale, L0_ffn_k_scale, L0_ffn_wo, L0_ffn_ln_g, L0_ffn_ln_b, L0_ffn_w1, L0_ffn_b1, L0_ffn_w2, L0_ffn_b2, L1_attn_Wq, L1_attn_Wk, L1_attn_Wv, L1_attn_Wb, L1_attn_Wgamma, L1_attn_rot_logit, L1_attn_conv_q, L1_attn_conv_k, L1_attn_conv_v, L1_attn_o_norm_w, L1_attn_Wo, L1_attn_frac_conv_w, L1_attn_frac_gate_w, L1_attn_frac_gate_b, L1_attn_mixer_norm_w, L1_ffn_w_gate, L1_ffn_w_up, L1_ffn_w_down):

    def _L0_attn_ref(hidden_states, Wq, bq, Wk, bk, Wv, bv, Wo, bo):
        import jax, jax.numpy as jnp
        import numpy as np
        HIDDEN = 128
        HEADS = 16
        HEAD_DIM = HIDDEN // HEADS
        SCALE = HEAD_DIM ** (-0.5)
        b, s, d = hidden_states.shape
        q = (hidden_states @ Wq.T + bq).reshape(b, s, HEADS, HEAD_DIM)
        k = (hidden_states @ Wk.T + bk).reshape(b, s, HEADS, HEAD_DIM)
        v = (hidden_states @ Wv.T + bv).reshape(b, s, HEADS, HEAD_DIM)
        q = q * SCALE
        scores = jnp.einsum('bqhd,bkhd->bhqk', q, k)
        probs = jax.nn.softmax(scores.astype(jnp.float32), axis=-1).astype(scores.dtype)
        out = jnp.einsum('bhqk,bkhd->bqhd', probs, v).reshape(b, s, d)
        return out @ Wo.T + bo

    def _L0_ffn_ref(x, wqkv, q_scale, k_scale, wo, ln_g, ln_b, w1, b1, w2, b2):
        import jax, jax.numpy as jnp
        import numpy as np
        DIM = 128
        DEPTH = 2
        HEADS = 8
        DIM_HEAD = 64
        WINDOW = 64
        INNER = HEADS * DIM_HEAD
        HID = int(DIM * 4 * 2 / 3)
        B, N = (2, 1024)
        QK_SCALE = 8.0

        def shift_token(t):
            t1, t2 = jnp.split(t, 2, axis=-1)
            t2 = jnp.pad(t2, ((0, 0), (1, 0), (0, 0)))[:, :-1]
            return jnp.concatenate([t1, t2], axis=-1)

        def l2norm(t):
            return t / jnp.clip(jnp.linalg.norm(t, axis=-1, keepdims=True), 1e-12)

        def rotate_half(x):
            x1, x2 = jnp.split(x, 2, axis=-1)
            return jnp.concatenate([-x2, x1], axis=-1)

        def rotary_xpos(q, k):
            n = q.shape[-2]
            half_idx = jnp.arange(0, DIM_HEAD, 2, dtype=jnp.float32)
            inv_freq = 1.0 / 10000.0 ** (half_idx / DIM_HEAD)
            t = jnp.arange(n, dtype=jnp.float32)
            freqs = t[:, None] * inv_freq[None, :]
            freqs = jnp.concatenate([freqs, freqs], axis=-1)
            base = (half_idx + 0.4 * DIM_HEAD) / (1.4 * DIM_HEAD)
            power = (t - n // 2) / float(WINDOW // 2)
            scale = base[None, :] ** power[:, None]
            scale = jnp.concatenate([scale, scale], axis=-1)
            cos, sin = (jnp.cos(freqs), jnp.sin(freqs))
            q = q * cos * scale + rotate_half(q) * sin * scale
            k = k * cos / scale + rotate_half(k) * sin / scale
            return (q, k)

        def local_attention(q, k, v):
            b, h, n, d = q.shape
            w = n // WINDOW
            bq = q.reshape(b, h, w, WINDOW, d) * QK_SCALE
            bk = k.reshape(b, h, w, WINDOW, d)
            bv = v.reshape(b, h, w, WINDOW, d)

            def look_around(t):
                p = jnp.pad(t, ((0, 0), (0, 0), (1, 0), (0, 0), (0, 0)))
                return jnp.concatenate([p[:, :, :w], p[:, :, 1:]], axis=3)
            bk, bv = (look_around(bk), look_around(bv))
            bt = jnp.arange(n).reshape(w, WINDOW)
            btp = jnp.pad(bt, ((1, 0), (0, 0)), constant_values=-1)
            btk = jnp.concatenate([btp[:w], btp[1:]], axis=1)
            sim = jnp.einsum('bhwid,bhwjd->bhwij', bq, bk)
            i = bt[:, :, None]
            j = btk[:, None, :]
            mask = (i < j) | (i > j + WINDOW) | (j == -1)
            sim = jnp.where(mask, -jnp.finfo(sim.dtype).max, sim)
            attn = jax.nn.softmax(sim, axis=-1)
            out = jnp.einsum('bhwij,bhwjd->bhwid', attn, bv)
            return out.reshape(b, h, n, d)

        def _layer(x, wqkv, qs, ksc, wo, lg, lb, w1, b1, w2, b2):
            b, n, _ = x.shape
            h = shift_token(x)
            qkv = h @ wqkv
            q, k, v = jnp.split(qkv, 3, axis=-1)
            to_heads = lambda t: t.reshape(b, n, HEADS, DIM_HEAD).transpose(0, 2, 1, 3)
            q, k, v = (to_heads(q), to_heads(k), to_heads(v))
            q = l2norm(q) * qs
            k = l2norm(k) * ksc
            q, k = rotary_xpos(q, k)
            o = local_attention(q, k, v)
            o = o.transpose(0, 2, 1, 3).reshape(b, n, INNER)
            x = x + o @ wo
            h = shift_token(x)
            mu = h.mean(-1, keepdims=True)
            var = h.var(-1, keepdims=True)
            h = (h - mu) / jnp.sqrt(var + 1e-05) * lg + lb
            h = h @ w1 + b1
            a, g = jnp.split(h, 2, axis=-1)
            h = a * jax.nn.gelu(g, approximate=False)
            x = x + h @ w2 + b2
            return x
        for l in range(DEPTH):
            x = _layer(x, wqkv[l], q_scale[l], k_scale[l], wo[l], ln_g[l], ln_b[l], w1[l], b1[l], w2[l], b2[l])
        return x

    def _L1_attn_ref(hidden_states, Wq, Wk, Wv, Wb, Wgamma, rot_logit, conv_q, conv_k, conv_v, o_norm_w, Wo, frac_conv_w, frac_gate_w, frac_gate_b, mixer_norm_w):
        import jax, jax.numpy as jnp
        import numpy as np
        CHUNK = 32

        def l2norm(x, eps=1e-06):
            return x * jax.lax.rsqrt(jnp.sum(x * x, axis=-1, keepdims=True) + eps)

        def rmsnorm(x, w, eps=1e-05):
            return x * jax.lax.rsqrt(jnp.mean(x * x, axis=-1, keepdims=True) + eps) * w

        def short_conv(x, w):
            K = w.shape[1]
            l = x.shape[1]
            xp = jnp.pad(x, ((0, 0), (K - 1, 0), (0, 0)))
            y = sum((xp[:, t:t + l, :] * w[:, t] for t in range(K)))
            return y * jax.nn.sigmoid(y)

        def build_sin_cos(l, d):
            inv_freq = 1.0 / 10000.0 ** (jnp.arange(0, d, 2, dtype=jnp.float32) / d)
            ang = jnp.arange(l, dtype=jnp.float32)[:, None] * inv_freq[None, :]
            return (jnp.sin(ang), jnp.cos(ang))

        def apply_rotary(x, sin, cos):
            s = sin[None, :, None, :]
            c = cos[None, :, None, :]
            x1, x2 = (x[..., ::2], x[..., 1::2])
            return jnp.concatenate([x1 * c - x2 * s, x1 * s + x2 * c], axis=-1)

        def delta_rule_chunkwise(q, k, v, beta, gamma, chunk=CHUNK):
            b, h, l, dk = q.shape
            dv = v.shape[-1]
            n = l // chunk
            q = l2norm(q)
            k = l2norm(k)
            v = v * beta[..., None]
            kb = k * beta[..., None]
            rs = lambda x: x.reshape(b, h, n, chunk, -1)
            q, k, v, kb = (rs(q), rs(k), rs(v), rs(kb))
            gm = gamma.reshape(b, h, n, chunk).mean(-1)
            idx = jnp.arange(chunk)
            strict_lower = (idx[:, None] > idx[None, :]).astype(q.dtype)
            A = -(kb @ jnp.swapaxes(k, -1, -2)) * strict_lower
            for i in range(1, chunk):
                A = A.at[..., i, :i].add(jnp.einsum('...j,...jc->...c', A[..., i, :i], A[..., :i, :i]))
            T = A + jnp.eye(chunk, dtype=A.dtype)
            u = T @ v
            w = T @ kb
            tril_inc = (idx[:, None] >= idx[None, :]).astype(q.dtype)

            def step(S, xs):
                qi, ki, ui, wi, g = xs
                attn = qi @ jnp.swapaxes(ki, -1, -2) * tril_inc
                u_t = ui - wi @ S
                o_i = qi @ S + attn @ u_t
                S_new = g[..., None, None] * S + jnp.einsum('bhck,bhcv->bhkv', ki, u_t)
                return (S_new, o_i)
            mv = lambda x: jnp.moveaxis(x, 2, 0)
            S0 = jnp.zeros((b, h, dk, dv), dtype=q.dtype)
            S, o = jax.lax.scan(step, S0, (mv(q), mv(k), mv(u), mv(w), mv(gm)))
            o = jnp.moveaxis(o, 0, 2).reshape(b, h, l, dv)
            return (o, S)

        def fractal_mixer(x, conv_w):
            out = 2.0 * x
            l = x.shape[1]
            for i in range(conv_w.shape[0]):
                dil = 2 ** i
                x_shift = jnp.pad(x, ((0, 0), (dil, 0), (0, 0)))[:, :l, :]
                out = out + x_shift * conv_w[i, :, 0] + x * conv_w[i, :, 1]
            return out
        x = hidden_states
        b, l, d = x.shape
        H = rot_logit.shape[0]
        q = short_conv(x @ Wq, conv_q)
        k = short_conv(x @ Wk, conv_k)
        v = short_conv(x @ Wv, conv_v)
        dk = q.shape[-1] // H
        dv = v.shape[-1] // H
        q = q.reshape(b, l, H, dk)
        k = k.reshape(b, l, H, dk)
        v = v.reshape(b, l, H, dv)
        sin, cos = build_sin_cos(l, dk)
        mix = jax.nn.sigmoid(rot_logit)[None, None, :, None]
        q = mix * apply_rotary(q, sin, cos) + (1.0 - mix) * q
        k = mix * apply_rotary(k, sin, cos) + (1.0 - mix) * k
        beta = jax.nn.sigmoid(x @ Wb)
        gamma = jax.nn.sigmoid(x @ Wgamma)
        bh = lambda t: jnp.transpose(t, (0, 2, 1, 3))
        o, _ = delta_rule_chunkwise(bh(q), bh(k), bh(v), jnp.transpose(beta, (0, 2, 1)), jnp.transpose(gamma, (0, 2, 1)))
        o = jnp.transpose(o, (0, 2, 1, 3))
        o = rmsnorm(o, o_norm_w)
        core = o.reshape(b, l, H * dv) @ Wo
        frac = rmsnorm(fractal_mixer(x, frac_conv_w), mixer_norm_w)
        gate = jax.nn.sigmoid(x @ frac_gate_w + frac_gate_b)
        return core + gate * frac

    def _L1_ffn_ref(x, w_gate, w_up, w_down):
        import jax, jax.numpy as jnp
        import numpy as np
        DIM = 128
        HIDDEN = 384
        SCALE = 1.0 / 127.0

        def _dequant(w_int, dtype):
            return w_int.astype(dtype) * jnp.asarray(SCALE, dtype)
        wg = _dequant(w_gate, x.dtype)
        wu = _dequant(w_up, x.dtype)
        wd = _dequant(w_down, x.dtype)
        gate = jnp.einsum('bsd,hd->bsh', x, wg)
        up = jnp.einsum('bsd,hd->bsh', x, wu)
        h = jax.nn.silu(gate) * up
        return jnp.einsum('bsh,dh->bsd', h, wd)
    x = L0_attn_hidden_states
    x = x + _layernorm(_L0_attn_ref(_layernorm(x, axis=-1), L0_attn_Wq, L0_attn_bq, L0_attn_Wk, L0_attn_bk, L0_attn_Wv, L0_attn_bv, L0_attn_Wo, L0_attn_bo), axis=-1)
    x = x + _layernorm(_L0_ffn_ref(_layernorm(x, axis=-1), L0_ffn_wqkv, L0_ffn_q_scale, L0_ffn_k_scale, L0_ffn_wo, L0_ffn_ln_g, L0_ffn_ln_b, L0_ffn_w1, L0_ffn_b1, L0_ffn_w2, L0_ffn_b2), axis=-1)
    x = x + _layernorm(_L1_attn_ref(_layernorm(x, axis=-1), L1_attn_Wq, L1_attn_Wk, L1_attn_Wv, L1_attn_Wb, L1_attn_Wgamma, L1_attn_rot_logit, L1_attn_conv_q, L1_attn_conv_k, L1_attn_conv_v, L1_attn_o_norm_w, L1_attn_Wo, L1_attn_frac_conv_w, L1_attn_frac_gate_w, L1_attn_frac_gate_b, L1_attn_mixer_norm_w), axis=-1)
    x = x + _layernorm(_L1_ffn_ref(_layernorm(x, axis=-1), L1_ffn_w_gate, L1_ffn_w_up, L1_ffn_w_down), axis=-1)
    return x

_drawn_inputs = setup_inputs


def setup_inputs(seed=0):
    import zlib

    import numpy as np

    out = dict(_drawn_inputs(seed))
    spreads = {'L0_ffn_q_scale': (1.0, 0.6),
     'L0_ffn_k_scale': (1.0, 0.6),
     'L0_ffn_ln_g': (1.0, 0.6),
     'L0_ffn_ln_b': (0.0, 0.8),
     'L0_ffn_b1': (0.0, 0.8),
     'L0_ffn_b2': (0.0, 0.8),
     'L1_attn_rot_logit': (0.0, 0.8),
     'L1_attn_o_norm_w': (1.0, 0.2),
     'L1_attn_mixer_norm_w': (1.0, 0.2)}
    factors = {'L0_attn_bq': 5.977,
     'L0_attn_bk': 64.0,
     'L0_ffn_w1': 6.484,
     'L0_ffn_w2': 6.977,
     'L1_attn_Wb': 3.041,
     'L1_attn_Wgamma': 8.0,
     'L1_attn_frac_conv_w': 7.921}
    for name, (base, spread) in spreads.items():
        noise = np.random.default_rng([zlib.crc32(name.encode()), seed]).standard_normal(out[name].shape)
        drawn = base * np.exp(spread * noise) if base else spread * noise
        out[name] = jnp.asarray(drawn.astype(out[name].dtype))
    for name, factor in factors.items():
        out[name] = (out[name] * factor).astype(out[name].dtype)
    return out
```

```python
from contextlib import ExitStack

import numpy as np
import concourse.bass as bass
from concourse import mybir

ALU = mybir.AluOpType
ACT = mybir.ActivationFunctionType
AX = mybir.AxisListType
F32 = mybir.dt.float32
BF16 = mybir.dt.bfloat16
I32 = mybir.dt.int32

P = 128
B, S = 8, 512
NT = S // P
LN_EPS = 1e-5

H0, HD0 = 16, 8
NPAIR = H0 // 2
NGROUP = H0 // 4
Q_PARTS = (0, 0, 1, 1, 0, 2)
K_PARTS = (0, 1, 0, 1, 2, 0)
MAX_ROW = len(Q_PARTS) * HD0

L1, H1, HD1, WIN = 2, 8, 64, 64
INNER = H1 * HD1
HID1 = int(P * 4 * 2 / 3)
HCH = [(c, min(P, HID1 - c)) for c in range(0, HID1, P)]
MASKED = -1e30

H2, HD2, TAPS, CHUNK, DILATIONS = 4, 32, 4, 32, 4
LEVELS = 4

HID3 = 384
HCH3 = HID3 // P
DEQUANT = float(np.float32(1.0 / 127.0))

MAGIC = 0x5F3759DF


class Count:

    def __init__(self, sem):
        self.sem, self.n = sem, 0


def up(count, ins):
    ins.then_inc(count.sem, 1)
    count.n += 1
    return count.n


def link(eng, count, ins):
    up(count, ins)
    eng.wait_ge(count.sem, count.n)


class Signals:

    def __init__(self, nc, ctx):
        self.nc, self.ctx, self.every = nc, ctx, []
        (self.ln_centred, self.ln_copied, self.ln_squared, self.ln_var, self.ln_diag, self.ln_spread, self.ln_done,
         self.dve) = self.new("ln_centred ln_copied ln_squared ln_var ln_diag ln_spread ln_done dve")

    def new(self, names):
        counts = [Count(self.ctx.enter_context(self.nc.semaphore(n))) for n in names.split()]
        self.every += counts
        return counts

    def clear(self):
        with self.nc.Block() as block:
            @block.gpsimd
            def _(pool):
                for count in self.every:
                    pool.sem_clear(count.sem)
        for count in self.every:
            count.n = 0


class Store:
    pass


def rsqrt_steps(dve, c, v, y, t):
    link(dve, c, dve.tensor_scalar(t.bitcast(I32), v.bitcast(I32), 1, None, ALU.arith_shift_right))
    link(dve, c, dve.tensor_scalar(y.bitcast(I32), t.bitcast(I32), -1.0, float(MAGIC), ALU.mult, ALU.add))
    for _ in range(3):
        link(dve, c, dve.tensor_tensor(t, y, y, ALU.mult))
        link(dve, c, dve.scalar_tensor_tensor(out=t, in0=t, scalar=-0.5, in1=v, op0=ALU.mult, op1=ALU.mult))
        link(dve, c, dve.scalar_tensor_tensor(out=y, in0=t, scalar=1.5, in1=y, op0=ALU.add, op1=ALU.mult))


class Norm:

    def __init__(self, m, sems):
        self.m, self.s = m, sems

    def pe(self, n, src, bank, other):
        m, s, pe, ps = self.m, self.s, self.m.nc.tensor, self.m.ps
        up(s.ln_centred, pe.matmul(ps[:, bank, :], m.centre[:], src, start=True, stop=True))
        pe.wait_ge(s.ln_squared.sem, n + 1)
        for t in range(NT):
            last = pe.matmul(ps[:, other, t:t + 1], m.lnsq[:, t * P:(t + 1) * P], m.mean_col[:, 0:1],
                             start=True, stop=True)
        up(s.ln_var, last)
        pe.wait_ge(s.ln_diag.sem, n + 1)
        up(s.ln_spread, pe.matmul(ps[:, other, :], m.ones[:], m.diag[:], start=True, stop=True))

    def act(self, n, bank):
        m, s, act, ps = self.m, self.s, self.m.nc.scalar, self.m.ps
        act.wait_ge(s.ln_centred.sem, n + 1)
        if n:
            act.wait_ge(s.ln_done.sem, n)
        act.activation(m.lnc[:], ps[:, bank, :], ACT.Copy).then_inc(s.ln_copied.sem, 1)
        act.activation(m.lnsq[:], ps[:, bank, :], ACT.Square).then_inc(s.ln_squared.sem, 1)

    def dve(self, n, other, out, eps=LN_EPS):
        m, s, dve, ps = self.m, self.s, self.m.nc.vector, self.m.ps
        dve.wait_ge(s.ln_var.sem, n + 1)
        link(dve, s.dve, dve.tensor_scalar(m.var[:, 0:NT], ps[:, other, 0:NT], 1.0, eps, ALU.mult, ALU.add))
        rsqrt_steps(dve, s.dve, m.var[:, 0:NT], m.rstd[:, 0:NT], m.tmp[:, 0:NT])
        for t in range(NT):
            last = dve.tensor_scalar(m.diag[:, t * P:(t + 1) * P], m.ident[:], m.rstd[:, t:t + 1], None, ALU.mult)
            if t < NT - 1:
                up(s.dve, last)
        up(s.ln_diag, last)
        dve.wait_ge(s.dve.sem, s.dve.n)
        dve.wait_ge(s.ln_spread.sem, n + 1)
        dve.wait_ge(s.ln_copied.sem, n + 1)
        up(s.ln_done, dve.tensor_tensor(out, m.lnc[:], ps[:, other, :], ALU.mult))


def attention_block(m, ctx):
    nc, ps = m.nc, m.ps
    s = Signals(nc, ctx)
    (s.qk_proj, s.v_proj, s.qk_f32, s.v_done, s.parts, s.placed, s.q_stack, s.k_stack, s.s_ready, s.maxed,
     s.m_parts, s.m_turned, s.q_full, s.st_ready, s.exp_done, s.av_done, s.o_copied, s.o_turned, s.att_done,
     s.a_turned, s.a_copied, s.y_ready, s.y_copied) = s.new(
        "qk_proj v_proj qk_f32 v_done parts placed q_stack k_stack s_ready maxed m_parts m_turned q_full "
        "st_ready exp_done av_done o_copied o_turned att_done a_turned a_copied y_ready y_copied")
    sb = lambda name, shape, dt: ctx.enter_context(nc.sbuf_tensor(name, shape, dt))
    xn = sb("a_xn", [P, S], F32)
    qk = sb("a_qk", [P, 2, S], F32)
    rest = sb("a_rest", [P, S], F32)
    parts = sb("a_parts", [P, 2, 3, S], BF16)
    kst = sb("a_kst", [P, H0, S], BF16)
    qst = sb("a_qst", [P, NPAIR, S], BF16)
    va = sb("a_va", [P, NT, H0, 32], F32)
    negm = sb("a_negm", [P, H0, NT], F32)
    mrest = sb("a_mrest", [P, NT, 2], F32)
    mx = sb("a_mx", [P, 2, NT, P], BF16)
    prob = sb("a_prob", [P, 2, 4, 2, S], F32)
    osb = sb("a_osb", [P, S], F32)
    rec = sb("a_rec", [P, NT, 4], F32)
    att = sb("a_att", [P, NT, P], F32)
    aT = sb("a_aT", [P, S], F32)
    y = sb("a_y", [P, S], F32)
    mxv = mx[:].rearrange("p r t (a c) -> p r t a c", a=2)
    norm = Norm(m, s)

    with nc.Block() as block:
        @block.vector
        def _(dve):
            up(s.dve, dve.memset(kst[:], 0.0))
            up(s.dve, dve.memset(mx[:], 0.0))
            link(dve, s.dve, dve.memset(va[:], 0.0))
            up(s.dve, dve.memset(va[:, :, :, HD0:HD0 + 1], 1.0))
    s.clear()

    with nc.Fori(0, B, 1) as b:
        x_b = m.x[:, bass.ts(b, S)]
        with nc.Block() as block:
            @block.tensor
            def _(pe):
                norm.pe(0, x_b, 0, 1)
                pe.wait_ge(s.ln_done.sem, 1)
                up(s.qk_proj, pe.matmul(ps[:, 2, :], m.wq[:], xn[:], start=True, stop=True))
                up(s.qk_proj, pe.matmul(ps[:, 3, :], m.wk[:], xn[:], start=True, stop=True))
                for t in range(NT):
                    last = pe.matmul(ps[:, 4, t * P:(t + 1) * P], xn[:, t * P:(t + 1) * P], m.wv[:],
                                     start=True, stop=True)
                up(s.v_proj, last)
                for n in range(2 * NPAIR):
                    p, which = n // 2, n % 2
                    pe.wait_ge(s.parts.sem, which + 1)
                    if n < 4:
                        pe.wait_ge(s.v_done.sem, 1)
                    else:
                        pe.wait_ge((s.k_stack if which else s.q_stack).sem, (n - 4) // 2 * (1 + which) + 1 + which)
                    for part in range(3):
                        last = pe.matmul(ps[:, 4 + n % 4, :], m.sel[:, which, p, part, :],
                                         parts[:, which, part, :], start=part == 0, stop=part == 2)
                    up(s.placed, last)

                def scores(g, i):
                    h, qt = 4 * g + i // 4, i % 4
                    n = 16 * g + i
                    if n == 0:
                        pe.wait_ge(s.ln_done.sem, 1)
                    pe.wait_ge(s.q_stack.sem, h // 2 + 1)
                    pe.wait_ge(s.k_stack.sem, h + 1)
                    if n >= 2:
                        pe.wait_ge(s.maxed.sem, n - 1)
                    up(s.s_ready, pe.matmul(ps[:, n % 2, :], qst[:, h // 2, qt * P:(qt + 1) * P], kst[:, h, :],
                                            start=True, stop=True))

                def turn_max(g):
                    pe.wait_ge(s.m_parts.sem, g + 1)
                    if g == 0:
                        pe.wait_ge(s.k_stack.sem, H0)
                    for r in range(2):
                        if g or r:
                            pe.wait_ge(s.q_full.sem, 2 * g + r)
                        if g >= 2:
                            pe.wait_ge(s.att_done.sem, g - 1)
                        for t in range(NT):
                            last = pe.matmul(ps[:, 7, t * P:(t + 1) * P], mx[:, r, t, :], m.ident_bf[:],
                                             start=True, stop=True)
                        up(s.m_turned, last)

                def scores_t(g, i):
                    n = 8 * g + i
                    kp, h = i // 4, 4 * g + i % 4
                    pe.wait_ge(s.q_full.sem, h // 2 + 1)
                    if n == 0:
                        pe.wait_ge(s.qk_f32.sem, 2)
                        pe.wait_ge(s.q_stack.sem, NPAIR)
                        pe.wait_ge(s.k_stack.sem, H0)
                    if n >= 2:
                        pe.wait_ge(s.exp_done.sem, n - 1)
                    for k2 in range(2):
                        kt = 2 * kp + k2
                        last = pe.matmul(ps[:, 2 + 2 * (n % 2) + k2, :], kst[:, h, kt * P:(kt + 1) * P],
                                         qst[:, h // 2, :], start=True, stop=True)
                    up(s.st_ready, last)

                def weigh(c):
                    g, kp = c // 2, c % 2
                    pe.wait_ge(s.exp_done.sem, 4 * (c + 1))
                    if kp == 0 and g:
                        pe.wait_ge(s.o_copied.sem, g)
                    for k2 in range(2):
                        for j in range(4):
                            last = pe.matmul(ps[32 * j:32 * j + 32, 6, :], va[:, 2 * kp + k2, 4 * g + j, :],
                                             prob[:, c % 2, j, k2, :], start=kp == 0 and k2 == 0,
                                             stop=kp == 1 and k2 == 1)
                    up(s.av_done, last)

                def turn_out(g):
                    pe.wait_ge(s.o_copied.sem, g + 1)
                    pe.wait_ge(s.q_full.sem, min(2 * g + 4, NPAIR))
                    if g:
                        pe.wait_ge(s.att_done.sem, g)
                    for t in range(NT):
                        last = pe.transpose(ps[:, 7, t * P:(t + 1) * P], osb[:, t * P:(t + 1) * P], m.ident[:])
                    up(s.o_turned, last)

                for i in range(16):
                    scores(0, i)
                turn_max(0)
                for g in range(NGROUP):
                    for i in range(8):
                        scores_t(g, i)
                        if g + 1 < NGROUP:
                            scores(g + 1, 2 * i)
                            scores(g + 1, 2 * i + 1)
                        if i % 4 == 1 and 2 * g + i // 4 > 0:
                            weigh(2 * g + i // 4 - 1)
                        if i == 5 and g:
                            turn_out(g - 1)
                    if g + 1 < NGROUP:
                        turn_max(g + 1)
                weigh(2 * NGROUP - 1)
                turn_out(NGROUP - 1)
                pe.wait_ge(s.att_done.sem, NGROUP)
                for t in range(NT):
                    last = pe.transpose(ps[:, 0, t * P:(t + 1) * P], att[:, t, :], m.ident[:])
                up(s.a_turned, last)
                pe.wait_ge(s.a_copied.sem, 1)
                up(s.y_ready, pe.matmul(ps[:, 1, :], m.wo[:], aT[:], start=True, stop=True))
                pe.wait_ge(s.y_copied.sem, 1)
                norm.pe(1, y[:], 2, 3)

            @block.scalar
            def _(act):
                norm.act(0, 0)
                act.wait_ge(s.qk_proj.sem, 1)
                act.activation(qk[:, 0, :], ps[:, 2, :], ACT.Identity, bias=m.bq_scaled[:, 0:1],
                               scale=HD0 ** -0.5).then_inc(s.qk_f32.sem, 1)
                act.wait_ge(s.qk_proj.sem, 2)
                act.activation(qk[:, 1, :], ps[:, 3, :], ACT.Identity, bias=m.bk[:, 0:1]).then_inc(s.qk_f32.sem, 1)
                for p in range(NPAIR):
                    act.wait_ge(s.placed.sem, 2 * p + 1)
                    act.activation(qst[:, p, :], ps[:, 4 + (2 * p) % 4, :], ACT.Copy).then_inc(s.q_stack.sem, 1)
                for c in range(2 * NGROUP):
                    for j in range(4):
                        n = 4 * c + j
                        act.wait_ge(s.st_ready.sem, n + 1)
                        if j == 0 and c >= 2:
                            act.wait_ge(s.av_done.sem, c - 1)
                        act.activation(prob[:, c % 2, j, :, :],
                                       ps[:, 2 + 2 * (n % 2):4 + 2 * (n % 2), :], ACT.Exp).then_inc(s.exp_done.sem, 1)
                    if c % 2 == 0 and c:
                        act.wait_ge(s.av_done.sem, c)
                        if c > 2:
                            act.wait_ge(s.o_turned.sem, c // 2 - 1)
                        act.activation(osb[:], ps[:, 6, :], ACT.Copy).then_inc(s.o_copied.sem, 1)
                act.wait_ge(s.av_done.sem, 2 * NGROUP)
                act.wait_ge(s.o_turned.sem, NGROUP - 1)
                act.activation(osb[:], ps[:, 6, :], ACT.Copy).then_inc(s.o_copied.sem, 1)
                act.wait_ge(s.a_turned.sem, 1)
                act.activation(aT[:], ps[:, 0, :], ACT.Copy).then_inc(s.a_copied.sem, 1)
                act.wait_ge(s.y_ready.sem, 1)
                act.activation(y[:], ps[:, 1, :], ACT.Identity, bias=m.bo[:, 0:1]).then_inc(s.y_copied.sem, 1)
                norm.act(1, 2)

            @block.vector
            def _(dve):
                norm.dve(0, 1, xn[:])
                dve.wait_ge(s.v_proj.sem, 1)
                for t in range(NT):
                    last = dve.tensor_tensor(va[:, t, :, 0:HD0],
                                             ps[:, 4, t * P:(t + 1) * P].rearrange("p (h d) -> p h d", h=H0),
                                             m.bv[:].rearrange("p (h d) -> p h d", h=H0), ALU.add)
                    if t < NT - 1:
                        up(s.dve, last)
                up(s.v_done, last)
                for w in range(2):
                    dve.wait_ge(s.qk_f32.sem, w + 1)
                    link(dve, s.dve, dve.tensor_copy(parts[:, w, 0, :], qk[:, w, :]))
                    link(dve, s.dve, dve.tensor_tensor(rest[:], qk[:, w, :], parts[:, w, 0, :], ALU.subtract))
                    link(dve, s.dve, dve.tensor_copy(parts[:, w, 1, :], rest[:]))
                    up(s.parts, dve.tensor_tensor(parts[:, w, 2, :], rest[:], parts[:, w, 1, :], ALU.subtract))
                    dve.wait_ge(s.parts.sem, w + 1)
                for p in range(NPAIR):
                    dve.wait_ge(s.placed.sem, 2 * p + 2)
                    for a in range(2):
                        rows = slice(64 * a, 64 * a + 64)
                        up(s.k_stack, dve.tensor_scalar(kst[rows, 2 * p + a, :], ps[rows, 4 + (2 * p + 1) % 4, :],
                                                        m.ones_rows[rows, 0:1], None, ALU.add))

                def maxima(g, i):
                    n = 16 * g + i
                    dve.wait_ge(s.s_ready.sem, n + 1)
                    up(s.maxed, dve.tensor_reduce(negm[:, 4 * g + i // 4, i % 4:i % 4 + 1], ps[:, n % 2, :], AX.X,
                                                  ALU.max, negate=True))

                def full_q(g):
                    dve.wait_ge(s.maxed.sem, 16 * (g + 1))
                    if g:
                        dve.wait_ge(s.m_turned.sem, 2 * g)
                    for r in range(2):
                        neg = negm[:, 4 * g + 2 * r:4 * g + 2 * r + 2, :].rearrange("p a t -> p t a")
                        link(dve, s.dve, dve.tensor_copy(mxv[:, r, :, :, MAX_ROW], neg))
                        link(dve, s.dve, dve.tensor_tensor(mrest[:], neg, mxv[:, r, :, :, MAX_ROW], ALU.subtract))
                        link(dve, s.dve, dve.tensor_copy(mxv[:, r, :, :, MAX_ROW + 1], mrest[:]))
                        last = dve.tensor_tensor(mxv[:, r, :, :, MAX_ROW + 2], mrest[:],
                                                 mxv[:, r, :, :, MAX_ROW + 1], ALU.subtract)
                        if r == 0:
                            link(dve, s.dve, last)
                    up(s.m_parts, last)
                    for r in range(2):
                        p = 2 * g + r
                        dve.wait_ge(s.m_turned.sem, p + 1)
                        up(s.q_full, dve.tensor_tensor(qst[:, p, :], qst[:, p, :], ps[:, 7, :], ALU.add))

                def finish(g):
                    dve.wait_ge(s.o_turned.sem, g + 1)
                    o = ps[:, 7, :].rearrange("p (t j c) -> p t j c", t=NT, j=4)
                    link(dve, s.dve, dve.reciprocal(rec[:], o[:, :, :, HD0]))
                    up(s.att_done, dve.tensor_tensor(
                        att[:, :, 32 * g:32 * g + 32].rearrange("p t (j d) -> p t j d", j=4), o[:, :, :, 0:HD0],
                        rec[:].unsqueeze(3).to_broadcast([P, NT, 4, HD0]), ALU.mult))

                for i in range(16):
                    maxima(0, i)
                full_q(0)
                for g in range(NGROUP):
                    for i in range(8):
                        if g + 1 < NGROUP:
                            maxima(g + 1, 2 * i)
                            maxima(g + 1, 2 * i + 1)
                        if i == 5 and g:
                            finish(g - 1)
                    if g + 1 < NGROUP:
                        full_q(g + 1)
                finish(NGROUP - 1)
                norm.dve(1, 3, y[:])
                dve.wait_ge(s.ln_done.sem, 2)
                up(s.dve, dve.tensor_tensor(x_b, x_b, y[:], ALU.add))
        s.clear()


def local_block(m, ctx):
    nc, ps = m.nc, m.ps
    s = Signals(nc, ctx)
    (s.act, s.pool, s.shifted, s.qkv_ready, s.q_raw, s.k_raw, s.v_raw, s.squared, s.summed, s.rnorm, s.k_scaled,
     s.swapped, s.rotated, s.q_turned, s.k_turned, s.q_t, s.k_t, s.scores_ready, s.neg_max, s.exp_done,
     s.p_turned, s.p_act, s.p_dve, s.o_ready, s.o_scaled, s.o_turned, s.o_t, s.res_ready, s.stream, s.g_ready,
     s.a_ready, s.gelu_done, s.h_done, s.down_ready) = s.new(
        "act pool shifted qkv_ready q_raw k_raw v_raw squared summed rnorm k_scaled swapped rotated q_turned "
        "k_turned q_t k_t scores_ready neg_max exp_done p_turned p_act p_dve o_ready o_scaled o_turned o_t "
        "res_ready stream g_ready a_ready gelu_done h_done down_ready")
    sb = lambda name, shape, dt=F32: ctx.enter_context(nc.sbuf_tensor(name, shape, dt))
    y = sb("b_y", [P, S])
    hT = sb("b_hT", [P, S])
    raw = sb("b_raw", [P, NT, 2, INNER])
    v = sb("b_v", [P, NT, INNER])
    sq = sb("b_sq", [P, 2, INNER])
    ssq = sb("b_ssq", [P, NT, 2, H1])
    rn = sb("b_rn", [P, NT, 2, H1])
    rn_t = sb("b_rn_t", [P, NT, 2, H1])
    rq = sb("b_rq", [P, NT, H1])
    direct = sb("b_direct", [P, 2, INNER])
    swap = sb("b_swap", [P, 2, 2, INNER])
    rot = sb("b_rot", [P, 2, 2, INNER])
    qT = sb("b_qT", [P, 2, 4, P])
    kT = sb("b_kT", [P, H1, S])
    prob = sb("b_prob", [P, H1, 2 * P])
    pT = sb("b_pT", [P, 2, 8, P])
    nmax = sb("b_nmax", [P, H1])
    nbias = sb("b_nbias", [P, 2, H1])
    den = sb("b_den", [P, 2, H1])
    rden = sb("b_rden", [P, H1])
    on = sb("b_on", [P, INNER])
    oT = sb("b_oT", [P, 4, S])
    hn = sb("b_hn", [P, S])
    gel = sb("b_gel", [P, 2, S])
    hm = sb("b_hm", [P, 3, S])
    norm = Norm(m, s)
    sc = ps[:, 0:4, :].rearrange("p b c -> p (b c)").rearrange("p (f h c) -> p f h c", f=2, h=4)

    with nc.Block() as block:
        @block.vector
        def _(dve):
            up(s.dve, dve.memset(kT[:], 0.0))
            up(s.dve, dve.memset(prob[:], 0.0))
            up(s.dve, dve.memset(hT[:], 0.0))
    s.clear()

    with nc.Fori(0, B, 1) as b:
        x_b = m.x[:, bass.ts(b, S)]
        with nc.Block() as block:
            @block.tensor
            def _(pe):
                norm.pe(0, x_b, 0, 1)
                for l in range(L1):
                    w = m.layer[l]
                    pe.wait_ge(s.shifted.sem, 4 * l + 2)
                    for n in range(3 * NT):
                        t, j = n // 3, n % 3
                        if n >= 6:
                            pe.wait_ge((s.q_raw, s.k_raw, s.v_raw)[j].sem, NT * l + t - 1)
                        elif n == 0 and l:
                            pe.wait_ge(s.stream.sem, 2 * l + 1)
                        up(s.qkv_ready, pe.matmul(ps[:, n % 6, :], hT[:, t * P:(t + 1) * P],
                                                  w.wqkv[:, j * INNER:(j + 1) * INNER], start=True, stop=True))
                    pe.wait_ge(s.q_raw.sem, NT * (l + 1))
                    pe.wait_ge(s.k_raw.sem, NT * (l + 1))
                    pe.wait_ge(s.v_raw.sem, NT * (l + 1))

                    def turn(t):
                        n = NT * l + t
                        pe.wait_ge(s.rotated.sem, n + 1)
                        for j, (done, turned) in enumerate(((s.k_t, s.q_turned), (s.q_t, s.k_turned))):
                            if j or n:
                                pe.wait_ge(done.sem, n + j if j else 2 * n)
                            for c in range(4):
                                last = pe.transpose(ps[:, 6, c * P:(c + 1) * P], rot[:, t % 2, j, c * P:(c + 1) * P],
                                                    m.ident[:])
                            up(turned, last)

                    def scores(t, f):
                        n = NT * l + t
                        lo = P if t == 0 else WIN
                        pe.wait_ge(s.q_t.sem, n + 1)
                        pe.wait_ge(s.k_t.sem, 2 * n + 2)
                        if n:
                            pe.wait_ge(s.exp_done.sem, 8 * (n - 1) + 4 * f + 4)
                        for hh in range(4):
                            h = 4 * f + hh
                            dst = sc[:, f, hh, lo:2 * P]
                            pe.matmul(dst, qT[:, t % 2, h // 2, :], kT[:, h, t * P + lo - P:(t + 1) * P],
                                      start=True, stop=False)
                            last = pe.matmul(dst, m.ident_bf[:], m.mask[:, lo - WIN:3 * WIN], start=False, stop=True)
                        up(s.scores_ready, last)

                    def turn_probs(t, f):
                        n = 2 * (NT * l + t) + f
                        pe.wait_ge(s.exp_done.sem, 4 * n + 4)
                        if n:
                            pe.wait_ge(s.p_act.sem, n)
                        earlier = 2 * (NT - 1) * l + 2 * (t - 1) + f
                        if t and earlier:
                            pe.wait_ge(s.p_dve.sem, earlier)
                        for c in (1, 0):
                            if c == 0 and t == 0:
                                continue
                            for hh in range(4):
                                last = pe.transpose(ps[:, 4 + c, hh * P:(hh + 1) * P],
                                                    prob[:, 4 * f + hh, c * P:(c + 1) * P], m.ident[:])
                        up(s.p_turned, last)

                    def weigh(t):
                        n = NT * l + t
                        if n:
                            pe.wait_ge(s.o_t.sem, n)
                        for f in range(2):
                            pe.wait_ge(s.p_act.sem, 2 * n + f + 1)
                            if t:
                                pe.wait_ge(s.p_dve.sem, 2 * (NT - 1) * l + 2 * (t - 1) + f + 1)
                            for hh in range(4):
                                h = 4 * f + hh
                                for c in (1, 0):
                                    if c == 0 and t == 0:
                                        continue
                                    last = pe.matmul(ps[:, 7, h * HD1:(h + 1) * HD1], pT[:, f, 4 * c + hh, :],
                                                     v[:, t - 1 + c, h * HD1:(h + 1) * HD1],
                                                     start=c == 1, stop=c == 0 or t == 0)
                        up(s.o_ready, last)
                        pe.wait_ge(s.o_scaled.sem, n + 1)
                        for c in range(4):
                            last = pe.transpose(ps[:, 7, c * P:(c + 1) * P], on[:, c * P:(c + 1) * P], m.ident[:])
                        up(s.o_turned, last)

                    for t in range(NT + 1):
                        if t < NT:
                            turn(t)
                        for f in range(2):
                            if t:
                                turn_probs(t - 1, f)
                            if t < NT:
                                scores(t, f)
                        if t:
                            weigh(t - 1)
                    pe.wait_ge(s.o_t.sem, NT * (l + 1))
                    for c in range(4):
                        last = pe.matmul(ps[:, 0, :], w.wo[:, c, :], oT[:, c, :], start=c == 0, stop=c == 3)
                    up(s.res_ready, last)
                    pe.wait_ge(s.shifted.sem, 4 * l + 4)
                    norm.pe(1 + l, hT[:], 1, 2)
                    pe.wait_ge(s.act.sem, l + 1)
                    for c, (c0, rows) in enumerate(HCH):
                        if c == 2:
                            pe.wait_ge(s.h_done.sem, 3 * l + 1)
                        g_bank, a_bank = 3 + 2 * (c % 2), 4 + 2 * (c % 2)
                        up(s.g_ready, pe.matmul(ps[0:rows, g_bank, :], w.w1[:, HID1 + c0:HID1 + c0 + rows], hn[:],
                                                start=True, stop=True))
                        up(s.a_ready, pe.matmul(ps[0:rows, a_bank, :], w.w1[:, c0:c0 + rows], hn[:],
                                                start=True, stop=True))
                    for c, (c0, rows) in enumerate(HCH):
                        pe.wait_ge(s.h_done.sem, 3 * l + c + 1)
                        last = pe.matmul(ps[:, 0, :], w.w2[0:rows, c, :], hm[0:rows, c, :], start=c == 0, stop=c == 2)
                    up(s.down_ready, last)
                pe.wait_ge(s.stream.sem, 1 + 2 * L1)
                norm.pe(1 + L1, y[:], 1, 2)

            @block.scalar
            def _(act):
                norm.act(0, 0)

                def shift(n):
                    act.wait_ge(s.stream.sem, n + 1)
                    act.activation(hT[0:64, :], y[0:64, :], ACT.Copy).then_inc(s.shifted.sem, 1)
                    act.activation(hT[64:P, 1:S], y[64:P, 0:S - 1], ACT.Copy).then_inc(s.shifted.sem, 1)

                for l in range(L1):
                    w = m.layer[l]
                    shift(2 * l)
                    for t in range(NT):
                        n = NT * l + t
                        act.wait_ge(s.qkv_ready.sem, 3 * n + 1)
                        act.activation(raw[:, t, 0, :], ps[:, (3 * t) % 6, :], ACT.Copy).then_inc(s.q_raw.sem, 1)
                        act.wait_ge(s.qkv_ready.sem, 3 * n + 3)
                        act.activation(v[:, t, :], ps[:, (3 * t + 2) % 6, :], ACT.Copy).then_inc(s.v_raw.sem, 1)
                    for t in range(NT + 1):
                        n = NT * l + t
                        if t < NT:
                            act.wait_ge(s.q_turned.sem, n + 1)
                            act.activation(qT[:, t % 2, :, :], ps[:, 6, :].rearrange("p (c k) -> p c k", c=4),
                                           ACT.Copy).then_inc(s.q_t.sem, 1)
                            act.wait_ge(s.k_turned.sem, n + 1)
                            for a in range(2):
                                rows = slice(64 * a, 64 * a + 64)
                                act.activation(kT[rows, a::2, t * P:(t + 1) * P],
                                               ps[rows, 6, :].rearrange("p (c k) -> p c k", c=4),
                                               ACT.Copy).then_inc(s.k_t.sem, 1)
                        for f in range(2):
                            if t:
                                k = 2 * (n - 1) + f
                                act.wait_ge(s.p_turned.sem, k + 1)
                                if k >= 2:
                                    act.wait_ge(s.o_ready.sem, k // 2)
                                act.activation(pT[:, f, 4:8, :], ps[:, 5, :].rearrange("p (c k) -> p c k", c=4),
                                               ACT.Copy).then_inc(s.p_act.sem, 1)
                            if t < NT:
                                lo = P if t == 0 else WIN
                                act.wait_ge(s.neg_max.sem, 2 * n + f + 1)
                                if n >= 2:
                                    act.wait_ge(s.o_scaled.sem, n - 1)
                                for hh in range(4):
                                    h = 4 * f + hh
                                    act.activation(prob[:, h, lo:2 * P], sc[:, f, hh, lo:2 * P], ACT.Exp,
                                                   bias=nbias[:, t % 2, h:h + 1], scale=rq[:, t, h:h + 1],
                                                   accum_out=den[:, t % 2, h:h + 1]).then_inc(s.exp_done.sem, 1)
                        if t:
                            act.wait_ge(s.o_turned.sem, n)
                            act.activation(oT[:, :, (t - 1) * P:t * P], ps[:, 7, :].rearrange("p (c k) -> p c k", c=4),
                                           ACT.Copy).then_inc(s.o_t.sem, 1)
                    shift(2 * l + 1)
                    norm.act(1 + l, 1)
                    act.wait_ge(s.ln_done.sem, 2 + l)
                    up(s.act, act.activation(hn[:], hn[:], ACT.Identity, bias=w.ln_b[:, 0:1], scale=w.ln_g[:, 0:1]))
                    for c, (c0, rows) in enumerate(HCH):
                        k = 3 * l + c
                        act.wait_ge(s.g_ready.sem, k + 1)
                        if k >= 2:
                            act.wait_ge(s.h_done.sem, k - 1)
                        act.activation(gel[0:rows, c % 2, :], ps[0:rows, 3 + 2 * (c % 2), :], ACT.Gelu,
                                       bias=w.b1[0:rows, 3 + c:4 + c]).then_inc(s.gelu_done.sem, 1)
                norm.act(1 + L1, 1)

            @block.gpsimd
            def _(pool):
                for l in range(L1):
                    w = m.layer[l]
                    for t in range(NT):
                        n = NT * l + t
                        for j, have in enumerate((s.q_raw, s.k_raw)):
                            pool.wait_ge(have.sem, n + 1)
                            if n and j == 0:
                                pool.wait_ge(s.summed.sem, n)
                            up(s.squared, pool.tensor_tensor(sq[:, j, :], raw[:, t, j, :], raw[:, t, j, :], ALU.mult))
                    for t in range(NT):
                        n = NT * l + t
                        pool.wait_ge(s.k_scaled.sem, n + 1)
                        if n >= 2:
                            pool.wait_ge(s.rotated.sem, n - 1)
                        src = raw[:, t, :, :].rearrange("p j (h d) -> p j h d", h=H1)
                        dst = swap[:, t % 2, :, :].rearrange("p j (h d) -> p j h d", h=H1)
                        for half in range(2):
                            o, i = slice(32 * half, 32 * half + 32), slice(32 - 32 * half, 64 - 32 * half)
                            for j in range(2):
                                up(s.swapped, pool.tensor_tensor(
                                    dst[:, j, :, o], src[:, j, :, i],
                                    w.tab_swap[:, t, j, o].unsqueeze(1).to_broadcast([P, H1, 32]), ALU.mult))

            @block.vector
            def _(dve):
                norm.dve(0, 1, y[:])
                dve.wait_ge(s.ln_done.sem, 1)
                up(s.stream, dve.tensor_scalar(y[:], y[:], 1.0, None, ALU.mult))
                for l in range(L1):
                    w = m.layer[l]
                    for t in range(NT):
                        n = NT * l + t
                        dve.wait_ge(s.qkv_ready.sem, 3 * n + 2)
                        if l and t == 0:
                            dve.wait_ge(s.rotated.sem, NT * l)
                        up(s.k_raw, dve.tensor_copy(raw[:, t, 1, :], ps[:, (3 * t + 1) % 6, :]))
                        if t:
                            dve.wait_ge(s.squared.sem, 2 * n)
                            up(s.summed, dve.tensor_reduce(ssq[:, t - 1, :, :],
                                                           sq[:].rearrange("p j (h d) -> p j h d", h=H1), AX.X, ALU.add))
                    dve.wait_ge(s.squared.sem, 2 * NT * (l + 1))
                    up(s.summed, dve.tensor_reduce(ssq[:, NT - 1, :, :], sq[:].rearrange("p j (h d) -> p j h d", h=H1),
                                                   AX.X, ALU.add))
                    dve.wait_ge(s.summed.sem, NT * (l + 1))
                    flat = lambda a: a[:].rearrange("p t j h -> p (t j h)")
                    link(dve, s.dve, dve.tensor_scalar(flat(ssq), flat(ssq), 1e-24, None, ALU.max))
                    rsqrt_steps(dve, s.dve, flat(ssq), flat(rn), flat(rn_t))
                    link(dve, s.dve, dve.tensor_scalar(rq[:], rn[:, :, 0, :], 8.0, None, ALU.mult))

                    def rotate(t):
                        n = NT * l + t
                        kk = raw[:, t, 1, :].rearrange("p (h d) -> p h d", h=H1)
                        up(s.k_scaled, dve.tensor_tensor(kk, kk, rn[:, t, 1, :].unsqueeze(2).to_broadcast([P, H1, HD1]),
                                                         ALU.mult))
                        dve.wait_ge(s.k_scaled.sem, n + 1)
                        for j in range(2):
                            up(s.dve, dve.tensor_tensor(
                                direct[:, j, :].rearrange("p (h d) -> p h d", h=H1),
                                raw[:, t, j, :].rearrange("p (h d) -> p h d", h=H1),
                                w.tab_direct[:, t, j, :].unsqueeze(1).to_broadcast([P, H1, HD1]), ALU.mult))
                        dve.wait_ge(s.dve.sem, s.dve.n)
                        dve.wait_ge(s.swapped.sem, 4 * (n + 1))
                        if n >= 2:
                            dve.wait_ge(s.k_turned.sem, n - 1)
                        up(s.rotated, dve.tensor_tensor(rot[:, t % 2, :, :], direct[:], swap[:, t % 2, :, :], ALU.add))
                        dve.wait_ge(s.rotated.sem, n + 1)

                    rotate(0)
                    for t in range(NT + 1):
                        n = NT * l + t
                        if t + 1 < NT:
                            rotate(t + 1)
                        for f in range(2):
                            if t > 1:
                                k = 2 * (n - 1) + f
                                dve.wait_ge(s.p_turned.sem, k + 1)
                                dve.wait_ge(s.o_ready.sem, k // 2)
                                up(s.p_dve, dve.tensor_copy(pT[:, f, 0:4, :],
                                                            ps[:, 4, :].rearrange("p (c k) -> p c k", c=4)))
                            if t < NT:
                                lo = P if t == 0 else WIN
                                hs = slice(4 * f, 4 * f + 4)
                                dve.wait_ge(s.scores_ready.sem, 2 * n + f + 1)
                                link(dve, s.dve, dve.tensor_reduce(nmax[:, hs], sc[:, f, :, lo:2 * P], AX.X, ALU.max,
                                                                   negate=True))
                                if n >= 2:
                                    dve.wait_ge(s.exp_done.sem, 8 * (n - 1))
                                up(s.neg_max, dve.tensor_tensor(nbias[:, t % 2, hs], nmax[:, hs], rq[:, t, hs], ALU.mult))
                        if t:
                            dve.wait_ge(s.o_ready.sem, n)
                            link(dve, s.dve, dve.reciprocal(rden[:], den[:, (t - 1) % 2, :]))
                            up(s.o_scaled, dve.tensor_tensor(
                                on[:].rearrange("p (h d) -> p h d", h=H1),
                                ps[:, 7, :].rearrange("p (h d) -> p h d", h=H1),
                                rden[:].unsqueeze(2).to_broadcast([P, H1, HD1]), ALU.mult))
                    dve.wait_ge(s.res_ready.sem, l + 1)
                    up(s.stream, dve.tensor_tensor(y[:], y[:], ps[:, 0, :], ALU.add))
                    norm.dve(1 + l, 2, hn[:])
                    for c, (c0, rows) in enumerate(HCH):
                        k = 3 * l + c
                        dve.wait_ge(s.a_ready.sem, k + 1)
                        dve.wait_ge(s.gelu_done.sem, k + 1)
                        up(s.h_done, dve.scalar_tensor_tensor(
                            out=hm[0:rows, c, :], in0=ps[0:rows, 4 + 2 * (c % 2), :], scalar=w.b1[0:rows, c:c + 1],
                            in1=gel[0:rows, c % 2, :], op0=ALU.add, op1=ALU.mult))
                    dve.wait_ge(s.down_ready.sem, l + 1)
                    up(s.stream, dve.scalar_tensor_tensor(out=y[:], in0=ps[:, 0, :], scalar=w.b2[:, 0:1], in1=y[:],
                                                          op0=ALU.add, op1=ALU.add))
                norm.dve(1 + L1, 2, hn[:])
                dve.wait_ge(s.ln_done.sem, 2 + L1)
                up(s.dve, dve.tensor_tensor(x_b, x_b, hn[:], ALU.add))
        s.clear()


def delta_prepare(m, ctx, st):
    nc, ps = m.nc, m.ps
    s = Signals(nc, ctx)
    (s.act, s.pool, s.conv_ready, s.gates_ready, s.sigmoid_done, s.silu_done, s.turned, s.tok_copied,
     s.half_done, s.base_done, s.rot_done, s.rot_squared, s.k_norm, s.q_norm, s.b_weighed, s.v_weighed,
     s.f_turned, s.q_t, s.kb_t, s.k_t, s.gamma_ready, s.gamma_wide, s.n_ready, s.nt_ready, s.at_ready, s.nt_raw,
     s.level_masked, s.t1_masked, s.tt_ready, s.t_ready, s.att_ready, s.x_ready, s.x_copied, s.tx_ready,
     s.txt_ready, s.uw_ready, s.wt_ready, s.uw_copied, s.out_ready, s.out_copied, s.qp_done, s.u_kept, s.k_kept) = s.new(
        "act pool conv_ready gates_ready sigmoid_done silu_done turned tok_copied half_done base_done "
        "rot_done rot_squared k_norm q_norm b_weighed v_weighed f_turned q_t kb_t k_t gamma_ready gamma_wide "
        "n_ready nt_ready at_ready nt_raw level_masked t1_masked tt_ready t_ready att_ready x_ready x_copied "
        "tx_ready txt_ready uw_ready wt_ready uw_copied out_ready out_copied qp_done u_kept k_kept")
    sb = lambda name, shape, dt=F32: ctx.enter_context(nc.sbuf_tensor(name, shape, dt))
    xp = sb("c_xp", [P, TAPS - 1 + S])
    xn = xp[:, TAPS - 1:TAPS - 1 + S]
    sg, act3 = sb("c_sg", [P, S]), sb("c_act3", [P, 3, S])
    bg, wide = sb("c_bg", [P, NT, 2, H2]), sb("c_wide", [P, NT, P])
    tok, half_a, half_b = sb("c_tok", [P, 2, S]), sb("c_half_a", [P, 2, S]), sb("c_half_b", [P, 2, S])
    ssq, rn, rn_t = (sb("c_" + n, [P, 2, NT * H2]) for n in ("ssq", "rn", "rn_t"))
    ktok = sb("c_ktok", [P, NT, P])
    vk = sb("c_vk", [P, NT, H2, 2, HD2])
    qT, kbT, kT = sb("c_qT", [P, S]), sb("c_kbT", [P, S]), sb("c_kT", [P, H2, S])
    four = lambda name: [sb(f"c_{name}{u}", [P, H2, P]) for u in range(2)]
    T, TT, X, NT_raw, att = four("T"), four("TT"), four("X"), four("NT"), four("att")
    NTs = [[sb(f"c_NTs{u}{i}", [P, H2, P]) for i in range(2)] for u in range(2)]
    uw = [sb(f"c_uw{u}", [P, H2, 2, HD2]) for u in range(2)]
    norm = Norm(m, s)
    heads = lambda a: a.unsqueeze(1).to_broadcast([P, H2, P])
    bank = lambda k: ps[:, k, :].rearrange("p (h c) -> p h c", h=H2)
    g16 = lambda a: a.rearrange("p (g c) -> p g c", c=HD2)
    even_odd = lambda a: a.rearrange("p (g i two) -> p g two i", two=2, i=HD2 // 2)
    halves = lambda a: a.rearrange("p (g two i) -> p g two i", two=2, i=HD2 // 2)

    def summed(t0, i, u):
        return (LEVELS + 1) * t0 + 2 * i + u + 1

    with nc.Block() as block:
        @block.vector
        def _(dve):
            up(s.dve, dve.memset(kT[:], 0.0))
            up(s.dve, dve.memset(xp[:], 0.0))
    s.clear()

    with nc.Fori(0, B, 1) as b:
        x_b = m.x[:, bass.ts(b, S)]
        mine = lambda a, t: a[:, t, bass.ds(b, 1), :].rearrange("p a c -> p (a c)")
        with nc.Block() as block:
            @block.tensor
            def _(pe):
                norm.pe(0, x_b, 0, 1)
                pe.wait_ge(s.ln_done.sem, 1)
                for j in range(3):
                    for tap in range(TAPS):
                        last = pe.matmul(ps[:, 2 + j, :], m.c_taps[:, j, tap, :], xp[:, tap:tap + S],
                                         start=tap == 0, stop=tap == TAPS - 1)
                    up(s.conv_ready, last)
                for t in range(NT):
                    last = pe.matmul(ps[:, 0, t * 8:t * 8 + 8], xn[:, t * P:(t + 1) * P], m.c_wbg[:],
                                     start=True, stop=True)
                up(s.gates_ready, last)
                for j in range(3):
                    pe.wait_ge(s.silu_done.sem, j + 1)
                    for t in range(NT):
                        last = pe.transpose(ps[:, 5 + j, t * P:(t + 1) * P], act3[:, j, t * P:(t + 1) * P], m.ident[:])
                    up(s.turned, last)
                pe.wait_ge(s.pool.sem, NT - 1)
                pe.wait_ge(s.gamma_wide.sem, 1)
                for t in range(NT):
                    last = pe.matmul(ps[:, 1, t * 4:t * 4 + 4], wide[:, t, :], m.c_chunk_mean[:], start=True, stop=True)
                up(s.gamma_ready, last)
                pe.wait_ge(s.q_norm.sem, 1)
                for t in range(NT):
                    last = pe.transpose(ps[:, 2, t * P:(t + 1) * P], half_a[:, 0, t * P:(t + 1) * P], m.ident[:])
                up(s.f_turned, last)
                pe.wait_ge(s.k_norm.sem, 1)
                for t in range(NT):
                    last = pe.transpose(ps[:, 3, t * P:(t + 1) * P], ktok[:, t, :], m.ident[:])
                up(s.f_turned, last)
                pe.wait_ge(s.b_weighed.sem, NT)
                for t in range(NT):
                    last = pe.transpose(ps[:, 4, t * P:(t + 1) * P], half_b[:, 0, t * P:(t + 1) * P], m.ident[:])
                up(s.f_turned, last)
                pe.wait_ge(s.q_t.sem, 1)
                pe.wait_ge(s.kb_t.sem, 1)
                pe.wait_ge(s.k_t.sem, H2)
                pe.wait_ge(s.v_weighed.sem, NT)
                for t0 in range(0, NT, 2):
                    for u in range(2):
                        t, tile = t0 + u, slice((t0 + u) * P, (t0 + u + 1) * P)
                        if t0:
                            pe.wait_ge(s.qp_done.sem, t - 1)
                            pe.wait_ge(s.out_copied.sem, 2 * t0)
                            pe.wait_ge(s.uw_copied.sem, t - 1)
                        for h in range(H2):
                            last = pe.matmul(ps[:, 4 * u, h * P:(h + 1) * P], kbT[:, tile], kT[:, h, tile],
                                             start=True, stop=True)
                        up(s.n_ready, last)
                        for h in range(H2):
                            last = pe.matmul(ps[:, 4 * u + 1, h * P:(h + 1) * P], kT[:, h, tile], kbT[:, tile],
                                             start=True, stop=True)
                        up(s.nt_ready, last)
                        for h in range(H2):
                            last = pe.matmul(ps[:, 4 * u + 2, h * P:(h + 1) * P], kT[:, h, tile], qT[:, tile],
                                             start=True, stop=True)
                        up(s.at_ready, last)
                    for i in range(LEVELS):
                        for u in range(2):
                            k = LEVELS * t0 + 2 * i + u
                            pe.wait_ge(s.level_masked.sem, k + 1)
                            pe.wait_ge(s.t_ready.sem, summed(t0, i, u))
                            if i:
                                pe.wait_ge(s.x_copied.sem, k - 1)
                            for h in range(H2):
                                last = pe.matmul(ps[:, 4 * u, h * P:(h + 1) * P], NTs[u][i % 2][:, h, :], T[u][:, h, :],
                                                 start=True, stop=True)
                            up(s.x_ready, last)
                        for u in range(2):
                            k = LEVELS * t0 + 2 * i + u
                            pe.wait_ge(s.x_copied.sem, k + 1)
                            pe.wait_ge(s.tt_ready.sem, summed(t0, i, u))
                            pe.wait_ge(s.att_ready.sem, t0 + u + 1)
                            for h in range(H2):
                                last = pe.matmul(ps[:, 4 * u + 1, h * P:(h + 1) * P], TT[u][:, h, :], X[u][:, h, :],
                                                 start=True, stop=True)
                            up(s.tx_ready, last)
                            for h in range(H2):
                                last = pe.matmul(ps[:, 4 * u + 2, h * P:(h + 1) * P], X[u][:, h, :], TT[u][:, h, :],
                                                 start=True, stop=True)
                            up(s.txt_ready, last)
                    for u in range(2):
                        t = t0 + u
                        pe.wait_ge(s.t_ready.sem, summed(t0, LEVELS, u))
                        pe.wait_ge(s.tt_ready.sem, summed(t0, LEVELS, u))
                        for h in range(H2):
                            last = pe.matmul(ps[:, 4 * u, h * 64:(h + 1) * 64], TT[u][:, h, :],
                                             vk[:, t, h, :, :].rearrange("p a c -> p (a c)"), start=True, stop=True)
                        up(s.uw_ready, last)
                        for h in range(H2):
                            last = pe.matmul(ps[32 * h:32 * h + 32, 4 * u + 1, 0:P], vk[:, t, h, 1, :], TT[u][:, h, :],
                                             start=True, stop=True)
                        up(s.wt_ready, last)
                    for u in range(2):
                        t = t0 + u
                        pe.wait_ge(s.uw_copied.sem, t + 1)
                        for h in range(H2):
                            pe.matmul(ps[:, 4 * u + 3, h * HD2:(h + 1) * HD2], att[u][:, h, :], uw[u][:, h, 0, :],
                                      start=True, stop=True)
                        for h in range(H2):
                            last = pe.matmul(ps[32 * h:32 * h + 32, 4 * u + 3, P:2 * P], uw[u][:, h, 1, :],
                                             att[u][:, h, :], start=True, stop=True)
                        up(s.out_ready, last)

            @block.scalar
            def _(act):
                norm.act(0, 0)
                for j in range(3):
                    act.wait_ge(s.conv_ready.sem, j + 1)
                    if j:
                        act.wait_ge(s.silu_done.sem, j)
                    act.activation(sg[:], ps[:, 2 + j, :], ACT.Sigmoid).then_inc(s.sigmoid_done.sem, 1)
                act.wait_ge(s.gates_ready.sem, 1)
                act.activation(bg[:].rearrange("p t g h -> p (t g h)"), ps[:, 0, 0:8 * NT],
                               ACT.Sigmoid).then_inc(s.sigmoid_done.sem, 1)
                for j in range(2):
                    act.wait_ge(s.turned.sem, j + 1)
                    act.activation(tok[:, j, :], ps[:, 5 + j, :], ACT.Copy).then_inc(s.tok_copied.sem, 1)
                for j in range(2):
                    act.wait_ge(s.rot_done.sem, 2 * j + 2)
                    act.activation(half_b[:, j, :], half_a[:, j, :], ACT.Square).then_inc(s.rot_squared.sem, 1)
                act.wait_ge(s.gamma_ready.sem, 1)
                act.activation(st.g[:, :, bass.ds(b, 1), :].rearrange("p t a c -> p t (a c)"),
                               ps[:, 1, 0:4 * NT].rearrange("p (t c) -> p t c", t=NT), ACT.Copy).then_inc(s.act.sem, 1)
                act.wait_ge(s.f_turned.sem, 1)
                act.activation(qT[:], ps[:, 2, :], ACT.Copy).then_inc(s.q_t.sem, 1)
                act.wait_ge(s.f_turned.sem, 2)
                for h in range(H2):
                    rows = slice(32 * h, 32 * h + 32)
                    act.activation(kT[rows, h, :], ps[rows, 3, :], ACT.Copy).then_inc(s.k_t.sem, 1)
                act.wait_ge(s.f_turned.sem, 3)
                act.activation(kbT[:], ps[:, 4, :], ACT.Copy).then_inc(s.kb_t.sem, 1)
                for t0 in range(0, NT, 2):
                    for u in range(2):
                        act.wait_ge(s.nt_ready.sem, t0 + u + 1)
                        if t0:
                            act.wait_ge(s.level_masked.sem, 2 * LEVELS * (t0 // 2))
                        act.activation(NT_raw[u][:], bank(4 * u + 1), ACT.Copy).then_inc(s.nt_raw.sem, 1)
                    for i in range(LEVELS):
                        for u in range(2):
                            k = LEVELS * t0 + 2 * i + u
                            act.wait_ge(s.x_ready.sem, k + 1)
                            if k >= 2:
                                act.wait_ge(s.txt_ready.sem, k - 1)
                            act.activation(X[u][:], bank(4 * u), ACT.Copy).then_inc(s.x_copied.sem, 1)
                    for u in range(2):
                        t = t0 + u
                        act.wait_ge(s.uw_ready.sem, t + 1)
                        if t0:
                            act.wait_ge(s.out_ready.sem, t - 1)
                            act.wait_ge(s.u_kept.sem, t - 1)
                        act.activation(uw[u][:].rearrange("p h a c -> p (h a c)"), ps[:, 4 * u, 0:2 * P],
                                       ACT.Copy).then_inc(s.uw_copied.sem, 1)
                        act.wait_ge(s.wt_ready.sem, t + 1)
                        act.activation(mine(st.wT, t), ps[:, 4 * u + 1, 0:P], ACT.Copy).then_inc(s.out_copied.sem, 1)
                    for u in range(2):
                        t = t0 + u
                        act.wait_ge(s.out_ready.sem, t + 1)
                        act.activation(mine(st.o, t), ps[:, 4 * u + 3, 0:P], ACT.Copy).then_inc(s.out_copied.sem, 1)

            @block.gpsimd
            def _(pool):
                pool.wait_ge(s.sigmoid_done.sem, 4)
                for t in range(NT):
                    up(s.pool if t < NT - 1 else s.gamma_wide, pool.tensor_copy(
                        wide[:, t, :].rearrange("p (h c) -> p h c", h=H2),
                        bg[:, t, 1, :].unsqueeze(2).to_broadcast([P, H2, HD2])))
                for j in range(2):
                    pool.wait_ge(s.tok_copied.sem, j + 1)
                    for half in range(2):
                        up(s.half_done, pool.tensor_tensor(halves(half_b[:, j, :])[:, :, half, :],
                                                           even_odd(tok[:, j, :])[:, :, 1 - half, :],
                                                           halves(m.c_sin[:])[:, :, half, :], ALU.mult))
                    up(s.base_done, pool.tensor_tensor(act3[:, j, :].rearrange("p (t h c) -> p t h c", t=NT, h=H2),
                                                       tok[:, j, :].rearrange("p (t h c) -> p t h c", t=NT, h=H2),
                                                       m.c_share[:].rearrange("p (t h c) -> p t h c", t=NT, h=H2),
                                                       ALU.mult))
                pool.wait_ge(s.k_norm.sem, 1)
                pool.tensor_copy(st.k[:, :, bass.ds(b, 1), :].rearrange("p t a c -> p t (a c)"),
                                 ktok[:]).then_inc(s.k_kept.sem, 1)
                for t0 in range(0, NT, 2):
                    for i in range(LEVELS):
                        for u in range(2):
                            k = LEVELS * t0 + 2 * i + u
                            if i == 0:
                                pool.wait_ge(s.nt_raw.sem, t0 + u + 1)
                            if k >= 4:
                                pool.wait_ge(s.x_ready.sem, k - 3)
                            up(s.level_masked, pool.tensor_tensor(NTs[u][i % 2][:], NT_raw[u][:],
                                                                  heads(m.c_level[:, i, :]), ALU.mult))
                    for u in range(2):
                        t = t0 + u
                        pool.wait_ge(s.uw_copied.sem, t + 1)
                        up(s.u_kept, pool.tensor_copy(mine(st.u, t).rearrange("p (h c) -> p h c", h=H2),
                                                      uw[u][:, :, 0, :]))

            @block.vector
            def _(dve):
                norm.dve(0, 1, xn)
                for j in range(3):
                    dve.wait_ge(s.sigmoid_done.sem, j + 1)
                    up(s.silu_done, dve.tensor_tensor(act3[:, j, :], ps[:, 2 + j, :], sg[:], ALU.mult))
                for j in range(2):
                    dve.wait_ge(s.tok_copied.sem, j + 1)
                    link(dve, s.dve, dve.tensor_tensor(halves(half_a[:, j, :]), even_odd(tok[:, j, :]),
                                                       halves(m.c_cos[:]), ALU.mult))
                    dve.wait_ge(s.half_done.sem, 2 * j + 2)
                    up(s.rot_done, dve.tensor_tensor(half_a[:, j, :], half_a[:, j, :], half_b[:, j, :], ALU.add))
                    dve.wait_ge(s.rot_done.sem, s.rot_done.n)
                    dve.wait_ge(s.base_done.sem, j + 1)
                    up(s.rot_done, dve.tensor_tensor(half_a[:, j, :], half_a[:, j, :], act3[:, j, :], ALU.add))
                dve.wait_ge(s.turned.sem, 3)
                dve.wait_ge(s.sigmoid_done.sem, 4)
                for t in range(NT):
                    up(s.v_weighed, dve.tensor_tensor(
                        vk[:, t, :, 0, :], ps[:, 7, t * P:(t + 1) * P].rearrange("p (h c) -> p h c", h=H2),
                        bg[:, t, 0, :].unsqueeze(2).to_broadcast([P, H2, HD2]), ALU.mult))
                for j in range(2):
                    dve.wait_ge(s.rot_squared.sem, j + 1)
                    link(dve, s.dve, dve.tensor_reduce(ssq[:, j, :], g16(half_b[:, j, :]), AX.X, ALU.add))
                flat = lambda a: a[:].rearrange("p j g -> p (j g)")
                link(dve, s.dve, dve.tensor_scalar(flat(ssq), flat(ssq), 1e-6, None, ALU.add))
                rsqrt_steps(dve, s.dve, flat(ssq), flat(rn), flat(rn_t))
                wide_rn = lambda j: rn[:, j, :].unsqueeze(2).to_broadcast([P, NT * H2, HD2])
                up(s.q_norm, dve.tensor_tensor(g16(half_a[:, 0, :]), g16(half_a[:, 0, :]), wide_rn(0), ALU.mult))
                up(s.k_norm, dve.tensor_tensor(g16(ktok[:].rearrange("p t c -> p (t c)")), g16(half_a[:, 1, :]),
                                               wide_rn(1), ALU.mult))
                dve.wait_ge(s.k_norm.sem, 1)
                for t in range(NT):
                    link(dve, s.dve, dve.tensor_tensor(
                        half_b[:, 0, t * P:(t + 1) * P].rearrange("p (h c) -> p h c", h=H2),
                        ktok[:, t, :].rearrange("p (h c) -> p h c", h=H2),
                        bg[:, t, 0, :].unsqueeze(2).to_broadcast([P, H2, HD2]), ALU.mult))
                    up(s.b_weighed, dve.tensor_copy(
                        vk[:, t, :, 1, :], half_b[:, 0, t * P:(t + 1) * P].rearrange("p (h c) -> p h c", h=H2)))
                for t0 in range(0, NT, 2):
                    for u in range(2):
                        t = t0 + u
                        dve.wait_ge(s.n_ready.sem, t + 1)
                        if t0:
                            dve.wait_ge(s.out_ready.sem, t - 1)
                        link(dve, s.dve, dve.tensor_tensor(T[u][:], bank(4 * u), heads(m.c_first[:, 0, :]), ALU.mult))
                        up(s.t_ready, dve.tensor_tensor(T[u][:], T[u][:], heads(m.ident[:]), ALU.add))
                        dve.wait_ge(s.nt_ready.sem, t + 1)
                        dve.wait_ge(s.nt_raw.sem, t + 1)
                        link(dve, s.dve, dve.tensor_tensor(TT[u][:], bank(4 * u + 1), heads(m.c_first[:, 1, :]),
                                                           ALU.mult))
                        up(s.tt_ready, dve.tensor_tensor(TT[u][:], TT[u][:], heads(m.ident[:]), ALU.add))
                        dve.wait_ge(s.at_ready.sem, t + 1)
                        up(s.att_ready, dve.tensor_tensor(att[u][:], bank(4 * u + 2), heads(m.c_causal[:]), ALU.mult))
                    for i in range(LEVELS):
                        for u in range(2):
                            k = LEVELS * t0 + 2 * i + u
                            dve.wait_ge(s.tx_ready.sem, k + 1)
                            dve.wait_ge(s.txt_ready.sem, k + 1)
                            dve.wait_ge(s.t_ready.sem, s.t_ready.n)
                            up(s.t_ready, dve.tensor_tensor(T[u][:], T[u][:], bank(4 * u + 1), ALU.add))
                            dve.wait_ge(s.tt_ready.sem, s.tt_ready.n)
                            up(s.tt_ready, dve.tensor_tensor(TT[u][:], TT[u][:], bank(4 * u + 2), ALU.add))
                    for u in range(2):
                        t = t0 + u
                        dve.wait_ge(s.out_ready.sem, t + 1)
                        dve.wait_ge(s.out_copied.sem, 4 * (t0 // 2) + 3 + u)
                        up(s.qp_done, dve.tensor_tensor(mine(st.qT, t), qT[:, t * P:(t + 1) * P],
                                                        ps[:, 4 * u + 3, P:2 * P], ALU.subtract))
        s.clear()


def delta_scan(m, ctx, st):
    nc, ps = m.nc, m.ps
    s = Signals(nc, ctx)
    (s.act, s.staged, s.staged_k, s.ws_ready, s.qs_ready, s.u_done, s.ku_ready, s.spread_dve, s.spread_act,
     s.stacked, s.o_done) = s.new(
        "act staged staged_k ws_ready qs_ready u_done ku_ready spread_dve spread_act stacked o_done")
    sb = lambda name, shape, dt=F32: ctx.enter_context(nc.sbuf_tensor(name, shape, dt))
    w_now, q_now, k_now, u_now = (sb("s_" + n, [P, B, P]) for n in ("w", "q", "k", "u"))
    stack, decayed = sb("s_stack", [P, B, HD2]), sb("s_decayed", [P, B, HD2])
    diag = sb("s_diag", [P, B, P])

    with nc.Block() as block:
        @block.vector
        def _(dve):
            up(s.dve, dve.memset(stack[:], 0.0))
            up(s.dve, dve.memset(diag[:], 0.0))
    s.clear()

    HB = B // 2
    with nc.Fori(0, NT, 1) as t:
        now = lambda a: a[:, bass.ds(t, 1), :, :].rearrange("p a b c -> p (a b) c")
        with nc.Block() as block:
            @block.tensor
            def _(pe):
                pe.wait_ge(s.staged.sem, 2)
                pe.wait_ge(s.staged_k.sem, 1)
                for r in range(4):
                    rows = slice(32 * r, 32 * r + 32)
                    if r:
                        pe.wait_ge(s.spread_dve.sem, 2 * r)
                        pe.wait_ge(s.spread_act.sem, 2 * r)
                    for b in range(B):
                        last = pe.matmul(ps[rows, b // HB, (b % HB) * P:(b % HB + 1) * P], w_now[:, b, rows], diag[:, b, :],
                                         start=True, stop=True)
                        if b == HB - 1 or b == B - 1:
                            up(s.ws_ready, last)
                    if r:
                        pe.wait_ge(s.o_done.sem, 2 * r)
                    for b in range(B):
                        last = pe.matmul(ps[rows, 2 + b // HB, (b % HB) * P:(b % HB + 1) * P], q_now[:, b, rows],
                                         diag[:, b, :], start=True, stop=True)
                    up(s.qs_ready, last)
                    if r:
                        pe.wait_ge(s.stacked.sem, r)
                    for b in range(B):
                        if b % HB == 0:
                            pe.wait_ge(s.u_done.sem, 2 * r + b // HB + 1)
                        for h in range(H2):
                            cols = slice(32 * h, 32 * h + 32)
                            last = pe.matmul(ps[cols, 4, b * HD2:(b + 1) * HD2], k_now[rows, b, cols],
                                             u_now[rows, b, cols], start=True, stop=True)
                    up(s.ku_ready, last)

            @block.scalar
            def _(act):
                act.activation(w_now[:], now(st.wT), ACT.Copy).then_inc(s.staged.sem, 1)
                act.activation(q_now[:], now(st.qT), ACT.Copy).then_inc(s.staged.sem, 1)
                for r in range(4):
                    act.wait_ge(s.stacked.sem, r + 1)
                    act.wait_ge(s.qs_ready.sem, r + 1)
                    for h in range(2):
                        blk = slice(32 * h, 32 * h + 32)
                        act.activation(diag[blk, :, blk], stack[blk, :, :], ACT.Copy).then_inc(s.spread_act.sem, 1)

            @block.vector
            def _(dve):
                up(s.staged_k, dve.tensor_copy(k_now[:], now(st.k)))
                for r in range(4):
                    rows = slice(32 * r, 32 * r + 32)
                    g = st.g[:, bass.ds(t, 1), :, r:r + 1].rearrange("p a b c -> p (a b c)")
                    if r:
                        dve.wait_ge(s.stacked.sem, r)
                        dve.wait_ge(s.spread_act.sem, 2 * r)
                    link(dve, s.dve, dve.tensor_tensor(decayed[:], stack[:], g.unsqueeze(2).to_broadcast([P, B, HD2]),
                                                       ALU.mult))
                    for half in range(2):
                        lo, hi = (0, HB) if half == 0 else (HB, B)
                        dve.wait_ge(s.ws_ready.sem, 2 * r + half + 1)
                        up(s.u_done, dve.tensor_tensor(
                            u_now[rows, lo:hi, :], now(st.u)[rows, lo:hi, :],
                            ps[rows, half, 0:(hi - lo) * P].rearrange("p (b c) -> p b c", c=P), ALU.subtract))
                    dve.wait_ge(s.ku_ready.sem, r + 1)
                    up(s.stacked, dve.tensor_tensor(stack[:], decayed[:],
                                                    ps[:, 4, 0:B * HD2].rearrange("p (b c) -> p b c", c=HD2), ALU.add))
                    dve.wait_ge(s.stacked.sem, r + 1)
                    for h in range(2, H2):
                        blk = slice(32 * h, 32 * h + 32)
                        up(s.spread_dve, dve.tensor_copy(diag[blk, :, blk], stack[blk, :, :]))
                    dve.wait_ge(s.qs_ready.sem, r + 1)
                    for half in range(2):
                        lo, hi = (0, HB) if half == 0 else (HB, B)
                        o = now(st.o)[rows, lo:hi, :]
                        up(s.o_done, dve.tensor_tensor(
                            o, o, ps[rows, 2 + half, 0:(hi - lo) * P].rearrange("p (b c) -> p b c", c=P), ALU.add))
        s.clear()


def delta_finish(m, ctx, st):
    nc, ps = m.nc, m.ps
    s = Signals(nc, ctx)
    (s.squared, s.o_norm, s.o_turned, s.o_t, s.core_ready, s.gate_ready, s.gate_done, s.frac, s.frac_squared,
     s.frac_var, s.frac_diag, s.frac_spread, s.frac_done, s.y_ready) = s.new(
        "squared o_norm o_turned o_t core_ready gate_ready gate_done frac frac_squared frac_var frac_diag "
        "frac_spread frac_done y_ready")
    sb = lambda name, shape, dt=F32: ctx.enter_context(nc.sbuf_tensor(name, shape, dt))
    PAD = 2 ** (DILATIONS - 1)
    xp = sb("f_xp", [P, PAD + S])
    xn = xp[:, PAD:PAD + S]
    osq, on, oT = sb("f_osq", [P, NT, P]), sb("f_on", [P, NT, P]), sb("f_oT", [P, S])
    ssq, rn, rn_t = (sb("f_" + n, [P, NT * H2]) for n in ("ssq", "rn", "rn_t"))
    frac, fsq, gate, y = sb("f_frac", [P, S]), sb("f_fsq", [P, S]), sb("f_gate", [P, S]), sb("f_y", [P, S])
    norm = Norm(m, s)

    with nc.Block() as block:
        @block.vector
        def _(dve):
            up(s.dve, dve.memset(xp[:], 0.0))
    s.clear()

    with nc.Fori(0, B, 1) as b:
        x_b = m.x[:, bass.ts(b, S)]
        o_b = st.o[:, :, bass.ds(b, 1), :].rearrange("p t a c -> p t (a c)")
        g16 = lambda a: a.rearrange("p t (h c) -> p (t h) c", h=H2)
        with nc.Block() as block:
            @block.tensor
            def _(pe):
                norm.pe(0, x_b, 0, 1)
                pe.wait_ge(s.ln_done.sem, 1)
                up(s.gate_ready, pe.matmul(ps[:, 2, :], m.c_gate_w[:], xn, start=True, stop=True))
                pe.wait_ge(s.o_norm.sem, 1)
                for t in range(NT):
                    last = pe.transpose(ps[:, 3, t * P:(t + 1) * P], on[:, t, :], m.ident[:])
                up(s.o_turned, last)
                pe.wait_ge(s.o_t.sem, 1)
                up(s.core_ready, pe.matmul(ps[:, 4, :], m.c_wo[:], oT[:], start=True, stop=True))
                pe.wait_ge(s.frac_squared.sem, 1)
                for t in range(NT):
                    last = pe.matmul(ps[:, 5, t:t + 1], fsq[:, t * P:(t + 1) * P], m.mean_col[:, 0:1],
                                     start=True, stop=True)
                up(s.frac_var, last)
                pe.wait_ge(s.frac_diag.sem, 1)
                up(s.frac_spread, pe.matmul(ps[:, 6, :], m.ones[:], m.diag[:], start=True, stop=True))
                pe.wait_ge(s.y_ready.sem, 1)
                norm.pe(1, y[:], 0, 1)

            @block.scalar
            def _(act):
                act.activation(osq[:], o_b, ACT.Square).then_inc(s.squared.sem, 1)
                norm.act(0, 0)
                act.wait_ge(s.gate_ready.sem, 1)
                act.activation(gate[:], ps[:, 2, :], ACT.Sigmoid, bias=m.c_gate_b[:, 0:1]).then_inc(s.gate_done.sem, 1)
                act.wait_ge(s.o_turned.sem, 1)
                act.activation(oT[:], ps[:, 3, :], ACT.Copy).then_inc(s.o_t.sem, 1)
                act.wait_ge(s.frac.sem, DILATIONS + 1)
                act.activation(fsq[:], frac[:], ACT.Square).then_inc(s.frac_squared.sem, 1)
                norm.act(1, 0)

            @block.vector
            def _(dve):
                norm.dve(0, 1, xn)
                dve.wait_ge(s.squared.sem, 1)
                link(dve, s.dve, dve.tensor_reduce(ssq[:], g16(osq[:]), AX.X, ALU.add))
                link(dve, s.dve, dve.tensor_scalar(ssq[:], ssq[:], 1.0 / HD2, 1e-5, ALU.mult, ALU.add))
                rsqrt_steps(dve, s.dve, ssq[:], rn[:], rn_t[:])
                for t in range(NT):
                    last = dve.tensor_tensor(on[:, t, :].rearrange("p (h c) -> p h c", h=H2),
                                             o_b[:, t, :].rearrange("p (h c) -> p h c", h=H2),
                                             rn[:, t * H2:(t + 1) * H2].unsqueeze(2).to_broadcast([P, H2, HD2]), ALU.mult)
                    if t < NT - 1:
                        up(s.dve, last)
                up(s.o_norm, last)
                dve.wait_ge(s.dve.sem, s.dve.n)
                dve.wait_ge(s.ln_done.sem, 1)
                up(s.frac, dve.tensor_scalar(frac[:], xn, m.c_frac_own[:, 0:1], None, ALU.mult))
                for i in range(DILATIONS):
                    dve.wait_ge(s.frac.sem, i + 1)
                    up(s.frac, dve.scalar_tensor_tensor(out=frac[:], in0=xp[:, PAD - 2 ** i:PAD - 2 ** i + S],
                                                        scalar=m.c_frac_w[:, i, 0:1], in1=frac[:], op0=ALU.mult,
                                                        op1=ALU.add))
                dve.wait_ge(s.frac_var.sem, 1)
                link(dve, s.dve, dve.tensor_scalar(m.var[:, 0:NT], ps[:, 5, 0:NT], 1.0, 1e-5, ALU.mult, ALU.add))
                rsqrt_steps(dve, s.dve, m.var[:, 0:NT], m.rstd[:, 0:NT], m.tmp[:, 0:NT])
                for t in range(NT):
                    last = dve.tensor_scalar(m.diag[:, t * P:(t + 1) * P], m.ident[:], m.rstd[:, t:t + 1], None,
                                             ALU.mult)
                    if t < NT - 1:
                        up(s.dve, last)
                up(s.frac_diag, last)
                dve.wait_ge(s.dve.sem, s.dve.n)
                dve.wait_ge(s.frac_spread.sem, 1)
                link(dve, s.dve, dve.scalar_tensor_tensor(out=frac[:], in0=frac[:], scalar=m.c_mix_w[:, 0:1],
                                                          in1=ps[:, 6, :], op0=ALU.mult, op1=ALU.mult))
                dve.wait_ge(s.gate_done.sem, 1)
                link(dve, s.dve, dve.tensor_tensor(frac[:], frac[:], gate[:], ALU.mult))
                dve.wait_ge(s.core_ready.sem, 1)
                up(s.y_ready, dve.tensor_tensor(y[:], frac[:], ps[:, 4, :], ALU.add))
                norm.dve(1, 1, y[:])
                dve.wait_ge(s.ln_done.sem, 2)
                up(s.dve, dve.tensor_tensor(x_b, x_b, y[:], ALU.add))
        s.clear()


def gated_block(m, ctx):
    nc, ps = m.nc, m.ps
    s = Signals(nc, ctx)
    (s.g_ready, s.u_ready, s.gate_done, s.silu_done, s.h_done, s.y_ready, s.y_copied) = s.new(
        "g_ready u_ready gate_done silu_done h_done y_ready y_copied")
    sb = lambda name, shape, dt=F32: ctx.enter_context(nc.sbuf_tensor(name, shape, dt))
    xn, y = sb("d_xn", [P, S]), sb("d_y", [P, S])
    sg, gated, h = sb("d_sg", [P, 2, S]), sb("d_gated", [P, 2, S]), sb("d_h", [P, HCH3, S])
    norm = Norm(m, s)

    with nc.Fori(0, B, 1) as b:
        x_b = m.x[:, bass.ts(b, S)]
        with nc.Block() as block:
            @block.tensor
            def _(pe):
                norm.pe(0, x_b, 0, 1)
                pe.wait_ge(s.ln_done.sem, 1)
                for c in range(HCH3):
                    if c == 2:
                        pe.wait_ge(s.h_done.sem, 1)
                    hid = slice(c * P, (c + 1) * P)
                    up(s.g_ready, pe.matmul(ps[:, 2 + 2 * (c % 2), :], m.d_gate[:, hid], xn[:], start=True, stop=True))
                    up(s.u_ready, pe.matmul(ps[:, 3 + 2 * (c % 2), :], m.d_up[:, hid], xn[:], start=True, stop=True))
                for c in range(HCH3):
                    pe.wait_ge(s.h_done.sem, c + 1)
                    last = pe.matmul(ps[:, 6, :], m.d_down[:, c, :], h[:, c, :], start=c == 0, stop=c == HCH3 - 1)
                up(s.y_ready, last)
                pe.wait_ge(s.y_copied.sem, 1)
                norm.pe(1, y[:], 0, 1)

            @block.scalar
            def _(act):
                norm.act(0, 0)
                for c in range(HCH3):
                    act.wait_ge(s.g_ready.sem, c + 1)
                    if c == 2:
                        act.wait_ge(s.silu_done.sem, 1)
                    act.activation(sg[:, c % 2, :], ps[:, 2 + 2 * (c % 2), :], ACT.Sigmoid).then_inc(s.gate_done.sem, 1)
                act.wait_ge(s.y_ready.sem, 1)
                act.activation(y[:], ps[:, 6, :], ACT.Copy).then_inc(s.y_copied.sem, 1)
                norm.act(1, 0)

            @block.vector
            def _(dve):
                norm.dve(0, 1, xn[:])
                for c in range(HCH3):
                    dve.wait_ge(s.gate_done.sem, c + 1)
                    if c == 2:
                        dve.wait_ge(s.h_done.sem, 1)
                    up(s.silu_done, dve.tensor_tensor(gated[:, c % 2, :], sg[:, c % 2, :], ps[:, 2 + 2 * (c % 2), :],
                                                      ALU.mult))
                    dve.wait_ge(s.silu_done.sem, c + 1)
                    dve.wait_ge(s.u_ready.sem, c + 1)
                    up(s.h_done, dve.tensor_tensor(h[:, c, :], gated[:, c % 2, :], ps[:, 3 + 2 * (c % 2), :], ALU.mult))
                norm.dve(1, 1, y[:])
                dve.wait_ge(s.ln_done.sem, 2)
                up(s.dve, dve.tensor_tensor(x_b, x_b, y[:], ALU.add))
        s.clear()


def build(nc, ins, out, blocks=range(4)):
    with ExitStack() as ctx:
        m = Store()
        m.nc = nc
        sb = lambda name, shape, dt=F32: ctx.enter_context(nc.sbuf_tensor(name, shape, dt))
        m.ps = ctx.enter_context(nc.psum_tensor("ps", [P, 8, S], F32))
        m.x = sb("x", [P, B * S])
        m.lnc, m.lnsq, m.diag = sb("lnc", [P, S]), sb("lnsq", [P, S]), sb("diag", [P, S])
        m.var, m.rstd, m.tmp = sb("var", [P, 64]), sb("rstd", [P, 64]), sb("tmp", [P, 64])
        loaded = ctx.enter_context(nc.semaphore("loaded"))
        ready = ctx.enter_context(nc.semaphore("ready"))
        loaded_b = ctx.enter_context(nc.semaphore("loaded_b"))
        ready_b = ctx.enter_context(nc.semaphore("ready_b"))
        loaded_d = ctx.enter_context(nc.semaphore("loaded_d"))
        ready_d = ctx.enter_context(nc.semaphore("ready_d"))
        loaded_c = ctx.enter_context(nc.semaphore("loaded_c"))
        ready_c = ctx.enter_context(nc.semaphore("ready_c"))
        chain_c = ctx.enter_context(nc.semaphore("chain_c"))
        stored = ctx.enter_context(nc.semaphore("stored"))
        small = {"ident": [P, P], "centre": [P, P], "ones": [P, P], "mean_col": [P, 1], "ones_rows": [P, 1]}
        m.ident, m.centre, m.ones, m.mean_col, m.ones_rows = (sb(n, shape) for n, shape in small.items())
        m.ident_bf = sb("ident_bf", [P, P], BF16)
        loads = [(t[:], ins[n]) for n, t in zip(small, (m.ident, m.centre, m.ones, m.mean_col, m.ones_rows))] + [(m.ident_bf[:], ins["ident_bf"])]
        loads.append((m.x[:], ins["xT"]))

        with ExitStack() as own:
            sa = lambda name, shape, dt=F32: own.enter_context(nc.sbuf_tensor(name, shape, dt))

            def taken(n, shape):
                dst = sa("a_" + n, shape)
                loads.append((dst[:], ins["a_" + n]))
                return dst

            m.wq, m.wk, m.wv, m.wo = (taken(n, [P, P]) for n in ("wq", "wk", "wv", "wo"))
            m.bq, m.bk, m.bo = (taken(n, [P, 1]) for n in ("bq", "bk", "bo"))
            m.bv = sa("a_bv", [P, P])
            loads.append((m.bv[:], ins["a_bv"].partition_broadcast(P)))
            m.bq_scaled = sa("a_bq_scaled", [P, 1])
            m.sel = sa("a_sel", [P, 2, NPAIR, 3, P], BF16)
            loads.append((m.sel[:], ins["a_sel"]))
            with nc.Block() as block:
                @block.sync
                def _(sp):
                    for dst, src in loads:
                        sp.dma_start(dst, src).then_inc(loaded, 16)
                    sp.wait_ge(loaded, 16 * len(loads))

                @block.vector
                def _(dve):
                    dve.wait_ge(loaded, 16 * len(loads))
                    dve.tensor_scalar(m.bq_scaled[:], m.bq[:], HD0 ** -0.5, None, ALU.mult).then_inc(ready, 1)
            if 0 in blocks:
                attention_block(m, own)
        if 1 in blocks:
            with ExitStack() as own:
                sa = lambda name, shape, dt=F32: own.enter_context(nc.sbuf_tensor(name, shape, dt))
                todo = []

                def load(dst, src):
                    todo.append((dst[:], src))
                    return dst

                m.layer = []
                for l in range(L1):
                    w = Store()
                    w.wqkv = load(sa(f"b_wqkv{l}", [P, 3 * INNER]), ins["b_wqkv"][l])
                    w.wo = load(sa(f"b_wo{l}", [P, 4, P]), ins["b_wo"][l])
                    w.w1 = load(sa(f"b_w1{l}", [P, 2 * HID1]), ins["b_w1"][l])
                    w.w2 = load(sa(f"b_w2{l}", [P, 3, P]), ins["b_w2"][l])
                    w.b1 = load(sa(f"b_b1{l}", [P, 6]), ins["b_b1"][l])
                    w.b2, w.ln_g, w.ln_b = (load(sa(f"b_{n}{l}", [P, 1]), ins["b_" + n][l])
                                            for n in ("b2", "ln_g", "ln_b"))
                    w.tab_direct = load(sa(f"b_direct{l}", [P, NT, 2, HD1]), ins["b_direct"])
                    w.tab_swap = load(sa(f"b_swap{l}", [P, NT, 2, HD1]), ins["b_swap"])
                    w.qk_scale = sa(f"b_qk_scale{l}", [P, 2, HD1])
                    for j, n in enumerate(("b_q_scale", "b_k_scale")):
                        todo.append((w.qk_scale[:, j, :], ins[n][l].partition_broadcast(P)))
                    m.layer.append(w)
                m.mask = load(sa("b_mask", [P, 3 * WIN], BF16), ins["b_mask"])
                with nc.Block() as block:
                    @block.sync
                    def _(sp):
                        for dst, src in todo:
                            sp.dma_start(dst, src).then_inc(loaded_b, 16)
                        sp.wait_ge(loaded_b, 16 * len(todo))

                    @block.vector
                    def _(dve):
                        dve.wait_ge(loaded_b, 16 * len(todo))
                        for w in m.layer:
                            for j in range(2):
                                for t in range(NT):
                                    dve.tensor_tensor(w.tab_direct[:, t, j, :], w.tab_direct[:, t, j, :],
                                                      w.qk_scale[:, j, :], ALU.mult).then_inc(ready_b, 1)
                                    for half in range(2):
                                        o, i = slice(32 * half, 32 * half + 32), slice(32 - 32 * half, 64 - 32 * half)
                                        dve.tensor_tensor(w.tab_swap[:, t, j, o], w.tab_swap[:, t, j, o],
                                                          w.qk_scale[:, j, i], ALU.mult).then_inc(ready_b, 1)
                local_block(m, own)
        if 2 in blocks:
            with ExitStack() as own:
                sa = lambda name, shape, dt=F32: own.enter_context(nc.sbuf_tensor(name, shape, dt))
                todo = []

                def load(name, shape, src=None):
                    dst = sa(name, shape)
                    todo.append((dst[:], ins[name] if src is None else src))
                    return dst

                m.c_wbg, m.c_chunk_mean = load("c_wbg", [P, 8]), load("c_chunk_mean", [P, 4])
                m.c_level, m.c_first = load("c_level", [P, LEVELS, P]), load("c_first", [P, 2, P])
                m.c_causal, m.c_cos, m.c_sin = load("c_causal", [P, P]), load("c_cos", [P, S]), load("c_sin", [P, S])
                m.c_wo, m.c_o_norm = load("c_wo", [P, P]), load("c_o_norm", [P, 1])
                m.c_gate_b = load("c_gate_b", [P, 1], ins["c_gate_b"].partition_broadcast(P))
                m.c_gate_col, m.c_mix_w = load("c_gate_col", [P, 1]), load("c_mix_w", [P, 1])
                m.c_frac_w = load("c_frac_w", [P, DILATIONS, 2])
                m.c_rot = load("c_rot", [P, H2], ins["c_rot"].partition_broadcast(P))
                m.c_taps, m.c_share, m.c_gate_w = sa("c_taps", [P, 3, TAPS, P]), sa("c_share", [P, S]), sa("c_gate_w", [P, P])
                m.c_frac_own = sa("c_frac_own", [P, 1])
                st = Store()
                st.wT, st.qT, st.k, st.u, st.o = (sa("st_" + n, [P, NT, B, P]) for n in ("wT", "qT", "k", "u", "o"))
                st.g = sa("st_g", [P, NT, B, 4])
                with ExitStack() as once:
                    so = lambda name, shape: once.enter_context(nc.sbuf_tensor(name, shape, F32))
                    w3, conv = so("c_w3", [P, 3, P]), so("c_conv", [P, 3, TAPS, P])
                    mix, share = so("c_mix", [P, H2]), so("c_share4", [P, H2])
                    todo += [(w3[:], ins["c_w3"]), (conv[:], ins["c_conv"].partition_broadcast(P))]
                    with nc.Block() as block:
                        @block.sync
                        def _(sp):
                            for dst, src in todo:
                                sp.dma_start(dst, src).then_inc(loaded_c, 16)

                        @block.scalar
                        def _(act):
                            act.wait_ge(loaded_c, 16 * len(todo))
                            act.activation(mix[:], m.c_rot[:], ACT.Sigmoid).then_inc(ready_c, 1)

                        @block.vector
                        def _(dve):
                            c = Count(chain_c)
                            dve.wait_ge(loaded_c, 16 * len(todo))
                            for j in range(3):
                                for tap in range(TAPS):
                                    up(c, dve.tensor_tensor(m.c_taps[:, j, tap, :], w3[:, j, :], conv[:, j, tap, :],
                                                            ALU.mult))
                            up(c, dve.tensor_scalar(m.c_gate_w[:], m.ones[:], m.c_gate_col[:, 0:1], None, ALU.mult))
                            up(c, dve.tensor_scalar(m.c_wo[:], m.c_wo[:], m.c_o_norm[:, 0:1], None, ALU.mult))
                            link(dve, c, dve.tensor_reduce(m.c_frac_own[:], m.c_frac_w[:, :, 1], AX.X, ALU.add))
                            up(c, dve.tensor_scalar(m.c_frac_own[:], m.c_frac_own[:], 2.0, None, ALU.add))
                            dve.wait_ge(ready_c, 1)
                            link(dve, c, dve.tensor_scalar(share[:], mix[:], -1.0, 1.0, ALU.mult, ALU.add))
                            link(dve, c, dve.memset(m.c_share[:], 1.0))
                            wide = lambda a: a[:].unsqueeze(2).to_broadcast([P, H2, HD2])
                            for tab, by in ((m.c_cos, mix), (m.c_sin, mix), (m.c_share, share)):
                                for t in range(NT):
                                    part = tab[:, t * P:(t + 1) * P].rearrange("p (h c) -> p h c", h=H2)
                                    up(c, dve.tensor_tensor(part, part, wide(by), ALU.mult))
                with ExitStack() as own1:
                    delta_prepare(m, own1, st)
                with ExitStack() as own2:
                    delta_scan(m, own2, st)
                with ExitStack() as own3:
                    delta_finish(m, own3, st)
        if 3 in blocks:
            with ExitStack() as own:
                sa = lambda name, shape, dt=F32: own.enter_context(nc.sbuf_tensor(name, shape, dt))
                ints = [(sa("d_gate_i", [P, HID3], I32), ins["d_gate"]), (sa("d_up_i", [P, HID3], I32), ins["d_up"]),
                        (sa("d_down_i", [P, HCH3, P], I32), ins["d_down"])]
                m.d_gate, m.d_up = sa("d_gate", [P, HID3]), sa("d_up", [P, HID3])
                m.d_down = sa("d_down", [P, HCH3, P])
                with nc.Block() as block:
                    @block.sync
                    def _(sp):
                        for dst, src in ints:
                            sp.dma_start(dst[:], src).then_inc(loaded_d, 16)

                    @block.vector
                    def _(dve):
                        dve.wait_ge(loaded_d, 16 * len(ints))
                        for dst, (src, _) in zip((m.d_gate, m.d_up, m.d_down), ints):
                            dve.tensor_scalar(dst[:], src[:], DEQUANT, None, ALU.mult).then_inc(ready_d, 1)
                gated_block(m, own)
        with nc.Block() as block:
            @block.sync
            def _(sp):
                sp.dma_start(out, m.x[:]).then_inc(stored, 16)
                sp.wait_ge(stored, 16)


def rotary_tables():
    f32 = np.float32
    half = np.arange(0, HD1, 2, dtype=f32)
    t = np.arange(S, dtype=f32)
    freqs = t[:, None] * (f32(1.0) / f32(10000.0) ** (half / f32(HD1)))[None, :]
    base = (half + f32(0.4 * HD1)) / f32(1.4 * HD1)
    scale = base[None, :] ** ((t - S // 2) / f32(WIN // 2))[:, None]
    direct, swap = np.zeros((S, 2, HD1), f32), np.zeros((S, 2, HD1), f32)
    for j, sc in enumerate((scale, 1.0 / scale)):
        direct[:, j] = np.concatenate([np.cos(freqs) * sc] * 2, axis=1)
        swap[:, j] = np.concatenate([-np.sin(freqs) * sc, np.sin(freqs) * sc], axis=1)
    tiles = lambda a: a.reshape(NT, P, 2, HD1).transpose(1, 0, 2, 3)
    return tiles(direct), tiles(swap)


def layout(inputs):
    f = {n: np.asarray(a) for n, a in inputs.items()}
    col = lambda a: np.ascontiguousarray(a).reshape(-1, 1)
    eye = np.eye(P, dtype=np.float32)
    bf16 = mybir.dt.np(BF16)
    d = {"xT": f["L0_attn_hidden_states"].reshape(B * S, P).T,
         "ident": eye, "centre": eye - np.float32(1.0 / P), "ones": np.ones((P, P), np.float32),
         "mean_col": np.full((P, 1), 1.0 / P, np.float32), "ident_bf": eye.astype(bf16)}
    for n in ("q", "k", "v", "o"):
        d["a_w" + n] = f["L0_attn_W" + n].T
    for n in ("q", "k", "o"):
        d["a_b" + n] = col(f["L0_attn_b" + n])
    d["a_bv"] = f["L0_attn_bv"]
    sel = np.zeros((P, 2, NPAIR, 3, P), np.float32)
    for w, slots in enumerate((Q_PARTS, K_PARTS)):
        for p in range(NPAIR):
            for a in range(2):
                for slot, part in enumerate(slots):
                    for e in range(HD0):
                        sel[(2 * p + a) * HD0 + e, w, p, part, 64 * a + slot * HD0 + e] = 1.0
    d["a_sel"] = sel.astype(bf16)
    rows = np.zeros((P, 1), np.float32)
    for a in range(2):
        rows[64 * a + MAX_ROW:64 * a + MAX_ROW + 3] = 1.0
    d["ones_rows"] = rows
    d["b_wqkv"] = f["L0_ffn_wqkv"]
    d["b_wo"] = f["L0_ffn_wo"].reshape(L1, 4, P, P).transpose(0, 2, 1, 3)
    d["b_w1"] = f["L0_ffn_w1"]
    w2 = np.zeros((L1, P, 3, P), np.float32)
    b1 = np.zeros((L1, P, 6), np.float32)
    for c, (c0, rows) in enumerate(HCH):
        w2[:, 0:rows, c, :] = f["L0_ffn_w2"][:, c0:c0 + rows, :]
        b1[:, 0:rows, c] = f["L0_ffn_b1"][:, c0:c0 + rows]
        b1[:, 0:rows, 3 + c] = f["L0_ffn_b1"][:, HID1 + c0:HID1 + c0 + rows]
    d["b_w2"], d["b_b1"] = w2, b1
    for n in ("b2", "ln_g", "ln_b"):
        d["b_" + n] = f["L0_ffn_" + n].reshape(L1, P, 1)
    d["b_q_scale"], d["b_k_scale"] = f["L0_ffn_q_scale"], f["L0_ffn_k_scale"]
    direct, swap = rotary_tables()
    d["b_direct"], d["b_swap"] = direct, swap
    q, k = np.arange(P)[:, None], np.arange(3 * WIN)[None, :] - WIN
    d["b_mask"] = np.where((k <= q) & (k >= q - WIN), 0.0, MASKED).astype(bf16)
    d["c_wbg"] = np.concatenate([f["L1_attn_Wb"], f["L1_attn_Wgamma"]], axis=1)
    i, j = np.arange(P)[:, None], np.arange(P)[None, :]
    same = i // CHUNK == j // CHUNK
    d["c_chunk_mean"] = (i // CHUNK == np.arange(4)[None, :]) / np.float32(CHUNK)
    below = lambda half: (i // (2 * half) == j // (2 * half)) & (i % (2 * half) >= half) & (j % (2 * half) < half)
    d["c_level"] = np.stack([-below(2 ** (1 + n)).T.astype(np.float32) for n in range(LEVELS)], axis=1)
    d["c_first"] = np.stack([-below(1).astype(np.float32), -below(1).T.astype(np.float32)], axis=1)
    d["c_causal"] = (same & (i <= j)).astype(np.float32)
    inv = np.float32(1.0) / np.float32(10000.0) ** (np.arange(0, HD2, 2, dtype=np.float32) / np.float32(HD2))
    ang = np.arange(S, dtype=np.float32)[:, None] * inv[None, :]
    for n, halves in (("c_cos", (np.cos(ang), np.cos(ang))), ("c_sin", (-np.sin(ang), np.sin(ang)))):
        one = np.concatenate(halves, axis=1).reshape(NT, P, 1, HD2)
        d[n] = np.broadcast_to(one, (NT, P, H2, HD2)).transpose(1, 0, 2, 3).reshape(P, S)
    d["c_wo"], d["c_o_norm"] = f["L1_attn_Wo"], col(np.tile(f["L1_attn_o_norm_w"], H2))
    d["c_gate_b"], d["c_gate_col"] = f["L1_attn_frac_gate_b"], col(f["L1_attn_frac_gate_w"])
    d["c_frac_w"] = f["L1_attn_frac_conv_w"].transpose(1, 0, 2)
    d["c_mix_w"], d["c_rot"] = col(f["L1_attn_mixer_norm_w"]), f["L1_attn_rot_logit"]
    d["c_w3"] = np.stack([f["L1_attn_W" + n] for n in "qkv"], axis=1)
    d["c_conv"] = np.stack([f["L1_attn_conv_" + n].T for n in "qkv"], axis=0)
    for n in d:
        if n.startswith("c_"):
            d[n] = d[n].astype(np.float32)
    d["d_gate"], d["d_up"] = f["L1_ffn_w_gate"].T, f["L1_ffn_w_up"].T
    d["d_down"] = f["L1_ffn_w_down"].T.reshape(HCH3, P, P).transpose(1, 0, 2)
    return {n: np.ascontiguousarray(a) for n, a in d.items()}


def kernel(**inputs):
    import concourse.bacc as bacc
    from concourse.bass_utils import run_bass_kernel_spmd

    arrays = layout(inputs)
    nc = bacc.Bacc("TRN2", target_bir_lowering=False, num_devices=1)
    ins = {n: nc.dram_tensor("in_" + n, a.shape, mybir.dt.from_np(a.dtype), kind="ExternalInput").ap()
           for n, a in arrays.items()}
    out = nc.dram_tensor("out_xT", (P, B * S), F32, kind="ExternalOutput").ap()
    build(nc, ins, out)
    r = run_bass_kernel_spmd(nc, [{"in_" + n: a for n, a in arrays.items()}], core_ids=[0])
    xT = np.asarray(r.results[0]["out_xT"])
    return np.ascontiguousarray(xT.T).reshape(B, S, P)
```

```python
from contextlib import ExitStack

import numpy as np
import concourse.bass as bass
from concourse import mybir

ALU = mybir.AluOpType
ACT = mybir.ActivationFunctionType
AX = mybir.AxisListType
F32 = mybir.dt.float32
BF16 = mybir.dt.bfloat16
I32 = mybir.dt.int32

P = 128
B, S = 8, 512
NT = S // P
LN_EPS = 1e-5

H0, HD0 = 16, 8
NPAIR = H0 // 2
NGROUP = H0 // 4
Q_PARTS = (0, 0, 1, 1, 0, 2)
K_PARTS = (0, 1, 0, 1, 2, 0)
MAX_ROW = len(Q_PARTS) * HD0

L1, H1, HD1, WIN = 2, 8, 64, 64
INNER = H1 * HD1
HID1 = int(P * 4 * 2 / 3)
HCH = [(c, min(P, HID1 - c)) for c in range(0, HID1, P)]
MASKED = -1e30

H2, HD2, TAPS, CHUNK, DILATIONS = 4, 32, 4, 32, 4
LEVELS = 4

HID3 = 384
HCH3 = HID3 // P
DEQUANT = float(np.float32(1.0 / 127.0))

MAGIC = 0x5F3759DF


class Count:

    def __init__(self, sem):
        self.sem, self.n = sem, 0


def up(count, ins):
    ins.then_inc(count.sem, 1)
    count.n += 1
    return count.n


def link(eng, count, ins):
    up(count, ins)
    eng.wait_ge(count.sem, count.n)


class Signals:

    def __init__(self, nc, ctx, batch=0):
        self.nc, self.ctx, self.batch, self.every = nc, ctx, batch, []
        (self.ln_centred, self.ln_copied, self.ln_squared, self.ln_var, self.ln_diag, self.ln_spread, self.ln_done,
         self.dve) = self.new("ln_centred ln_copied ln_squared ln_var ln_diag ln_spread ln_done dve")

    def new(self, names):
        counts = [Count(self.ctx.enter_context(self.nc.semaphore(f"{n}_{self.batch}"))) for n in names.split()]
        self.every += counts
        return counts


def clear(nc, signals):
    with nc.Block() as block:
        @block.gpsimd
        def _(pool):
            for s in signals:
                for count in s.every:
                    pool.sem_clear(count.sem)
    for s in signals:
        for count in s.every:
            count.n = 0


def in_turn(*programs):
    programs = list(programs)
    while programs:
        programs = [p for p in programs if next(p, "done") != "done"]


class Store:
    pass


def rsqrt_steps(dve, c, v, y, t):
    link(dve, c, dve.tensor_scalar(t.bitcast(I32), v.bitcast(I32), 1, None, ALU.arith_shift_right))
    link(dve, c, dve.tensor_scalar(y.bitcast(I32), t.bitcast(I32), -1.0, float(MAGIC), ALU.mult, ALU.add))
    for _ in range(3):
        link(dve, c, dve.tensor_tensor(t, y, y, ALU.mult))
        link(dve, c, dve.scalar_tensor_tensor(out=t, in0=t, scalar=-0.5, in1=v, op0=ALU.mult, op1=ALU.mult))
        link(dve, c, dve.scalar_tensor_tensor(out=y, in0=t, scalar=1.5, in1=y, op0=ALU.add, op1=ALU.mult))


class Norm:

    def __init__(self, m, sems, u=0):
        self.m, self.s, b = m, sems, m.norm_buffers[u]
        self.lnc, self.lnsq, self.diag, self.var, self.rstd, self.tmp = b.lnc, b.lnsq, b.diag, b.var, b.rstd, b.tmp

    def pe(self, n, src, bank, other):
        m, s, pe, ps = self.m, self.s, self.m.nc.tensor, self.m.ps
        up(s.ln_centred, pe.matmul(ps[:, bank, :], m.centre[:], src, start=True, stop=True))
        yield
        pe.wait_ge(s.ln_squared.sem, n + 1)
        for t in range(NT):
            last = pe.matmul(ps[:, other, t:t + 1], self.lnsq[:, t * P:(t + 1) * P], m.mean_col[:, 0:1],
                             start=True, stop=True)
        up(s.ln_var, last)
        yield
        pe.wait_ge(s.ln_diag.sem, n + 1)
        up(s.ln_spread, pe.matmul(ps[:, other, :], m.ones[:], self.diag[:], start=True, stop=True))
        yield

    def act(self, n, bank):
        m, s, act, ps = self.m, self.s, self.m.nc.scalar, self.m.ps
        act.wait_ge(s.ln_centred.sem, n + 1)
        if n:
            act.wait_ge(s.ln_done.sem, n)
        act.activation(self.lnc[:], ps[:, bank, :], ACT.Copy).then_inc(s.ln_copied.sem, 1)
        act.activation(self.lnsq[:], ps[:, bank, :], ACT.Square).then_inc(s.ln_squared.sem, 1)
        yield

    def dve(self, n, other, out, eps=LN_EPS):
        m, s, dve, ps = self.m, self.s, self.m.nc.vector, self.m.ps
        dve.wait_ge(s.ln_var.sem, n + 1)
        link(dve, s.dve, dve.tensor_scalar(self.var[:, 0:NT], ps[:, other, 0:NT], 1.0, eps, ALU.mult, ALU.add))
        rsqrt_steps(dve, s.dve, self.var[:, 0:NT], self.rstd[:, 0:NT], self.tmp[:, 0:NT])
        for t in range(NT):
            last = dve.tensor_scalar(self.diag[:, t * P:(t + 1) * P], m.ident[:], self.rstd[:, t:t + 1], None,
                                     ALU.mult)
            if t < NT - 1:
                up(s.dve, last)
        up(s.ln_diag, last)
        yield
        dve.wait_ge(s.dve.sem, s.dve.n)
        dve.wait_ge(s.ln_spread.sem, n + 1)
        dve.wait_ge(s.ln_copied.sem, n + 1)
        up(s.ln_done, dve.tensor_tensor(out, self.lnc[:], ps[:, other, :], ALU.mult))
        yield


def attention_block(m, ctx):
    nc, ps = m.nc, m.ps
    s = Signals(nc, ctx)
    (s.qk_proj, s.v_proj, s.qk_f32, s.v_done, s.parts, s.placed, s.q_stack, s.k_stack, s.s_ready, s.maxed,
     s.m_parts, s.m_turned, s.q_full, s.st_ready, s.exp_done, s.av_done, s.o_copied, s.o_turned, s.att_done,
     s.a_turned, s.a_copied, s.y_ready, s.y_copied) = s.new(
        "qk_proj v_proj qk_f32 v_done parts placed q_stack k_stack s_ready maxed m_parts m_turned q_full "
        "st_ready exp_done av_done o_copied o_turned att_done a_turned a_copied y_ready y_copied")
    sb = lambda name, shape, dt: ctx.enter_context(nc.sbuf_tensor(name, shape, dt))
    xn = sb("a_xn", [P, S], F32)
    qk = sb("a_qk", [P, 2, S], F32)
    rest = sb("a_rest", [P, S], F32)
    parts = sb("a_parts", [P, 2, 3, S], BF16)
    kst = sb("a_kst", [P, H0, S], BF16)
    qst = sb("a_qst", [P, NPAIR, S], BF16)
    va = sb("a_va", [P, NT, H0, 32], F32)
    negm = sb("a_negm", [P, H0, NT], F32)
    mrest = sb("a_mrest", [P, NT, 2], F32)
    mx = sb("a_mx", [P, 2, NT, P], BF16)
    prob = sb("a_prob", [P, 2, 4, 2, S], F32)
    osb = sb("a_osb", [P, S], F32)
    rec = sb("a_rec", [P, NT, 4], F32)
    att = sb("a_att", [P, NT, P], F32)
    aT = sb("a_aT", [P, S], F32)
    y = sb("a_y", [P, S], F32)
    mxv = mx[:].rearrange("p r t (a c) -> p r t a c", a=2)
    norm = Norm(m, s)

    with nc.Block() as block:
        @block.vector
        def _(dve):
            up(s.dve, dve.memset(kst[:], 0.0))
            up(s.dve, dve.memset(mx[:], 0.0))
            link(dve, s.dve, dve.memset(va[:], 0.0))
            up(s.dve, dve.memset(va[:, :, :, HD0:HD0 + 1], 1.0))
    clear(nc, [s])

    with nc.Fori(0, B, 1) as b:
        x_b = m.x[:, bass.ts(b, S)]
        with nc.Block() as block:
            @block.tensor
            def _(pe):
                for _ in norm.pe(0, x_b, 0, 1):
                    pass
                pe.wait_ge(s.ln_done.sem, 1)
                up(s.qk_proj, pe.matmul(ps[:, 2, :], m.wq[:], xn[:], start=True, stop=True))
                up(s.qk_proj, pe.matmul(ps[:, 3, :], m.wk[:], xn[:], start=True, stop=True))
                for t in range(NT):
                    last = pe.matmul(ps[:, 4, t * P:(t + 1) * P], xn[:, t * P:(t + 1) * P], m.wv[:],
                                     start=True, stop=True)
                up(s.v_proj, last)
                for n in range(2 * NPAIR):
                    p, which = n // 2, n % 2
                    pe.wait_ge(s.parts.sem, which + 1)
                    if n < 4:
                        pe.wait_ge(s.v_done.sem, 1)
                    else:
                        pe.wait_ge((s.k_stack if which else s.q_stack).sem, (n - 4) // 2 * (1 + which) + 1 + which)
                    for part in range(3):
                        last = pe.matmul(ps[:, 4 + n % 4, :], m.sel[:, which, p, part, :],
                                         parts[:, which, part, :], start=part == 0, stop=part == 2)
                    up(s.placed, last)

                def scores(g, i):
                    h, qt = 4 * g + i // 4, i % 4
                    n = 16 * g + i
                    if n == 0:
                        pe.wait_ge(s.ln_done.sem, 1)
                    pe.wait_ge(s.q_stack.sem, h // 2 + 1)
                    pe.wait_ge(s.k_stack.sem, h + 1)
                    if n >= 2:
                        pe.wait_ge(s.maxed.sem, n - 1)
                    up(s.s_ready, pe.matmul(ps[:, n % 2, :], qst[:, h // 2, qt * P:(qt + 1) * P], kst[:, h, :],
                                            start=True, stop=True))

                def turn_max(g):
                    pe.wait_ge(s.m_parts.sem, g + 1)
                    if g == 0:
                        pe.wait_ge(s.k_stack.sem, H0)
                    for r in range(2):
                        if g or r:
                            pe.wait_ge(s.q_full.sem, 2 * g + r)
                        if g >= 2:
                            pe.wait_ge(s.att_done.sem, g - 1)
                        for t in range(NT):
                            last = pe.matmul(ps[:, 7, t * P:(t + 1) * P], mx[:, r, t, :], m.ident_bf[:],
                                             start=True, stop=True)
                        up(s.m_turned, last)

                def scores_t(g, i):
                    n = 8 * g + i
                    kp, h = i // 4, 4 * g + i % 4
                    pe.wait_ge(s.q_full.sem, h // 2 + 1)
                    if n == 0:
                        pe.wait_ge(s.qk_f32.sem, 2)
                        pe.wait_ge(s.q_stack.sem, NPAIR)
                        pe.wait_ge(s.k_stack.sem, H0)
                    if n >= 2:
                        pe.wait_ge(s.exp_done.sem, n - 1)
                    for k2 in range(2):
                        kt = 2 * kp + k2
                        last = pe.matmul(ps[:, 2 + 2 * (n % 2) + k2, :], kst[:, h, kt * P:(kt + 1) * P],
                                         qst[:, h // 2, :], start=True, stop=True)
                    up(s.st_ready, last)

                def weigh(c):
                    g, kp = c // 2, c % 2
                    pe.wait_ge(s.exp_done.sem, 4 * (c + 1))
                    if kp == 0 and g:
                        pe.wait_ge(s.o_copied.sem, g)
                    for k2 in range(2):
                        for j in range(4):
                            last = pe.matmul(ps[32 * j:32 * j + 32, 6, :], va[:, 2 * kp + k2, 4 * g + j, :],
                                             prob[:, c % 2, j, k2, :], start=kp == 0 and k2 == 0,
                                             stop=kp == 1 and k2 == 1)
                    up(s.av_done, last)

                def turn_out(g):
                    pe.wait_ge(s.o_copied.sem, g + 1)
                    pe.wait_ge(s.q_full.sem, min(2 * g + 4, NPAIR))
                    if g:
                        pe.wait_ge(s.att_done.sem, g)
                    for t in range(NT):
                        last = pe.transpose(ps[:, 7, t * P:(t + 1) * P], osb[:, t * P:(t + 1) * P], m.ident[:])
                    up(s.o_turned, last)

                for i in range(16):
                    scores(0, i)
                turn_max(0)
                for g in range(NGROUP):
                    for i in range(8):
                        scores_t(g, i)
                        if g + 1 < NGROUP:
                            scores(g + 1, 2 * i)
                            scores(g + 1, 2 * i + 1)
                        if i % 4 == 1 and 2 * g + i // 4 > 0:
                            weigh(2 * g + i // 4 - 1)
                        if i == 5 and g:
                            turn_out(g - 1)
                    if g + 1 < NGROUP:
                        turn_max(g + 1)
                weigh(2 * NGROUP - 1)
                turn_out(NGROUP - 1)
                pe.wait_ge(s.att_done.sem, NGROUP)
                for t in range(NT):
                    last = pe.transpose(ps[:, 0, t * P:(t + 1) * P], att[:, t, :], m.ident[:])
                up(s.a_turned, last)
                pe.wait_ge(s.a_copied.sem, 1)
                up(s.y_ready, pe.matmul(ps[:, 1, :], m.wo[:], aT[:], start=True, stop=True))
                pe.wait_ge(s.y_copied.sem, 1)
                for _ in norm.pe(1, y[:], 2, 3):
                    pass

            @block.scalar
            def _(act):
                for _ in norm.act(0, 0):
                    pass
                act.wait_ge(s.qk_proj.sem, 1)
                act.activation(qk[:, 0, :], ps[:, 2, :], ACT.Identity, bias=m.bq_scaled[:, 0:1],
                               scale=HD0 ** -0.5).then_inc(s.qk_f32.sem, 1)
                act.wait_ge(s.qk_proj.sem, 2)
                act.activation(qk[:, 1, :], ps[:, 3, :], ACT.Identity, bias=m.bk[:, 0:1]).then_inc(s.qk_f32.sem, 1)
                for p in range(NPAIR):
                    act.wait_ge(s.placed.sem, 2 * p + 1)
                    act.activation(qst[:, p, :], ps[:, 4 + (2 * p) % 4, :], ACT.Copy).then_inc(s.q_stack.sem, 1)
                for c in range(2 * NGROUP):
                    for j in range(4):
                        n = 4 * c + j
                        act.wait_ge(s.st_ready.sem, n + 1)
                        if j == 0 and c >= 2:
                            act.wait_ge(s.av_done.sem, c - 1)
                        act.activation(prob[:, c % 2, j, :, :],
                                       ps[:, 2 + 2 * (n % 2):4 + 2 * (n % 2), :], ACT.Exp).then_inc(s.exp_done.sem, 1)
                    if c % 2 == 0 and c:
                        act.wait_ge(s.av_done.sem, c)
                        if c > 2:
                            act.wait_ge(s.o_turned.sem, c // 2 - 1)
                        act.activation(osb[:], ps[:, 6, :], ACT.Copy).then_inc(s.o_copied.sem, 1)
                act.wait_ge(s.av_done.sem, 2 * NGROUP)
                act.wait_ge(s.o_turned.sem, NGROUP - 1)
                act.activation(osb[:], ps[:, 6, :], ACT.Copy).then_inc(s.o_copied.sem, 1)
                act.wait_ge(s.a_turned.sem, 1)
                act.activation(aT[:], ps[:, 0, :], ACT.Copy).then_inc(s.a_copied.sem, 1)
                act.wait_ge(s.y_ready.sem, 1)
                act.activation(y[:], ps[:, 1, :], ACT.Identity, bias=m.bo[:, 0:1]).then_inc(s.y_copied.sem, 1)
                for _ in norm.act(1, 2):
                    pass

            @block.vector
            def _(dve):
                for _ in norm.dve(0, 1, xn[:]):
                    pass
                dve.wait_ge(s.v_proj.sem, 1)
                for t in range(NT):
                    last = dve.tensor_tensor(va[:, t, :, 0:HD0],
                                             ps[:, 4, t * P:(t + 1) * P].rearrange("p (h d) -> p h d", h=H0),
                                             m.bv[:].rearrange("p (h d) -> p h d", h=H0), ALU.add)
                    if t < NT - 1:
                        up(s.dve, last)
                up(s.v_done, last)
                for w in range(2):
                    dve.wait_ge(s.qk_f32.sem, w + 1)
                    link(dve, s.dve, dve.tensor_copy(parts[:, w, 0, :], qk[:, w, :]))
                    link(dve, s.dve, dve.tensor_tensor(rest[:], qk[:, w, :], parts[:, w, 0, :], ALU.subtract))
                    link(dve, s.dve, dve.tensor_copy(parts[:, w, 1, :], rest[:]))
                    up(s.parts, dve.tensor_tensor(parts[:, w, 2, :], rest[:], parts[:, w, 1, :], ALU.subtract))
                    dve.wait_ge(s.parts.sem, w + 1)
                for p in range(NPAIR):
                    dve.wait_ge(s.placed.sem, 2 * p + 2)
                    for a in range(2):
                        rows = slice(64 * a, 64 * a + 64)
                        up(s.k_stack, dve.tensor_scalar(kst[rows, 2 * p + a, :], ps[rows, 4 + (2 * p + 1) % 4, :],
                                                        m.ones_rows[rows, 0:1], None, ALU.add))

                def maxima(g, i):
                    n = 16 * g + i
                    dve.wait_ge(s.s_ready.sem, n + 1)
                    up(s.maxed, dve.tensor_reduce(negm[:, 4 * g + i // 4, i % 4:i % 4 + 1], ps[:, n % 2, :], AX.X,
                                                  ALU.max, negate=True))

                def full_q(g):
                    dve.wait_ge(s.maxed.sem, 16 * (g + 1))
                    if g:
                        dve.wait_ge(s.m_turned.sem, 2 * g)
                    for r in range(2):
                        neg = negm[:, 4 * g + 2 * r:4 * g + 2 * r + 2, :].rearrange("p a t -> p t a")
                        link(dve, s.dve, dve.tensor_copy(mxv[:, r, :, :, MAX_ROW], neg))
                        link(dve, s.dve, dve.tensor_tensor(mrest[:], neg, mxv[:, r, :, :, MAX_ROW], ALU.subtract))
                        link(dve, s.dve, dve.tensor_copy(mxv[:, r, :, :, MAX_ROW + 1], mrest[:]))
                        last = dve.tensor_tensor(mxv[:, r, :, :, MAX_ROW + 2], mrest[:],
                                                 mxv[:, r, :, :, MAX_ROW + 1], ALU.subtract)
                        if r == 0:
                            link(dve, s.dve, last)
                    up(s.m_parts, last)
                    for r in range(2):
                        p = 2 * g + r
                        dve.wait_ge(s.m_turned.sem, p + 1)
                        up(s.q_full, dve.tensor_tensor(qst[:, p, :], qst[:, p, :], ps[:, 7, :], ALU.add))

                def finish(g):
                    dve.wait_ge(s.o_turned.sem, g + 1)
                    o = ps[:, 7, :].rearrange("p (t j c) -> p t j c", t=NT, j=4)
                    link(dve, s.dve, dve.reciprocal(rec[:], o[:, :, :, HD0]))
                    up(s.att_done, dve.tensor_tensor(
                        att[:, :, 32 * g:32 * g + 32].rearrange("p t (j d) -> p t j d", j=4), o[:, :, :, 0:HD0],
                        rec[:].unsqueeze(3).to_broadcast([P, NT, 4, HD0]), ALU.mult))

                for i in range(16):
                    maxima(0, i)
                full_q(0)
                for g in range(NGROUP):
                    for i in range(8):
                        if g + 1 < NGROUP:
                            maxima(g + 1, 2 * i)
                            maxima(g + 1, 2 * i + 1)
                        if i == 5 and g:
                            finish(g - 1)
                    if g + 1 < NGROUP:
                        full_q(g + 1)
                finish(NGROUP - 1)
                for _ in norm.dve(1, 3, y[:]):
                    pass
                dve.wait_ge(s.ln_done.sem, 2)
                up(s.dve, dve.tensor_tensor(x_b, x_b, y[:], ALU.add))
        clear(nc, [s])


def local_block(m, ctx):
    nc = m.nc
    sb = lambda name, shape, dt=F32: ctx.enter_context(nc.sbuf_tensor(name, shape, dt))
    signals, buffers = [], []
    for u in range(2):
        s, own = Signals(nc, ctx, u), Store()
        (s.act, s.shifted, s.qkv_ready, s.q_raw, s.k_raw, s.v_raw, s.squared, s.summed, s.k_scaled,
         s.swapped, s.rotated, s.q_turned, s.k_turned, s.q_t, s.k_t, s.scores_ready, s.neg_max, s.exp_done,
         s.own_turned, s.past_turned, s.own_kept, s.past_kept, s.o_ready, s.o_scaled, s.o_turned, s.o_t, s.res_ready,
         s.stream, s.ga_ready, s.gelu_done, s.h_done, s.down_ready) = s.new(
            "act shifted qkv_ready q_raw k_raw v_raw squared summed k_scaled swapped rotated q_turned k_turned "
            "q_t k_t scores_ready neg_max exp_done own_turned past_turned own_kept past_kept o_ready o_scaled "
            "o_turned o_t res_ready stream ga_ready gelu_done h_done down_ready")
        signals.append(s)
        own.y, own.hT, own.hn = (sb(f"b_{n}{u}", [P, S]) for n in ("y", "hT", "hn"))
        own.raw, own.v = sb(f"b_raw{u}", [P, NT, 2, INNER]), sb(f"b_v{u}", [P, NT, INNER])
        own.ssq, own.rn, own.rn_t = (sb(f"b_{n}{u}", [P, NT, 2, H1]) for n in ("ssq", "rn", "rn_t"))
        own.rq = sb(f"b_rq{u}", [P, NT, H1])
        own.rot = sb(f"b_rot{u}", [P, 2, INNER])
        own.qT, own.kT = sb(f"b_qT{u}", [P, 4, P]), sb(f"b_kT{u}", [P, H1, S])
        own.prob, own.pT = sb(f"b_prob{u}", [P, H1, 2 * P]), sb(f"b_pT{u}", [P, 2, 8, P])
        own.nmax, own.rden = sb(f"b_nmax{u}", [P, H1]), sb(f"b_rden{u}", [P, H1])
        own.nbias, own.den = sb(f"b_nbias{u}", [P, 2, H1]), sb(f"b_den{u}", [P, 2, H1])
        n = m.norm_buffers[u]
        own.on, own.swap = n.diag, n.both
        own.sq = own.pT[:].rearrange("p f c k -> p (f c k)")[:, 0:2 * INNER].rearrange("p (j c) -> p j c", j=2)
        own.gel = own.rot
        own.oT = own.raw[:].rearrange("p t j (c k) -> p t j c k", c=4)[:, :, 0, :, :]
        own.hm = own.v
        buffers.append(own)

    with nc.Block() as block:
        @block.vector
        def _(dve):
            for s, o in zip(signals, buffers):
                up(s.dve, dve.memset(o.kT[:], 0.0))
                up(s.dve, dve.memset(o.prob[:], 0.0))
                up(s.dve, dve.memset(o.hT[:], 0.0))
    clear(nc, signals)

    with nc.Fori(0, B // 2, 1) as b:
        x_pair = m.x[:, bass.ts(b, 2 * S)]
        with nc.Block() as block:
            @block.tensor
            def _(pe):
                def program(u):
                    s, o, ps, norm = signals[u], buffers[u], m.ps, Norm(m, signals[u], u)
                    k0 = 4 * u
                    sc = ps[:, k0:k0 + 2, :].rearrange("p b c -> p (b c)").rearrange("p (h c) -> p h c", h=4)
                    yield from norm.pe(0, x_pair[:, u * S:(u + 1) * S], k0, k0 + 1)
                    for l in range(L1):
                        w = m.layer[l]
                        pe.wait_ge(s.shifted.sem, 4 * l + 2)
                        pe.wait_ge(s.stream.sem, 2 * l + 1)
                        for n in range(3 * NT):
                            t, j = n // 3, n % 3
                            if n >= 4:
                                pe.wait_ge((s.q_raw, s.k_raw, s.v_raw)[(n - 4) % 3].sem, NT * l + (n - 4) // 3 + 1)
                            up(s.qkv_ready, pe.matmul(ps[:, k0 + n % 4, :], o.hT[:, t * P:(t + 1) * P],
                                                      w.wqkv[:, j * INNER:(j + 1) * INNER], start=True, stop=True))
                            yield
                        pe.wait_ge(s.q_raw.sem, NT * (l + 1))
                        pe.wait_ge(s.k_raw.sem, NT * (l + 1))
                        pe.wait_ge(s.v_raw.sem, NT * (l + 1))

                        def turn(t):
                            n = NT * l + t
                            pe.wait_ge(s.rotated.sem, n + 1)
                            for j, turned in enumerate((s.q_turned, s.k_turned)):
                                if j:
                                    pe.wait_ge(s.q_t.sem, n + 1)
                                elif n:
                                    pe.wait_ge(s.k_t.sem, 2 * n)
                                    if t != 1 or l:
                                        pe.wait_ge(s.own_kept.sem, 2 * (n - 1 if t else n))
                                for c in range(4):
                                    last = pe.transpose(ps[:, k0 + 2, c * P:(c + 1) * P],
                                                        o.rot[:, j, c * P:(c + 1) * P], m.ident[:])
                                up(turned, last)
                                yield

                        def scores(t, f):
                            n = NT * l + t
                            lo = P if t == 0 else WIN
                            pe.wait_ge(s.q_t.sem, n + 1)
                            pe.wait_ge(s.k_t.sem, 2 * n + 2)
                            if 2 * n + f:
                                pe.wait_ge(s.exp_done.sem, 4 * (2 * n + f))
                            for hh in range(4):
                                h = 4 * f + hh
                                dst = sc[:, hh, lo:2 * P]
                                pe.matmul(dst, o.qT[:, h // 2, :], o.kT[:, h, t * P + lo - P:(t + 1) * P],
                                          start=True, stop=False)
                                last = pe.matmul(dst, m.ident_bf[:], m.mask[:, lo - WIN:3 * WIN], start=False, stop=True)
                            up(s.scores_ready, last)

                        def turn_probs(t, f):
                            n = 2 * (NT * l + t) + f
                            past = 2 * (NT - 1) * l + 2 * (t - 1) + f
                            pe.wait_ge(s.exp_done.sem, 4 * n + 4)
                            if n:
                                pe.wait_ge(s.own_kept.sem, n)
                            pe.wait_ge(s.k_t.sem, 2 * (NT * l + min(t + 2, NT)))
                            for hh in range(4):
                                last = pe.transpose(ps[:, k0 + 2, hh * P:(hh + 1) * P],
                                                    o.prob[:, 4 * f + hh, P:2 * P], m.ident[:])
                            up(s.own_turned, last)
                            if t:
                                if past:
                                    pe.wait_ge(s.past_kept.sem, past)
                                pe.wait_ge(s.o_t.sem, NT * l + t)
                                for hh in range(4):
                                    last = pe.transpose(ps[:, k0 + 3, hh * P:(hh + 1) * P],
                                                        o.prob[:, 4 * f + hh, 0:P], m.ident[:])
                                up(s.past_turned, last)

                        def weigh(t):
                            n = NT * l + t
                            if n:
                                pe.wait_ge(s.o_t.sem, n)
                            past = 2 * (NT - 1) * l + 2 * t
                            pe.wait_ge(s.own_kept.sem, 2 * n + 2)
                            if past:
                                pe.wait_ge(s.past_kept.sem, past)
                            for h in range(H1):
                                for c in (1, 0):
                                    if c == 0 and t == 0:
                                        continue
                                    last = pe.matmul(ps[:, k0 + 3, h * HD1:(h + 1) * HD1],
                                                     o.pT[:, h // 4, 4 * c + h % 4, :],
                                                     o.v[:, t - 1 + c, h * HD1:(h + 1) * HD1],
                                                     start=c == 1, stop=c == 0 or t == 0)
                            up(s.o_ready, last)
                            yield
                            pe.wait_ge(s.o_scaled.sem, n + 1)
                            for c in range(4):
                                last = pe.transpose(ps[:, k0 + 3, c * P:(c + 1) * P], o.on[:, c * P:(c + 1) * P],
                                                    m.ident[:])
                            up(s.o_turned, last)

                        for t in range(NT + 1):
                            if t < NT:
                                yield from turn(t)
                            for f in range(2):
                                if t:
                                    turn_probs(t - 1, f)
                                    yield
                                if t < NT:
                                    scores(t, f)
                                    yield
                            if t:
                                yield from weigh(t - 1)
                                yield
                        pe.wait_ge(s.o_t.sem, NT * (l + 1))
                        for c in range(4):
                            last = pe.matmul(ps[:, k0, :], w.wo[:, c, :], o.oT[:, :, c, :], start=c == 0, stop=c == 3)
                        up(s.res_ready, last)
                        yield
                        pe.wait_ge(s.shifted.sem, 4 * l + 4)
                        yield from norm.pe(1 + l, o.hT[:], k0 + 1, k0 + 2)
                        pe.wait_ge(s.act.sem, l + 1)
                        for c, (c0, rows) in enumerate(HCH):
                            if c == 2:
                                pe.wait_ge(s.h_done.sem, 3 * l + 1)
                            g_bank, a_bank = k0 + 2 * (c % 2), k0 + 2 * (c % 2) + 1
                            pe.matmul(ps[0:rows, g_bank, :], w.w1[:, HID1 + c0:HID1 + c0 + rows], o.hn[:],
                                      start=True, stop=True)
                            up(s.ga_ready, pe.matmul(ps[0:rows, a_bank, :], w.w1[:, c0:c0 + rows], o.hn[:],
                                                     start=True, stop=True))
                            yield
                        pe.wait_ge(s.h_done.sem, 3 * l + 2)
                        for c, (c0, rows) in enumerate(HCH):
                            if c == 2:
                                yield
                                pe.wait_ge(s.h_done.sem, 3 * l + c + 1)
                            last = pe.matmul(ps[:, k0 + 2, :], w.w2[0:rows, c, :], o.hm[0:rows, c, :],
                                             start=c == 0, stop=c == 2)
                        up(s.down_ready, last)
                        yield
                    pe.wait_ge(s.stream.sem, 1 + 2 * L1)
                    yield from norm.pe(1 + L1, o.y[:], k0, k0 + 1)

                in_turn(program(0), program(1))

            @block.scalar
            def _(act):
                def program(u):
                    s, o, ps, norm = signals[u], buffers[u], m.ps, Norm(m, signals[u], u)
                    k0 = 4 * u
                    sc = ps[:, k0:k0 + 2, :].rearrange("p b c -> p (b c)").rearrange("p (h c) -> p h c", h=4)
                    yield from norm.act(0, k0)

                    def shift(n):
                        act.wait_ge(s.stream.sem, n + 1)
                        act.activation(o.hT[0:64, :], o.y[0:64, :], ACT.Copy).then_inc(s.shifted.sem, 1)
                        act.activation(o.hT[64:P, 1:S], o.y[64:P, 0:S - 1], ACT.Copy).then_inc(s.shifted.sem, 1)

                    for l in range(L1):
                        w = m.layer[l]
                        shift(2 * l)
                        yield
                        for t in range(NT):
                            n = NT * l + t
                            act.wait_ge(s.qkv_ready.sem, 3 * n + 1)
                            act.activation(o.raw[:, t, 0, :], ps[:, k0 + (3 * t) % 4, :],
                                           ACT.Copy).then_inc(s.q_raw.sem, 1)
                            yield
                            act.wait_ge(s.k_raw.sem, n + 1)
                            act.wait_ge(s.q_raw.sem, n + 1)
                            if n:
                                act.wait_ge(s.summed.sem, n)
                            if l and t == 0:
                                act.wait_ge(s.o_ready.sem, NT * l)
                            act.activation(o.sq, o.raw[:, t, :, :], ACT.Square).then_inc(s.squared.sem, 1)
                            yield
                            yield
                        for t in range(NT + 1):
                            n = NT * l + t
                            if t < NT:
                                act.wait_ge(s.q_turned.sem, n + 1)
                                if n:
                                    act.wait_ge(s.scores_ready.sem, 2 * n)
                                act.activation(o.qT[:], ps[:, k0 + 2, :].rearrange("p (c k) -> p c k", c=4),
                                               ACT.Copy).then_inc(s.q_t.sem, 1)
                                yield
                                act.wait_ge(s.k_turned.sem, n + 1)
                                for a in range(2):
                                    rows = slice(64 * a, 64 * a + 64)
                                    act.activation(o.kT[rows, a::2, t * P:(t + 1) * P],
                                                   ps[rows, k0 + 2, :].rearrange("p (c k) -> p c k", c=4),
                                                   ACT.Copy).then_inc(s.k_t.sem, 1)
                                yield
                            for f in range(2):
                                if t:
                                    k = 2 * (n - 1) + f
                                    act.wait_ge(s.own_turned.sem, k + 1)
                                    if k >= 2:
                                        act.wait_ge(s.o_ready.sem, k // 2)
                                    act.activation(o.pT[:, f, 4:8, :],
                                                   ps[:, k0 + 2, :].rearrange("p (c k) -> p c k", c=4),
                                                   ACT.Copy).then_inc(s.own_kept.sem, 1)
                                    yield
                                if t < NT:
                                    lo = P if t == 0 else WIN
                                    act.wait_ge(s.neg_max.sem, 2 * n + f + 1)
                                    if n >= 2:
                                        act.wait_ge(s.o_scaled.sem, n - 1)
                                    if n:
                                        act.wait_ge(s.own_turned.sem, 2 * n + f - 1)
                                        past = 2 * (NT - 1) * l + 2 * (t - 1) + f - 1
                                        if t and past > 0:
                                            act.wait_ge(s.past_turned.sem, past)
                                    for hh in range(4):
                                        h = 4 * f + hh
                                        act.activation(o.prob[:, h, lo:2 * P], sc[:, hh, lo:2 * P], ACT.Exp,
                                                       bias=o.nbias[:, t % 2, h:h + 1], scale=o.rq[:, t, h:h + 1],
                                                       accum_out=o.den[:, t % 2, h:h + 1]).then_inc(s.exp_done.sem, 1)
                                    yield
                            if t:
                                act.wait_ge(s.o_turned.sem, n)
                                act.activation(o.oT[:, t - 1, :, :], ps[:, k0 + 3, :].rearrange("p (c k) -> p c k", c=4),
                                               ACT.Copy).then_inc(s.o_t.sem, 1)
                                yield
                        shift(2 * l + 1)
                        yield
                        yield from norm.act(1 + l, k0 + 1)
                        act.wait_ge(s.ln_done.sem, 2 + l)
                        up(s.act, act.activation(o.hn[:], o.hn[:], ACT.Identity, bias=w.ln_b[:, 0:1],
                                                 scale=w.ln_g[:, 0:1]))
                        yield
                        for c, (c0, rows) in enumerate(HCH):
                            k = 3 * l + c
                            act.wait_ge(s.ga_ready.sem, k + 1)
                            if k >= 2:
                                act.wait_ge(s.h_done.sem, k - 1)
                            act.activation(o.gel[0:rows, c % 2, :], ps[0:rows, k0 + 2 * (c % 2), :], ACT.Gelu,
                                           bias=w.b1[0:rows, 3 + c:4 + c]).then_inc(s.gelu_done.sem, 1)
                            yield
                    yield from norm.act(1 + L1, k0)

                in_turn(program(0), program(1))

            @block.gpsimd
            def _(pool):
                def program(u):
                    s, o = signals[u], buffers[u]
                    for l in range(L1):
                        w = m.layer[l]
                        for t in range(NT):
                            n = NT * l + t
                            pool.wait_ge(s.k_scaled.sem, n + 1)
                            if n:
                                pool.wait_ge(s.rotated.sem, n)
                            src = o.raw[:, t, :, :].rearrange("p j (h d) -> p j h d", h=H1)
                            dst = o.swap[:].rearrange("p j (h d) -> p j h d", h=H1)
                            for half in range(2):
                                to, fro = slice(32 * half, 32 * half + 32), slice(32 - 32 * half, 64 - 32 * half)
                                for j in range(2):
                                    up(s.swapped, pool.tensor_tensor(
                                        dst[:, j, :, to], src[:, j, :, fro],
                                        w.tab_swap[:, t, j, to].unsqueeze(1).to_broadcast([P, H1, 32]), ALU.mult))
                            yield

                in_turn(program(0), program(1))

            @block.vector
            def _(dve):
                def program(u):
                    s, o, ps, norm = signals[u], buffers[u], m.ps, Norm(m, signals[u], u)
                    k0 = 4 * u
                    sc = ps[:, k0:k0 + 2, :].rearrange("p b c -> p (b c)").rearrange("p (h c) -> p h c", h=4)
                    heads = lambda a: a.rearrange("p (h d) -> p h d", h=H1)
                    yield from norm.dve(0, k0 + 1, o.y[:])
                    dve.wait_ge(s.ln_done.sem, 1)
                    up(s.stream, dve.tensor_scalar(o.y[:], o.y[:], 1.0, None, ALU.mult))
                    yield
                    for l in range(L1):
                        w = m.layer[l]
                        def rotate(t):
                            n = NT * l + t
                            kk = heads(o.raw[:, t, 1, :])
                            up(s.k_scaled, dve.tensor_tensor(
                                kk, kk, o.rn[:, t, 1, :].unsqueeze(2).to_broadcast([P, H1, HD1]), ALU.mult))
                            dve.wait_ge(s.k_scaled.sem, n + 1)
                            if n:
                                dve.wait_ge(s.k_turned.sem, n)
                            for j in range(2):
                                up(s.dve, dve.tensor_tensor(
                                    heads(o.rot[:, j, :]), heads(o.raw[:, t, j, :]),
                                    w.tab_direct[:, t, j, :].unsqueeze(1).to_broadcast([P, H1, HD1]), ALU.mult))
                            yield
                            dve.wait_ge(s.dve.sem, s.dve.n)
                            dve.wait_ge(s.swapped.sem, 4 * (n + 1))
                            up(s.rotated, dve.tensor_tensor(o.rot[:], o.rot[:], o.swap[:], ALU.add))
                            dve.wait_ge(s.rotated.sem, n + 1)
                            yield

                        def norms(lo, hi):
                            dve.wait_ge(s.summed.sem, NT * l + hi)
                            flat = lambda a: a[:, lo:hi, :, :].rearrange("p t j h -> p (t j h)")
                            link(dve, s.dve, dve.tensor_scalar(flat(o.ssq), flat(o.ssq), 1e-24, None, ALU.max))
                            rsqrt_steps(dve, s.dve, flat(o.ssq), flat(o.rn), flat(o.rn_t))
                            link(dve, s.dve, dve.tensor_scalar(o.rq[:, lo:hi, :], o.rn[:, lo:hi, 0, :], 8.0, None,
                                                               ALU.mult))

                        first = None
                        for t in range(NT):
                            n = NT * l + t
                            dve.wait_ge(s.qkv_ready.sem, 3 * n + 2)
                            up(s.k_raw, dve.tensor_copy(o.raw[:, t, 1, :], ps[:, k0 + (3 * t + 1) % 4, :]))
                            yield
                            dve.wait_ge(s.qkv_ready.sem, 3 * n + 3)
                            up(s.v_raw, dve.tensor_copy(o.v[:, t, :], ps[:, k0 + (3 * t + 2) % 4, :]))
                            if t:
                                dve.wait_ge(s.squared.sem, n)
                                up(s.summed, dve.tensor_reduce(o.ssq[:, t - 1, :, :],
                                                               o.sq.rearrange("p j (h d) -> p j h d", h=H1),
                                                               AX.X, ALU.add))
                            yield
                            if t == 1:
                                norms(0, 1)
                                first = rotate(0)
                            if t >= 1:
                                next(first, None)
                        dve.wait_ge(s.squared.sem, NT * (l + 1))
                        up(s.summed, dve.tensor_reduce(o.ssq[:, NT - 1, :, :],
                                                       o.sq.rearrange("p j (h d) -> p j h d", h=H1), AX.X, ALU.add))
                        norms(1, NT)
                        for t in range(NT + 1):
                            n = NT * l + t
                            if t + 1 < NT:
                                following = rotate(t + 1)
                                next(following)
                                yield
                            for f in range(2):
                                if t > 1:
                                    k = 2 * (n - 1) + f
                                    dve.wait_ge(s.past_turned.sem, 2 * (NT - 1) * l + 2 * (t - 2) + f + 1)
                                    dve.wait_ge(s.o_ready.sem, k // 2)
                                    up(s.past_kept, dve.tensor_copy(
                                        o.pT[:, f, 0:4, :], ps[:, k0 + 3, :].rearrange("p (c k) -> p c k", c=4)))
                                    yield
                                if t < NT:
                                    lo = P if t == 0 else WIN
                                    hs = slice(4 * f, 4 * f + 4)
                                    dve.wait_ge(s.scores_ready.sem, 2 * n + f + 1)
                                    link(dve, s.dve, dve.tensor_reduce(o.nmax[:, hs], sc[:, :, lo:2 * P], AX.X, ALU.max,
                                                                       negate=True))
                                    if n >= 2:
                                        dve.wait_ge(s.exp_done.sem, 8 * (n - 1))
                                    up(s.neg_max, dve.tensor_tensor(o.nbias[:, t % 2, hs], o.nmax[:, hs],
                                                                    o.rq[:, t, hs], ALU.mult))
                                    yield
                                if f == 0 and t + 1 < NT:
                                    next(following)
                                    yield
                            if t:
                                dve.wait_ge(s.o_ready.sem, n)
                                link(dve, s.dve, dve.reciprocal(o.rden[:], o.den[:, (t - 1) % 2, :]))
                                up(s.o_scaled, dve.tensor_tensor(
                                    heads(o.on[:]), heads(ps[:, k0 + 3, :]),
                                    o.rden[:].unsqueeze(2).to_broadcast([P, H1, HD1]), ALU.mult))
                                yield
                        dve.wait_ge(s.res_ready.sem, l + 1)
                        up(s.stream, dve.tensor_tensor(o.y[:], o.y[:], ps[:, k0, :], ALU.add))
                        yield
                        yield from norm.dve(1 + l, k0 + 2, o.hn[:])
                        for c, (c0, rows) in enumerate(HCH):
                            k = 3 * l + c
                            dve.wait_ge(s.gelu_done.sem, k + 1)
                            up(s.h_done, dve.scalar_tensor_tensor(
                                out=o.hm[0:rows, c, :], in0=ps[0:rows, k0 + 2 * (c % 2) + 1, :],
                                scalar=w.b1[0:rows, c:c + 1], in1=o.gel[0:rows, c % 2, :], op0=ALU.add, op1=ALU.mult))
                            yield
                        dve.wait_ge(s.down_ready.sem, l + 1)
                        up(s.stream, dve.scalar_tensor_tensor(out=o.y[:], in0=ps[:, k0 + 2, :], scalar=w.b2[:, 0:1],
                                                              in1=o.y[:], op0=ALU.add, op1=ALU.add))
                        yield
                    yield from norm.dve(1 + L1, k0 + 1, o.hn[:])
                    dve.wait_ge(s.ln_done.sem, 2 + L1)
                    x_b = x_pair[:, u * S:(u + 1) * S]
                    up(s.dve, dve.tensor_tensor(x_b, x_b, o.hn[:], ALU.add))

                in_turn(program(0), program(1))
        clear(nc, signals)


def delta_prepare(m, ctx, st):
    nc, ps = m.nc, m.ps
    s = Signals(nc, ctx)
    (s.act, s.pool, s.conv_ready, s.gates_ready, s.sigmoid_done, s.silu_done, s.turned, s.tok_copied,
     s.half_done, s.base_done, s.rot_done, s.rot_squared, s.k_norm, s.q_norm, s.b_weighed, s.v_weighed,
     s.f_turned, s.q_t, s.kb_t, s.k_t, s.gamma_ready, s.gamma_wide, s.n_ready, s.nt_ready, s.at_ready, s.nt_raw,
     s.level_masked, s.t1_masked, s.tt_ready, s.t_ready, s.att_ready, s.x_ready, s.x_copied, s.tx_ready,
     s.txt_ready, s.uw_ready, s.wt_ready, s.uw_copied, s.out_ready, s.out_copied, s.qp_done, s.u_kept, s.k_kept) = s.new(
        "act pool conv_ready gates_ready sigmoid_done silu_done turned tok_copied half_done base_done "
        "rot_done rot_squared k_norm q_norm b_weighed v_weighed f_turned q_t kb_t k_t gamma_ready gamma_wide "
        "n_ready nt_ready at_ready nt_raw level_masked t1_masked tt_ready t_ready att_ready x_ready x_copied "
        "tx_ready txt_ready uw_ready wt_ready uw_copied out_ready out_copied qp_done u_kept k_kept")
    sb = lambda name, shape, dt=F32: ctx.enter_context(nc.sbuf_tensor(name, shape, dt))
    xp = sb("c_xp", [P, TAPS - 1 + S])
    xn = xp[:, TAPS - 1:TAPS - 1 + S]
    sg, act3 = sb("c_sg", [P, S]), sb("c_act3", [P, 3, S])
    bg, wide = sb("c_bg", [P, NT, 2, H2]), sb("c_wide", [P, NT, P])
    tok, half_a, half_b = sb("c_tok", [P, 2, S]), sb("c_half_a", [P, 2, S]), sb("c_half_b", [P, 2, S])
    ssq, rn, rn_t = (sb("c_" + n, [P, 2, NT * H2]) for n in ("ssq", "rn", "rn_t"))
    ktok = sb("c_ktok", [P, NT, P])
    vk = sb("c_vk", [P, NT, H2, 2, HD2])
    qT, kbT, kT = sb("c_qT", [P, S]), sb("c_kbT", [P, S]), sb("c_kT", [P, H2, S])
    four = lambda name: [sb(f"c_{name}{u}", [P, H2, P]) for u in range(2)]
    T, TT, X, NT_raw, att = four("T"), four("TT"), four("X"), four("NT"), four("att")
    NTs = [[sb(f"c_NTs{u}{i}", [P, H2, P]) for i in range(2)] for u in range(2)]
    uw = [sb(f"c_uw{u}", [P, H2, 2, HD2]) for u in range(2)]
    norm = Norm(m, s)
    heads = lambda a: a.unsqueeze(1).to_broadcast([P, H2, P])
    bank = lambda k: ps[:, k, :].rearrange("p (h c) -> p h c", h=H2)
    g16 = lambda a: a.rearrange("p (g c) -> p g c", c=HD2)
    even_odd = lambda a: a.rearrange("p (g i two) -> p g two i", two=2, i=HD2 // 2)
    halves = lambda a: a.rearrange("p (g two i) -> p g two i", two=2, i=HD2 // 2)

    def summed(t0, i, u):
        return (LEVELS + 1) * t0 + 2 * i + u + 1

    with nc.Block() as block:
        @block.vector
        def _(dve):
            up(s.dve, dve.memset(kT[:], 0.0))
            up(s.dve, dve.memset(xp[:], 0.0))
    clear(nc, [s])

    with nc.Fori(0, B, 1) as b:
        x_b = m.x[:, bass.ts(b, S)]
        mine = lambda a, t: a[:, t, bass.ds(b, 1), :].rearrange("p a c -> p (a c)")
        with nc.Block() as block:
            @block.tensor
            def _(pe):
                for _ in norm.pe(0, x_b, 0, 1):
                    pass
                pe.wait_ge(s.ln_done.sem, 1)
                for j in range(3):
                    for tap in range(TAPS):
                        last = pe.matmul(ps[:, 2 + j, :], m.c_taps[:, j, tap, :], xp[:, tap:tap + S],
                                         start=tap == 0, stop=tap == TAPS - 1)
                    up(s.conv_ready, last)
                for t in range(NT):
                    last = pe.matmul(ps[:, 0, t * 8:t * 8 + 8], xn[:, t * P:(t + 1) * P], m.c_wbg[:],
                                     start=True, stop=True)
                up(s.gates_ready, last)
                for j in range(3):
                    pe.wait_ge(s.silu_done.sem, j + 1)
                    for t in range(NT):
                        last = pe.transpose(ps[:, 5 + j, t * P:(t + 1) * P], act3[:, j, t * P:(t + 1) * P], m.ident[:])
                    up(s.turned, last)
                pe.wait_ge(s.pool.sem, NT - 1)
                pe.wait_ge(s.gamma_wide.sem, 1)
                for t in range(NT):
                    last = pe.matmul(ps[:, 1, t * 4:t * 4 + 4], wide[:, t, :], m.c_chunk_mean[:], start=True, stop=True)
                up(s.gamma_ready, last)
                pe.wait_ge(s.q_norm.sem, 1)
                for t in range(NT):
                    last = pe.transpose(ps[:, 2, t * P:(t + 1) * P], half_a[:, 0, t * P:(t + 1) * P], m.ident[:])
                up(s.f_turned, last)
                pe.wait_ge(s.k_norm.sem, 1)
                for t in range(NT):
                    last = pe.transpose(ps[:, 3, t * P:(t + 1) * P], ktok[:, t, :], m.ident[:])
                up(s.f_turned, last)
                pe.wait_ge(s.b_weighed.sem, NT)
                for t in range(NT):
                    last = pe.transpose(ps[:, 4, t * P:(t + 1) * P], half_b[:, 0, t * P:(t + 1) * P], m.ident[:])
                up(s.f_turned, last)
                pe.wait_ge(s.q_t.sem, 1)
                pe.wait_ge(s.kb_t.sem, 1)
                pe.wait_ge(s.k_t.sem, H2)
                pe.wait_ge(s.v_weighed.sem, NT)
                for t0 in range(0, NT, 2):
                    for u in range(2):
                        t, tile = t0 + u, slice((t0 + u) * P, (t0 + u + 1) * P)
                        if t0:
                            pe.wait_ge(s.qp_done.sem, t - 1)
                            pe.wait_ge(s.out_copied.sem, 2 * t0)
                            pe.wait_ge(s.uw_copied.sem, t - 1)
                        for h in range(H2):
                            last = pe.matmul(ps[:, 4 * u, h * P:(h + 1) * P], kbT[:, tile], kT[:, h, tile],
                                             start=True, stop=True)
                        up(s.n_ready, last)
                        for h in range(H2):
                            last = pe.matmul(ps[:, 4 * u + 1, h * P:(h + 1) * P], kT[:, h, tile], kbT[:, tile],
                                             start=True, stop=True)
                        up(s.nt_ready, last)
                        for h in range(H2):
                            last = pe.matmul(ps[:, 4 * u + 2, h * P:(h + 1) * P], kT[:, h, tile], qT[:, tile],
                                             start=True, stop=True)
                        up(s.at_ready, last)
                    for i in range(LEVELS):
                        for u in range(2):
                            k = LEVELS * t0 + 2 * i + u
                            pe.wait_ge(s.level_masked.sem, k + 1)
                            pe.wait_ge(s.t_ready.sem, summed(t0, i, u))
                            if i:
                                pe.wait_ge(s.x_copied.sem, k - 1)
                            for h in range(H2):
                                last = pe.matmul(ps[:, 4 * u, h * P:(h + 1) * P], NTs[u][i % 2][:, h, :], T[u][:, h, :],
                                                 start=True, stop=True)
                            up(s.x_ready, last)
                        for u in range(2):
                            k = LEVELS * t0 + 2 * i + u
                            pe.wait_ge(s.x_copied.sem, k + 1)
                            pe.wait_ge(s.tt_ready.sem, summed(t0, i, u))
                            pe.wait_ge(s.att_ready.sem, t0 + u + 1)
                            for h in range(H2):
                                last = pe.matmul(ps[:, 4 * u + 1, h * P:(h + 1) * P], TT[u][:, h, :], X[u][:, h, :],
                                                 start=True, stop=True)
                            up(s.tx_ready, last)
                            for h in range(H2):
                                last = pe.matmul(ps[:, 4 * u + 2, h * P:(h + 1) * P], X[u][:, h, :], TT[u][:, h, :],
                                                 start=True, stop=True)
                            up(s.txt_ready, last)
                    for u in range(2):
                        t = t0 + u
                        pe.wait_ge(s.t_ready.sem, summed(t0, LEVELS, u))
                        pe.wait_ge(s.tt_ready.sem, summed(t0, LEVELS, u))
                        for h in range(H2):
                            last = pe.matmul(ps[:, 4 * u, h * 64:(h + 1) * 64], TT[u][:, h, :],
                                             vk[:, t, h, :, :].rearrange("p a c -> p (a c)"), start=True, stop=True)
                        up(s.uw_ready, last)
                        for h in range(H2):
                            last = pe.matmul(ps[32 * h:32 * h + 32, 4 * u + 1, 0:P], vk[:, t, h, 1, :], TT[u][:, h, :],
                                             start=True, stop=True)
                        up(s.wt_ready, last)
                    for u in range(2):
                        t = t0 + u
                        pe.wait_ge(s.uw_copied.sem, t + 1)
                        for h in range(H2):
                            pe.matmul(ps[:, 4 * u + 3, h * HD2:(h + 1) * HD2], att[u][:, h, :], uw[u][:, h, 0, :],
                                      start=True, stop=True)
                        for h in range(H2):
                            last = pe.matmul(ps[32 * h:32 * h + 32, 4 * u + 3, P:2 * P], uw[u][:, h, 1, :],
                                             att[u][:, h, :], start=True, stop=True)
                        up(s.out_ready, last)

            @block.scalar
            def _(act):
                for _ in norm.act(0, 0):
                    pass
                for j in range(3):
                    act.wait_ge(s.conv_ready.sem, j + 1)
                    if j:
                        act.wait_ge(s.silu_done.sem, j)
                    act.activation(sg[:], ps[:, 2 + j, :], ACT.Sigmoid).then_inc(s.sigmoid_done.sem, 1)
                act.wait_ge(s.gates_ready.sem, 1)
                act.activation(bg[:].rearrange("p t g h -> p (t g h)"), ps[:, 0, 0:8 * NT],
                               ACT.Sigmoid).then_inc(s.sigmoid_done.sem, 1)
                for j in range(2):
                    act.wait_ge(s.turned.sem, j + 1)
                    act.activation(tok[:, j, :], ps[:, 5 + j, :], ACT.Copy).then_inc(s.tok_copied.sem, 1)
                for j in range(2):
                    act.wait_ge(s.rot_done.sem, 2 * j + 2)
                    act.activation(half_b[:, j, :], half_a[:, j, :], ACT.Square).then_inc(s.rot_squared.sem, 1)
                act.wait_ge(s.gamma_ready.sem, 1)
                act.activation(st.g[:, :, bass.ds(b, 1), :].rearrange("p t a c -> p t (a c)"),
                               ps[:, 1, 0:4 * NT].rearrange("p (t c) -> p t c", t=NT), ACT.Copy).then_inc(s.act.sem, 1)
                act.wait_ge(s.f_turned.sem, 1)
                act.activation(qT[:], ps[:, 2, :], ACT.Copy).then_inc(s.q_t.sem, 1)
                act.wait_ge(s.f_turned.sem, 2)
                for h in range(H2):
                    rows = slice(32 * h, 32 * h + 32)
                    act.activation(kT[rows, h, :], ps[rows, 3, :], ACT.Copy).then_inc(s.k_t.sem, 1)
                act.wait_ge(s.f_turned.sem, 3)
                act.activation(kbT[:], ps[:, 4, :], ACT.Copy).then_inc(s.kb_t.sem, 1)
                for t0 in range(0, NT, 2):
                    for u in range(2):
                        act.wait_ge(s.nt_ready.sem, t0 + u + 1)
                        if t0:
                            act.wait_ge(s.level_masked.sem, 2 * LEVELS * (t0 // 2))
                        act.activation(NT_raw[u][:], bank(4 * u + 1), ACT.Copy).then_inc(s.nt_raw.sem, 1)
                    for i in range(LEVELS):
                        for u in range(2):
                            k = LEVELS * t0 + 2 * i + u
                            act.wait_ge(s.x_ready.sem, k + 1)
                            if k >= 2:
                                act.wait_ge(s.txt_ready.sem, k - 1)
                            act.activation(X[u][:], bank(4 * u), ACT.Copy).then_inc(s.x_copied.sem, 1)
                    for u in range(2):
                        t = t0 + u
                        act.wait_ge(s.uw_ready.sem, t + 1)
                        if t0:
                            act.wait_ge(s.out_ready.sem, t - 1)
                            act.wait_ge(s.u_kept.sem, t - 1)
                        act.activation(uw[u][:].rearrange("p h a c -> p (h a c)"), ps[:, 4 * u, 0:2 * P],
                                       ACT.Copy).then_inc(s.uw_copied.sem, 1)
                        act.wait_ge(s.wt_ready.sem, t + 1)
                        act.activation(mine(st.wT, t), ps[:, 4 * u + 1, 0:P], ACT.Copy).then_inc(s.out_copied.sem, 1)
                    for u in range(2):
                        t = t0 + u
                        act.wait_ge(s.out_ready.sem, t + 1)
                        act.activation(mine(st.o, t), ps[:, 4 * u + 3, 0:P], ACT.Copy).then_inc(s.out_copied.sem, 1)

            @block.gpsimd
            def _(pool):
                pool.wait_ge(s.sigmoid_done.sem, 4)
                for t in range(NT):
                    up(s.pool if t < NT - 1 else s.gamma_wide, pool.tensor_copy(
                        wide[:, t, :].rearrange("p (h c) -> p h c", h=H2),
                        bg[:, t, 1, :].unsqueeze(2).to_broadcast([P, H2, HD2])))
                for j in range(2):
                    pool.wait_ge(s.tok_copied.sem, j + 1)
                    for half in range(2):
                        up(s.half_done, pool.tensor_tensor(halves(half_b[:, j, :])[:, :, half, :],
                                                           even_odd(tok[:, j, :])[:, :, 1 - half, :],
                                                           halves(m.c_sin[:])[:, :, half, :], ALU.mult))
                    up(s.base_done, pool.tensor_tensor(act3[:, j, :].rearrange("p (t h c) -> p t h c", t=NT, h=H2),
                                                       tok[:, j, :].rearrange("p (t h c) -> p t h c", t=NT, h=H2),
                                                       m.c_share[:].rearrange("p (t h c) -> p t h c", t=NT, h=H2),
                                                       ALU.mult))
                pool.wait_ge(s.k_norm.sem, 1)
                pool.tensor_copy(st.k[:, :, bass.ds(b, 1), :].rearrange("p t a c -> p t (a c)"),
                                 ktok[:]).then_inc(s.k_kept.sem, 1)
                for t0 in range(0, NT, 2):
                    for i in range(LEVELS):
                        for u in range(2):
                            k = LEVELS * t0 + 2 * i + u
                            if i == 0:
                                pool.wait_ge(s.nt_raw.sem, t0 + u + 1)
                            if k >= 4:
                                pool.wait_ge(s.x_ready.sem, k - 3)
                            up(s.level_masked, pool.tensor_tensor(NTs[u][i % 2][:], NT_raw[u][:],
                                                                  heads(m.c_level[:, i, :]), ALU.mult))
                    for u in range(2):
                        t = t0 + u
                        pool.wait_ge(s.uw_copied.sem, t + 1)
                        up(s.u_kept, pool.tensor_copy(mine(st.u, t).rearrange("p (h c) -> p h c", h=H2),
                                                      uw[u][:, :, 0, :]))

            @block.vector
            def _(dve):
                for _ in norm.dve(0, 1, xn):
                    pass
                for j in range(3):
                    dve.wait_ge(s.sigmoid_done.sem, j + 1)
                    up(s.silu_done, dve.tensor_tensor(act3[:, j, :], ps[:, 2 + j, :], sg[:], ALU.mult))
                for j in range(2):
                    dve.wait_ge(s.tok_copied.sem, j + 1)
                    link(dve, s.dve, dve.tensor_tensor(halves(half_a[:, j, :]), even_odd(tok[:, j, :]),
                                                       halves(m.c_cos[:]), ALU.mult))
                    dve.wait_ge(s.half_done.sem, 2 * j + 2)
                    up(s.rot_done, dve.tensor_tensor(half_a[:, j, :], half_a[:, j, :], half_b[:, j, :], ALU.add))
                    dve.wait_ge(s.rot_done.sem, s.rot_done.n)
                    dve.wait_ge(s.base_done.sem, j + 1)
                    up(s.rot_done, dve.tensor_tensor(half_a[:, j, :], half_a[:, j, :], act3[:, j, :], ALU.add))
                dve.wait_ge(s.turned.sem, 3)
                dve.wait_ge(s.sigmoid_done.sem, 4)
                for t in range(NT):
                    up(s.v_weighed, dve.tensor_tensor(
                        vk[:, t, :, 0, :], ps[:, 7, t * P:(t + 1) * P].rearrange("p (h c) -> p h c", h=H2),
                        bg[:, t, 0, :].unsqueeze(2).to_broadcast([P, H2, HD2]), ALU.mult))
                for j in range(2):
                    dve.wait_ge(s.rot_squared.sem, j + 1)
                    link(dve, s.dve, dve.tensor_reduce(ssq[:, j, :], g16(half_b[:, j, :]), AX.X, ALU.add))
                flat = lambda a: a[:].rearrange("p j g -> p (j g)")
                link(dve, s.dve, dve.tensor_scalar(flat(ssq), flat(ssq), 1e-6, None, ALU.add))
                rsqrt_steps(dve, s.dve, flat(ssq), flat(rn), flat(rn_t))
                wide_rn = lambda j: rn[:, j, :].unsqueeze(2).to_broadcast([P, NT * H2, HD2])
                up(s.q_norm, dve.tensor_tensor(g16(half_a[:, 0, :]), g16(half_a[:, 0, :]), wide_rn(0), ALU.mult))
                up(s.k_norm, dve.tensor_tensor(g16(ktok[:].rearrange("p t c -> p (t c)")), g16(half_a[:, 1, :]),
                                               wide_rn(1), ALU.mult))
                dve.wait_ge(s.k_norm.sem, 1)
                for t in range(NT):
                    link(dve, s.dve, dve.tensor_tensor(
                        half_b[:, 0, t * P:(t + 1) * P].rearrange("p (h c) -> p h c", h=H2),
                        ktok[:, t, :].rearrange("p (h c) -> p h c", h=H2),
                        bg[:, t, 0, :].unsqueeze(2).to_broadcast([P, H2, HD2]), ALU.mult))
                    up(s.b_weighed, dve.tensor_copy(
                        vk[:, t, :, 1, :], half_b[:, 0, t * P:(t + 1) * P].rearrange("p (h c) -> p h c", h=H2)))
                for t0 in range(0, NT, 2):
                    for u in range(2):
                        t = t0 + u
                        dve.wait_ge(s.n_ready.sem, t + 1)
                        if t0:
                            dve.wait_ge(s.out_ready.sem, t - 1)
                        link(dve, s.dve, dve.tensor_tensor(T[u][:], bank(4 * u), heads(m.c_first[:, 0, :]), ALU.mult))
                        up(s.t_ready, dve.tensor_tensor(T[u][:], T[u][:], heads(m.ident[:]), ALU.add))
                        dve.wait_ge(s.nt_ready.sem, t + 1)
                        dve.wait_ge(s.nt_raw.sem, t + 1)
                        link(dve, s.dve, dve.tensor_tensor(TT[u][:], bank(4 * u + 1), heads(m.c_first[:, 1, :]),
                                                           ALU.mult))
                        up(s.tt_ready, dve.tensor_tensor(TT[u][:], TT[u][:], heads(m.ident[:]), ALU.add))
                        dve.wait_ge(s.at_ready.sem, t + 1)
                        up(s.att_ready, dve.tensor_tensor(att[u][:], bank(4 * u + 2), heads(m.c_causal[:]), ALU.mult))
                    for i in range(LEVELS):
                        for u in range(2):
                            k = LEVELS * t0 + 2 * i + u
                            dve.wait_ge(s.tx_ready.sem, k + 1)
                            dve.wait_ge(s.txt_ready.sem, k + 1)
                            dve.wait_ge(s.t_ready.sem, s.t_ready.n)
                            up(s.t_ready, dve.tensor_tensor(T[u][:], T[u][:], bank(4 * u + 1), ALU.add))
                            dve.wait_ge(s.tt_ready.sem, s.tt_ready.n)
                            up(s.tt_ready, dve.tensor_tensor(TT[u][:], TT[u][:], bank(4 * u + 2), ALU.add))
                    for u in range(2):
                        t = t0 + u
                        dve.wait_ge(s.out_ready.sem, t + 1)
                        dve.wait_ge(s.out_copied.sem, 4 * (t0 // 2) + 3 + u)
                        up(s.qp_done, dve.tensor_tensor(mine(st.qT, t), qT[:, t * P:(t + 1) * P],
                                                        ps[:, 4 * u + 3, P:2 * P], ALU.subtract))
        clear(nc, [s])


def delta_scan(m, ctx, st):
    nc, ps = m.nc, m.ps
    s = Signals(nc, ctx)
    (s.act, s.staged, s.staged_k, s.ws_ready, s.qs_ready, s.u_done, s.ku_ready, s.spread_dve, s.spread_act,
     s.stacked, s.o_done) = s.new(
        "act staged staged_k ws_ready qs_ready u_done ku_ready spread_dve spread_act stacked o_done")
    sb = lambda name, shape, dt=F32: ctx.enter_context(nc.sbuf_tensor(name, shape, dt))
    w_now, q_now, k_now, u_now = (sb("s_" + n, [P, B, P]) for n in ("w", "q", "k", "u"))
    stack, decayed = sb("s_stack", [P, B, HD2]), sb("s_decayed", [P, B, HD2])
    diag = sb("s_diag", [P, B, P])

    with nc.Block() as block:
        @block.vector
        def _(dve):
            up(s.dve, dve.memset(stack[:], 0.0))
            up(s.dve, dve.memset(diag[:], 0.0))
    clear(nc, [s])

    HB = B // 2
    with nc.Fori(0, NT, 1) as t:
        now = lambda a: a[:, bass.ds(t, 1), :, :].rearrange("p a b c -> p (a b) c")
        with nc.Block() as block:
            @block.tensor
            def _(pe):
                pe.wait_ge(s.staged.sem, 2)
                pe.wait_ge(s.staged_k.sem, 1)
                for r in range(4):
                    rows = slice(32 * r, 32 * r + 32)
                    if r:
                        pe.wait_ge(s.spread_dve.sem, 2 * r)
                        pe.wait_ge(s.spread_act.sem, 2 * r)
                    for b in range(B):
                        last = pe.matmul(ps[rows, b // HB, (b % HB) * P:(b % HB + 1) * P], w_now[:, b, rows], diag[:, b, :],
                                         start=True, stop=True)
                        if b == HB - 1 or b == B - 1:
                            up(s.ws_ready, last)
                    if r:
                        pe.wait_ge(s.o_done.sem, 2 * r)
                    for b in range(B):
                        last = pe.matmul(ps[rows, 2 + b // HB, (b % HB) * P:(b % HB + 1) * P], q_now[:, b, rows],
                                         diag[:, b, :], start=True, stop=True)
                    up(s.qs_ready, last)
                    if r:
                        pe.wait_ge(s.stacked.sem, r)
                    for b in range(B):
                        if b % HB == 0:
                            pe.wait_ge(s.u_done.sem, 2 * r + b // HB + 1)
                        for h in range(H2):
                            cols = slice(32 * h, 32 * h + 32)
                            last = pe.matmul(ps[cols, 4, b * HD2:(b + 1) * HD2], k_now[rows, b, cols],
                                             u_now[rows, b, cols], start=True, stop=True)
                    up(s.ku_ready, last)

            @block.scalar
            def _(act):
                act.activation(w_now[:], now(st.wT), ACT.Copy).then_inc(s.staged.sem, 1)
                act.activation(q_now[:], now(st.qT), ACT.Copy).then_inc(s.staged.sem, 1)
                for r in range(4):
                    act.wait_ge(s.stacked.sem, r + 1)
                    act.wait_ge(s.qs_ready.sem, r + 1)
                    for h in range(2):
                        blk = slice(32 * h, 32 * h + 32)
                        act.activation(diag[blk, :, blk], stack[blk, :, :], ACT.Copy).then_inc(s.spread_act.sem, 1)

            @block.vector
            def _(dve):
                up(s.staged_k, dve.tensor_copy(k_now[:], now(st.k)))
                for r in range(4):
                    rows = slice(32 * r, 32 * r + 32)
                    g = st.g[:, bass.ds(t, 1), :, r:r + 1].rearrange("p a b c -> p (a b c)")
                    if r:
                        dve.wait_ge(s.stacked.sem, r)
                        dve.wait_ge(s.spread_act.sem, 2 * r)
                    link(dve, s.dve, dve.tensor_tensor(decayed[:], stack[:], g.unsqueeze(2).to_broadcast([P, B, HD2]),
                                                       ALU.mult))
                    for half in range(2):
                        lo, hi = (0, HB) if half == 0 else (HB, B)
                        dve.wait_ge(s.ws_ready.sem, 2 * r + half + 1)
                        up(s.u_done, dve.tensor_tensor(
                            u_now[rows, lo:hi, :], now(st.u)[rows, lo:hi, :],
                            ps[rows, half, 0:(hi - lo) * P].rearrange("p (b c) -> p b c", c=P), ALU.subtract))
                    dve.wait_ge(s.ku_ready.sem, r + 1)
                    up(s.stacked, dve.tensor_tensor(stack[:], decayed[:],
                                                    ps[:, 4, 0:B * HD2].rearrange("p (b c) -> p b c", c=HD2), ALU.add))
                    dve.wait_ge(s.stacked.sem, r + 1)
                    for h in range(2, H2):
                        blk = slice(32 * h, 32 * h + 32)
                        up(s.spread_dve, dve.tensor_copy(diag[blk, :, blk], stack[blk, :, :]))
                    dve.wait_ge(s.qs_ready.sem, r + 1)
                    for half in range(2):
                        lo, hi = (0, HB) if half == 0 else (HB, B)
                        o = now(st.o)[rows, lo:hi, :]
                        up(s.o_done, dve.tensor_tensor(
                            o, o, ps[rows, 2 + half, 0:(hi - lo) * P].rearrange("p (b c) -> p b c", c=P), ALU.add))
        clear(nc, [s])


def delta_finish(m, ctx, st):
    nc = m.nc
    sb = lambda name, shape, dt=F32: ctx.enter_context(nc.sbuf_tensor(name, shape, dt))
    PAD = 2 ** (DILATIONS - 1)
    signals, buffers = [], []
    for u in range(2):
        s, own = Signals(nc, ctx, u), Store()
        (s.squared, s.o_norm, s.o_turned, s.o_t, s.core_ready, s.gate_ready, s.gate_done, s.frac,
         s.frac_squared, s.frac_var, s.frac_diag, s.frac_spread, s.y_ready) = s.new(
            "squared o_norm o_turned o_t core_ready gate_ready gate_done frac frac_squared frac_var "
            "frac_diag frac_spread y_ready")
        own.xp = sb(f"f_xp{u}", [P, PAD + S])
        own.xn = own.xp[:, PAD:PAD + S]
        own.osq, own.on, own.oT = sb(f"f_osq{u}", [P, NT, P]), sb(f"f_on{u}", [P, NT, P]), sb(f"f_oT{u}", [P, S])
        own.ssq, own.rn, own.rn_t = (sb(f"f_{n}{u}", [P, NT * H2]) for n in ("ssq", "rn", "rn_t"))
        own.frac, own.fsq, own.gate, own.y = (sb(f"f_{n}{u}", [P, S]) for n in ("frac", "fsq", "gate", "y"))
        signals.append(s)
        buffers.append(own)

    with nc.Block() as block:
        @block.vector
        def _(dve):
            for s, o in zip(signals, buffers):
                up(s.dve, dve.memset(o.xp[:], 0.0))
    clear(nc, signals)

    with nc.Fori(0, B // 2, 1) as b:
        x_pair = m.x[:, bass.ts(b, 2 * S)]
        o_pair = st.o[:, :, bass.ts(b, 2), :]
        g16 = lambda a: a.rearrange("p t (h c) -> p (t h) c", h=H2)
        with nc.Block() as block:
            @block.tensor
            def _(pe):
                def program(u):
                    s, o, ps, norm, k0 = signals[u], buffers[u], m.ps, Norm(m, signals[u], u), 4 * u
                    yield from norm.pe(0, x_pair[:, u * S:(u + 1) * S], k0, k0 + 1)
                    pe.wait_ge(s.o_norm.sem, 1)
                    for t in range(NT):
                        last = pe.transpose(ps[:, k0 + 3, t * P:(t + 1) * P], o.on[:, t, :], m.ident[:])
                    up(s.o_turned, last)
                    yield
                    pe.wait_ge(s.ln_done.sem, 1)
                    up(s.gate_ready, pe.matmul(ps[:, k0 + 2, :], m.c_gate_w[:], o.xn, start=True, stop=True))
                    yield
                    pe.wait_ge(s.o_t.sem, 1)
                    up(s.core_ready, pe.matmul(ps[:, k0 + 3, :], m.c_wo[:], o.oT[:], start=True, stop=True))
                    yield
                    pe.wait_ge(s.frac_squared.sem, 1)
                    for t in range(NT):
                        last = pe.matmul(ps[:, k0, t:t + 1], o.fsq[:, t * P:(t + 1) * P], m.mean_col[:, 0:1],
                                         start=True, stop=True)
                    up(s.frac_var, last)
                    yield
                    pe.wait_ge(s.frac_diag.sem, 1)
                    up(s.frac_spread, pe.matmul(ps[:, k0 + 1, :], m.ones[:], norm.diag[:], start=True, stop=True))
                    yield
                    pe.wait_ge(s.y_ready.sem, 1)
                    yield from norm.pe(1, o.y[:], k0, k0 + 1)

                in_turn(program(0), program(1))

            @block.scalar
            def _(act):
                def program(u):
                    s, o, ps, norm, k0 = signals[u], buffers[u], m.ps, Norm(m, signals[u], u), 4 * u
                    act.activation(o.osq[:], o_pair[:, :, u, :], ACT.Square).then_inc(s.squared.sem, 1)
                    yield
                    yield from norm.act(0, k0)
                    act.wait_ge(s.o_turned.sem, 1)
                    act.activation(o.oT[:], ps[:, k0 + 3, :], ACT.Copy).then_inc(s.o_t.sem, 1)
                    yield
                    act.wait_ge(s.gate_ready.sem, 1)
                    act.activation(o.gate[:], ps[:, k0 + 2, :], ACT.Sigmoid,
                                   bias=m.c_gate_b[:, 0:1]).then_inc(s.gate_done.sem, 1)
                    yield
                    act.wait_ge(s.frac.sem, DILATIONS + 1)
                    act.activation(o.fsq[:], o.frac[:], ACT.Square).then_inc(s.frac_squared.sem, 1)
                    yield
                    yield from norm.act(1, k0)

                in_turn(program(0), program(1))

            @block.vector
            def _(dve):
                def program(u):
                    s, o, ps, norm, k0 = signals[u], buffers[u], m.ps, Norm(m, signals[u], u), 4 * u
                    o_b = o_pair[:, :, u, :]
                    dve.wait_ge(s.squared.sem, 1)
                    link(dve, s.dve, dve.tensor_reduce(o.ssq[:], g16(o.osq[:]), AX.X, ALU.add))
                    link(dve, s.dve, dve.tensor_scalar(o.ssq[:], o.ssq[:], 1.0 / HD2, 1e-5, ALU.mult, ALU.add))
                    rsqrt_steps(dve, s.dve, o.ssq[:], o.rn[:], o.rn_t[:])
                    for t in range(NT):
                        last = dve.tensor_tensor(o.on[:, t, :].rearrange("p (h c) -> p h c", h=H2),
                                                 o_b[:, t, :].rearrange("p (h c) -> p h c", h=H2),
                                                 o.rn[:, t * H2:(t + 1) * H2].unsqueeze(2).to_broadcast([P, H2, HD2]),
                                                 ALU.mult)
                        if t < NT - 1:
                            up(s.dve, last)
                    up(s.o_norm, last)
                    yield
                    yield from norm.dve(0, k0 + 1, o.xn)
                    dve.wait_ge(s.ln_done.sem, 1)
                    up(s.frac, dve.tensor_scalar(o.frac[:], o.xn, m.c_frac_own[:, 0:1], None, ALU.mult))
                    for i in range(DILATIONS):
                        dve.wait_ge(s.frac.sem, i + 1)
                        up(s.frac, dve.scalar_tensor_tensor(out=o.frac[:], in0=o.xp[:, PAD - 2 ** i:PAD - 2 ** i + S],
                                                            scalar=m.c_frac_w[:, i, 0:1], in1=o.frac[:], op0=ALU.mult,
                                                            op1=ALU.add))
                    yield
                    dve.wait_ge(s.frac_var.sem, 1)
                    link(dve, s.dve, dve.tensor_scalar(norm.var[:, 0:NT], ps[:, k0, 0:NT], 1.0, 1e-5, ALU.mult,
                                                       ALU.add))
                    rsqrt_steps(dve, s.dve, norm.var[:, 0:NT], norm.rstd[:, 0:NT], norm.tmp[:, 0:NT])
                    for t in range(NT):
                        last = dve.tensor_scalar(norm.diag[:, t * P:(t + 1) * P], m.ident[:], norm.rstd[:, t:t + 1],
                                                 None, ALU.mult)
                        if t < NT - 1:
                            up(s.dve, last)
                    up(s.frac_diag, last)
                    yield
                    dve.wait_ge(s.dve.sem, s.dve.n)
                    dve.wait_ge(s.frac_spread.sem, 1)
                    link(dve, s.dve, dve.scalar_tensor_tensor(out=o.frac[:], in0=o.frac[:], scalar=m.c_mix_w[:, 0:1],
                                                              in1=ps[:, k0 + 1, :], op0=ALU.mult, op1=ALU.mult))
                    dve.wait_ge(s.gate_done.sem, 1)
                    link(dve, s.dve, dve.tensor_tensor(o.frac[:], o.frac[:], o.gate[:], ALU.mult))
                    dve.wait_ge(s.core_ready.sem, 1)
                    up(s.y_ready, dve.tensor_tensor(o.y[:], o.frac[:], ps[:, k0 + 3, :], ALU.add))
                    yield
                    yield from norm.dve(1, k0 + 1, o.y[:])
                    dve.wait_ge(s.ln_done.sem, 2)
                    x_b = x_pair[:, u * S:(u + 1) * S]
                    up(s.dve, dve.tensor_tensor(x_b, x_b, o.y[:], ALU.add))

                in_turn(program(0), program(1))
        clear(nc, signals)


def gated_block(m, ctx):
    nc = m.nc
    sb = lambda name, shape, dt=F32: ctx.enter_context(nc.sbuf_tensor(name, shape, dt))
    signals, buffers = [], []
    for u in range(2):
        s, own = Signals(nc, ctx, u), Store()
        (s.gu_ready, s.gate_done, s.silu_done, s.h_done, s.y_ready, s.y_copied) = s.new(
            "gu_ready gate_done silu_done h_done y_ready y_copied")
        own.xn, own.y = sb(f"d_xn{u}", [P, S]), sb(f"d_y{u}", [P, S])
        own.sg, own.gated = sb(f"d_sg{u}", [P, 2, S]), sb(f"d_gated{u}", [P, 2, S])
        own.h = sb(f"d_h{u}", [P, HCH3, S])
        signals.append(s)
        buffers.append(own)

    with nc.Fori(0, B // 2, 1) as b:
        x_pair = m.x[:, bass.ts(b, 2 * S)]
        with nc.Block() as block:
            @block.tensor
            def _(pe):
                def program(u):
                    s, o, ps, norm, k0 = signals[u], buffers[u], m.ps, Norm(m, signals[u], u), 4 * u
                    yield from norm.pe(0, x_pair[:, u * S:(u + 1) * S], k0, k0 + 1)
                    pe.wait_ge(s.ln_done.sem, 1)
                    for c in range(HCH3):
                        if c == 2:
                            pe.wait_ge(s.h_done.sem, 1)
                        hid, bank = slice(c * P, (c + 1) * P), k0 + 2 * (c % 2)
                        pe.matmul(ps[:, bank, :], m.d_gate[:, hid], o.xn[:], start=True, stop=True)
                        up(s.gu_ready, pe.matmul(ps[:, bank + 1, :], m.d_up[:, hid], o.xn[:], start=True, stop=True))
                        yield
                    for c in range(HCH3):
                        pe.wait_ge(s.h_done.sem, max(c + 1, 2))
                        last = pe.matmul(ps[:, k0 + 2, :], m.d_down[:, c, :], o.h[:, c, :],
                                         start=c == 0, stop=c == HCH3 - 1)
                        yield
                    up(s.y_ready, last)
                    yield
                    pe.wait_ge(s.y_copied.sem, 1)
                    yield from norm.pe(1, o.y[:], k0, k0 + 1)

                in_turn(program(0), program(1))

            @block.scalar
            def _(act):
                def program(u):
                    s, o, ps, norm, k0 = signals[u], buffers[u], m.ps, Norm(m, signals[u], u), 4 * u
                    yield from norm.act(0, k0)
                    for c in range(HCH3):
                        act.wait_ge(s.gu_ready.sem, c + 1)
                        if c == 2:
                            act.wait_ge(s.silu_done.sem, 1)
                        act.activation(o.sg[:, c % 2, :], ps[:, k0 + 2 * (c % 2), :],
                                       ACT.Sigmoid).then_inc(s.gate_done.sem, 1)
                        yield
                    act.wait_ge(s.y_ready.sem, 1)
                    act.activation(o.y[:], ps[:, k0 + 2, :], ACT.Copy).then_inc(s.y_copied.sem, 1)
                    yield
                    yield from norm.act(1, k0)

                in_turn(program(0), program(1))

            @block.vector
            def _(dve):
                def program(u):
                    s, o, ps, norm, k0 = signals[u], buffers[u], m.ps, Norm(m, signals[u], u), 4 * u
                    yield from norm.dve(0, k0 + 1, o.xn[:])
                    for c in range(HCH3):
                        bank = k0 + 2 * (c % 2)
                        dve.wait_ge(s.gate_done.sem, c + 1)
                        if c == 2:
                            dve.wait_ge(s.h_done.sem, 1)
                        up(s.silu_done, dve.tensor_tensor(o.gated[:, c % 2, :], o.sg[:, c % 2, :], ps[:, bank, :],
                                                          ALU.mult))
                        dve.wait_ge(s.silu_done.sem, c + 1)
                        up(s.h_done, dve.tensor_tensor(o.h[:, c, :], o.gated[:, c % 2, :], ps[:, bank + 1, :], ALU.mult))
                        yield
                    yield from norm.dve(1, k0 + 1, o.y[:])
                    dve.wait_ge(s.ln_done.sem, 2)
                    x_b = x_pair[:, u * S:(u + 1) * S]
                    up(s.dve, dve.tensor_tensor(x_b, x_b, o.y[:], ALU.add))

                in_turn(program(0), program(1))
        clear(nc, signals)


def build(nc, ins, out, blocks=range(4)):
    with ExitStack() as ctx:
        m = Store()
        m.nc = nc
        sb = lambda name, shape, dt=F32: ctx.enter_context(nc.sbuf_tensor(name, shape, dt))
        m.ps = ctx.enter_context(nc.psum_tensor("ps", [P, 8, S], F32))
        m.x = sb("x", [P, B * S])
        m.norm_buffers = []
        for u in range(2):
            n = Store()
            n.both = sb(f"ln_both{u}", [P, 2, S])
            n.lnc, n.lnsq, n.diag = n.both[:, 0, :], n.both[:, 1, :], sb(f"ln_diag{u}", [P, S])
            n.var, n.rstd, n.tmp = (sb(f"ln_{name}{u}", [P, NT]) for name in ("var", "rstd", "tmp"))
            m.norm_buffers.append(n)
        loaded = ctx.enter_context(nc.semaphore("loaded"))
        ready = ctx.enter_context(nc.semaphore("ready"))
        loaded_b = ctx.enter_context(nc.semaphore("loaded_b"))
        ready_b = ctx.enter_context(nc.semaphore("ready_b"))
        loaded_d = ctx.enter_context(nc.semaphore("loaded_d"))
        ready_d = ctx.enter_context(nc.semaphore("ready_d"))
        loaded_c = ctx.enter_context(nc.semaphore("loaded_c"))
        ready_c = ctx.enter_context(nc.semaphore("ready_c"))
        chain_c = ctx.enter_context(nc.semaphore("chain_c"))
        stored = ctx.enter_context(nc.semaphore("stored"))
        small = {"ident": [P, P], "centre": [P, P], "ones": [P, P], "mean_col": [P, 1], "ones_rows": [P, 1]}
        m.ident, m.centre, m.ones, m.mean_col, m.ones_rows = (sb(n, shape) for n, shape in small.items())
        m.ident_bf = sb("ident_bf", [P, P], BF16)
        loads = [(t[:], ins[n]) for n, t in zip(small, (m.ident, m.centre, m.ones, m.mean_col, m.ones_rows))] + [(m.ident_bf[:], ins["ident_bf"])]
        loads.append((m.x[:], ins["xT"]))

        with ExitStack() as own:
            sa = lambda name, shape, dt=F32: own.enter_context(nc.sbuf_tensor(name, shape, dt))

            def taken(n, shape):
                dst = sa("a_" + n, shape)
                loads.append((dst[:], ins["a_" + n]))
                return dst

            m.wq, m.wk, m.wv, m.wo = (taken(n, [P, P]) for n in ("wq", "wk", "wv", "wo"))
            m.bq, m.bk, m.bo = (taken(n, [P, 1]) for n in ("bq", "bk", "bo"))
            m.bv = sa("a_bv", [P, P])
            loads.append((m.bv[:], ins["a_bv"].partition_broadcast(P)))
            m.bq_scaled = sa("a_bq_scaled", [P, 1])
            m.sel = sa("a_sel", [P, 2, NPAIR, 3, P], BF16)
            loads.append((m.sel[:], ins["a_sel"]))
            with nc.Block() as block:
                @block.sync
                def _(sp):
                    for dst, src in loads:
                        sp.dma_start(dst, src).then_inc(loaded, 16)
                    sp.wait_ge(loaded, 16 * len(loads))

                @block.vector
                def _(dve):
                    dve.wait_ge(loaded, 16 * len(loads))
                    dve.tensor_scalar(m.bq_scaled[:], m.bq[:], HD0 ** -0.5, None, ALU.mult).then_inc(ready, 1)
            if 0 in blocks:
                attention_block(m, own)
        if 1 in blocks:
            with ExitStack() as own:
                sa = lambda name, shape, dt=F32: own.enter_context(nc.sbuf_tensor(name, shape, dt))
                todo = []

                def load(dst, src):
                    todo.append((dst[:], src))
                    return dst

                m.layer = []
                for l in range(L1):
                    w = Store()
                    w.wqkv = load(sa(f"b_wqkv{l}", [P, 3 * INNER]), ins["b_wqkv"][l])
                    w.wo = load(sa(f"b_wo{l}", [P, 4, P]), ins["b_wo"][l])
                    w.w1 = load(sa(f"b_w1{l}", [P, 2 * HID1]), ins["b_w1"][l])
                    w.w2 = load(sa(f"b_w2{l}", [P, 3, P]), ins["b_w2"][l])
                    w.b1 = load(sa(f"b_b1{l}", [P, 6]), ins["b_b1"][l])
                    w.b2, w.ln_g, w.ln_b = (load(sa(f"b_{n}{l}", [P, 1]), ins["b_" + n][l])
                                            for n in ("b2", "ln_g", "ln_b"))
                    w.tab_direct = load(sa(f"b_direct{l}", [P, NT, 2, HD1]), ins["b_direct"])
                    w.tab_swap = load(sa(f"b_swap{l}", [P, NT, 2, HD1]), ins["b_swap"])
                    w.qk_scale = sa(f"b_qk_scale{l}", [P, 2, HD1])
                    for j, n in enumerate(("b_q_scale", "b_k_scale")):
                        todo.append((w.qk_scale[:, j, :], ins[n][l].partition_broadcast(P)))
                    m.layer.append(w)
                m.mask = load(sa("b_mask", [P, 3 * WIN], BF16), ins["b_mask"])
                with nc.Block() as block:
                    @block.sync
                    def _(sp):
                        for dst, src in todo:
                            sp.dma_start(dst, src).then_inc(loaded_b, 16)
                        sp.wait_ge(loaded_b, 16 * len(todo))

                    @block.vector
                    def _(dve):
                        dve.wait_ge(loaded_b, 16 * len(todo))
                        for w in m.layer:
                            for j in range(2):
                                for t in range(NT):
                                    dve.tensor_tensor(w.tab_direct[:, t, j, :], w.tab_direct[:, t, j, :],
                                                      w.qk_scale[:, j, :], ALU.mult).then_inc(ready_b, 1)
                                    for half in range(2):
                                        o, i = slice(32 * half, 32 * half + 32), slice(32 - 32 * half, 64 - 32 * half)
                                        dve.tensor_tensor(w.tab_swap[:, t, j, o], w.tab_swap[:, t, j, o],
                                                          w.qk_scale[:, j, i], ALU.mult).then_inc(ready_b, 1)
                local_block(m, own)
        if 2 in blocks:
            with ExitStack() as own:
                sa = lambda name, shape, dt=F32: own.enter_context(nc.sbuf_tensor(name, shape, dt))
                todo = []

                def load(name, shape, src=None):
                    dst = sa(name, shape)
                    todo.append((dst[:], ins[name] if src is None else src))
                    return dst

                m.c_wbg, m.c_chunk_mean = load("c_wbg", [P, 8]), load("c_chunk_mean", [P, 4])
                m.c_level, m.c_first = load("c_level", [P, LEVELS, P]), load("c_first", [P, 2, P])
                m.c_causal, m.c_cos, m.c_sin = load("c_causal", [P, P]), load("c_cos", [P, S]), load("c_sin", [P, S])
                m.c_wo, m.c_o_norm = load("c_wo", [P, P]), load("c_o_norm", [P, 1])
                m.c_gate_b = load("c_gate_b", [P, 1], ins["c_gate_b"].partition_broadcast(P))
                m.c_gate_col, m.c_mix_w = load("c_gate_col", [P, 1]), load("c_mix_w", [P, 1])
                m.c_frac_w = load("c_frac_w", [P, DILATIONS, 2])
                m.c_rot = load("c_rot", [P, H2], ins["c_rot"].partition_broadcast(P))
                m.c_taps, m.c_share, m.c_gate_w = sa("c_taps", [P, 3, TAPS, P]), sa("c_share", [P, S]), sa("c_gate_w", [P, P])
                m.c_frac_own = sa("c_frac_own", [P, 1])
                st = Store()
                st.wT, st.qT, st.k, st.u, st.o = (sa("st_" + n, [P, NT, B, P]) for n in ("wT", "qT", "k", "u", "o"))
                st.g = sa("st_g", [P, NT, B, 4])
                with ExitStack() as once:
                    so = lambda name, shape: once.enter_context(nc.sbuf_tensor(name, shape, F32))
                    w3, conv = so("c_w3", [P, 3, P]), so("c_conv", [P, 3, TAPS, P])
                    mix, share = so("c_mix", [P, H2]), so("c_share4", [P, H2])
                    todo += [(w3[:], ins["c_w3"]), (conv[:], ins["c_conv"].partition_broadcast(P))]
                    with nc.Block() as block:
                        @block.sync
                        def _(sp):
                            for dst, src in todo:
                                sp.dma_start(dst, src).then_inc(loaded_c, 16)

                        @block.scalar
                        def _(act):
                            act.wait_ge(loaded_c, 16 * len(todo))
                            act.activation(mix[:], m.c_rot[:], ACT.Sigmoid).then_inc(ready_c, 1)

                        @block.vector
                        def _(dve):
                            c = Count(chain_c)
                            dve.wait_ge(loaded_c, 16 * len(todo))
                            for j in range(3):
                                for tap in range(TAPS):
                                    up(c, dve.tensor_tensor(m.c_taps[:, j, tap, :], w3[:, j, :], conv[:, j, tap, :],
                                                            ALU.mult))
                            up(c, dve.tensor_scalar(m.c_gate_w[:], m.ones[:], m.c_gate_col[:, 0:1], None, ALU.mult))
                            up(c, dve.tensor_scalar(m.c_wo[:], m.c_wo[:], m.c_o_norm[:, 0:1], None, ALU.mult))
                            link(dve, c, dve.tensor_reduce(m.c_frac_own[:], m.c_frac_w[:, :, 1], AX.X, ALU.add))
                            up(c, dve.tensor_scalar(m.c_frac_own[:], m.c_frac_own[:], 2.0, None, ALU.add))
                            dve.wait_ge(ready_c, 1)
                            link(dve, c, dve.tensor_scalar(share[:], mix[:], -1.0, 1.0, ALU.mult, ALU.add))
                            link(dve, c, dve.memset(m.c_share[:], 1.0))
                            wide = lambda a: a[:].unsqueeze(2).to_broadcast([P, H2, HD2])
                            for tab, by in ((m.c_cos, mix), (m.c_sin, mix), (m.c_share, share)):
                                for t in range(NT):
                                    part = tab[:, t * P:(t + 1) * P].rearrange("p (h c) -> p h c", h=H2)
                                    up(c, dve.tensor_tensor(part, part, wide(by), ALU.mult))
                with ExitStack() as own1:
                    delta_prepare(m, own1, st)
                with ExitStack() as own2:
                    delta_scan(m, own2, st)
                with ExitStack() as own3:
                    delta_finish(m, own3, st)
        if 3 in blocks:
            with ExitStack() as own:
                sa = lambda name, shape, dt=F32: own.enter_context(nc.sbuf_tensor(name, shape, dt))
                ints = [(sa("d_gate_i", [P, HID3], I32), ins["d_gate"]), (sa("d_up_i", [P, HID3], I32), ins["d_up"]),
                        (sa("d_down_i", [P, HCH3, P], I32), ins["d_down"])]
                m.d_gate, m.d_up = sa("d_gate", [P, HID3]), sa("d_up", [P, HID3])
                m.d_down = sa("d_down", [P, HCH3, P])
                with nc.Block() as block:
                    @block.sync
                    def _(sp):
                        for dst, src in ints:
                            sp.dma_start(dst[:], src).then_inc(loaded_d, 16)

                    @block.vector
                    def _(dve):
                        dve.wait_ge(loaded_d, 16 * len(ints))
                        for dst, (src, _) in zip((m.d_gate, m.d_up, m.d_down), ints):
                            dve.tensor_scalar(dst[:], src[:], DEQUANT, None, ALU.mult).then_inc(ready_d, 1)
                gated_block(m, own)
        with nc.Block() as block:
            @block.sync
            def _(sp):
                sp.dma_start(out, m.x[:]).then_inc(stored, 16)
                sp.wait_ge(stored, 16)


def rotary_tables():
    f32 = np.float32
    half = np.arange(0, HD1, 2, dtype=f32)
    t = np.arange(S, dtype=f32)
    freqs = t[:, None] * (f32(1.0) / f32(10000.0) ** (half / f32(HD1)))[None, :]
    base = (half + f32(0.4 * HD1)) / f32(1.4 * HD1)
    scale = base[None, :] ** ((t - S // 2) / f32(WIN // 2))[:, None]
    direct, swap = np.zeros((S, 2, HD1), f32), np.zeros((S, 2, HD1), f32)
    for j, sc in enumerate((scale, 1.0 / scale)):
        direct[:, j] = np.concatenate([np.cos(freqs) * sc] * 2, axis=1)
        swap[:, j] = np.concatenate([-np.sin(freqs) * sc, np.sin(freqs) * sc], axis=1)
    tiles = lambda a: a.reshape(NT, P, 2, HD1).transpose(1, 0, 2, 3)
    return tiles(direct), tiles(swap)


def layout(inputs):
    f = {n: np.asarray(a) for n, a in inputs.items()}
    col = lambda a: np.ascontiguousarray(a).reshape(-1, 1)
    eye = np.eye(P, dtype=np.float32)
    bf16 = mybir.dt.np(BF16)
    d = {"xT": f["L0_attn_hidden_states"].reshape(B * S, P).T,
         "ident": eye, "centre": eye - np.float32(1.0 / P), "ones": np.ones((P, P), np.float32),
         "mean_col": np.full((P, 1), 1.0 / P, np.float32), "ident_bf": eye.astype(bf16)}
    for n in ("q", "k", "v", "o"):
        d["a_w" + n] = f["L0_attn_W" + n].T
    for n in ("q", "k", "o"):
        d["a_b" + n] = col(f["L0_attn_b" + n])
    d["a_bv"] = f["L0_attn_bv"]
    sel = np.zeros((P, 2, NPAIR, 3, P), np.float32)
    for w, slots in enumerate((Q_PARTS, K_PARTS)):
        for p in range(NPAIR):
            for a in range(2):
                for slot, part in enumerate(slots):
                    for e in range(HD0):
                        sel[(2 * p + a) * HD0 + e, w, p, part, 64 * a + slot * HD0 + e] = 1.0
    d["a_sel"] = sel.astype(bf16)
    rows = np.zeros((P, 1), np.float32)
    for a in range(2):
        rows[64 * a + MAX_ROW:64 * a + MAX_ROW + 3] = 1.0
    d["ones_rows"] = rows
    d["b_wqkv"] = f["L0_ffn_wqkv"]
    d["b_wo"] = f["L0_ffn_wo"].reshape(L1, 4, P, P).transpose(0, 2, 1, 3)
    d["b_w1"] = f["L0_ffn_w1"]
    w2 = np.zeros((L1, P, 3, P), np.float32)
    b1 = np.zeros((L1, P, 6), np.float32)
    for c, (c0, rows) in enumerate(HCH):
        w2[:, 0:rows, c, :] = f["L0_ffn_w2"][:, c0:c0 + rows, :]
        b1[:, 0:rows, c] = f["L0_ffn_b1"][:, c0:c0 + rows]
        b1[:, 0:rows, 3 + c] = f["L0_ffn_b1"][:, HID1 + c0:HID1 + c0 + rows]
    d["b_w2"], d["b_b1"] = w2, b1
    for n in ("b2", "ln_g", "ln_b"):
        d["b_" + n] = f["L0_ffn_" + n].reshape(L1, P, 1)
    d["b_q_scale"], d["b_k_scale"] = f["L0_ffn_q_scale"], f["L0_ffn_k_scale"]
    direct, swap = rotary_tables()
    d["b_direct"], d["b_swap"] = direct, swap
    q, k = np.arange(P)[:, None], np.arange(3 * WIN)[None, :] - WIN
    d["b_mask"] = np.where((k <= q) & (k >= q - WIN), 0.0, MASKED).astype(bf16)
    d["c_wbg"] = np.concatenate([f["L1_attn_Wb"], f["L1_attn_Wgamma"]], axis=1)
    i, j = np.arange(P)[:, None], np.arange(P)[None, :]
    same = i // CHUNK == j // CHUNK
    d["c_chunk_mean"] = (i // CHUNK == np.arange(4)[None, :]) / np.float32(CHUNK)
    below = lambda half: (i // (2 * half) == j // (2 * half)) & (i % (2 * half) >= half) & (j % (2 * half) < half)
    d["c_level"] = np.stack([-below(2 ** (1 + n)).T.astype(np.float32) for n in range(LEVELS)], axis=1)
    d["c_first"] = np.stack([-below(1).astype(np.float32), -below(1).T.astype(np.float32)], axis=1)
    d["c_causal"] = (same & (i <= j)).astype(np.float32)
    inv = np.float32(1.0) / np.float32(10000.0) ** (np.arange(0, HD2, 2, dtype=np.float32) / np.float32(HD2))
    ang = np.arange(S, dtype=np.float32)[:, None] * inv[None, :]
    for n, halves in (("c_cos", (np.cos(ang), np.cos(ang))), ("c_sin", (-np.sin(ang), np.sin(ang)))):
        one = np.concatenate(halves, axis=1).reshape(NT, P, 1, HD2)
        d[n] = np.broadcast_to(one, (NT, P, H2, HD2)).transpose(1, 0, 2, 3).reshape(P, S)
    d["c_wo"], d["c_o_norm"] = f["L1_attn_Wo"], col(np.tile(f["L1_attn_o_norm_w"], H2))
    d["c_gate_b"], d["c_gate_col"] = f["L1_attn_frac_gate_b"], col(f["L1_attn_frac_gate_w"])
    d["c_frac_w"] = f["L1_attn_frac_conv_w"].transpose(1, 0, 2)
    d["c_mix_w"], d["c_rot"] = col(f["L1_attn_mixer_norm_w"]), f["L1_attn_rot_logit"]
    d["c_w3"] = np.stack([f["L1_attn_W" + n] for n in "qkv"], axis=1)
    d["c_conv"] = np.stack([f["L1_attn_conv_" + n].T for n in "qkv"], axis=0)
    for n in d:
        if n.startswith("c_"):
            d[n] = d[n].astype(np.float32)
    d["d_gate"], d["d_up"] = f["L1_ffn_w_gate"].T, f["L1_ffn_w_up"].T
    d["d_down"] = f["L1_ffn_w_down"].T.reshape(HCH3, P, P).transpose(1, 0, 2)
    return {n: np.ascontiguousarray(a) for n, a in d.items()}


def kernel(**inputs):
    import concourse.bacc as bacc
    from concourse.bass_utils import run_bass_kernel_spmd

    arrays = layout(inputs)
    nc = bacc.Bacc("TRN2", target_bir_lowering=False, num_devices=1)
    ins = {n: nc.dram_tensor("in_" + n, a.shape, mybir.dt.from_np(a.dtype), kind="ExternalInput").ap()
           for n, a in arrays.items()}
    out = nc.dram_tensor("out_xT", (P, B * S), F32, kind="ExternalOutput").ap()
    build(nc, ins, out)
    r = run_bass_kernel_spmd(nc, [{"in_" + n: a for n, a in arrays.items()}], core_ids=[0])
    xT = np.asarray(r.results[0]["out_xT"])
    return np.ascontiguousarray(xT.T).reshape(B, S, P)
```

```python
from contextlib import ExitStack

import numpy as np
import concourse.bass as bass
from concourse import mybir

ALU = mybir.AluOpType
ACT = mybir.ActivationFunctionType
AX = mybir.AxisListType
F32 = mybir.dt.float32
BF16 = mybir.dt.bfloat16
I32 = mybir.dt.int32

P = 128
B, S = 8, 512
NT = S // P
LN_EPS = 1e-5

H0, HD0 = 16, 8
NPAIR = H0 // 2
NGROUP = H0 // 4
Q_PARTS = (0, 0, 1, 1, 0, 2)
K_PARTS = (0, 1, 0, 1, 2, 0)
MAX_ROW = len(Q_PARTS) * HD0

L1, H1, HD1, WIN = 2, 8, 64, 64
INNER = H1 * HD1
HID1 = int(P * 4 * 2 / 3)
HCH = [(c, min(P, HID1 - c)) for c in range(0, HID1, P)]
MASKED = -1e30

H2, HD2, TAPS, CHUNK, DILATIONS = 4, 32, 4, 32, 4
LEVELS = 4

HID3 = 384
HCH3 = HID3 // P
DEQUANT = float(np.float32(1.0 / 127.0))

MAGIC = 0x5F3759DF


class Count:

    def __init__(self, sem):
        self.sem, self.n = sem, 0


def up(count, ins):
    ins.then_inc(count.sem, 1)
    count.n += 1
    return count.n


def link(eng, count, ins):
    up(count, ins)
    eng.wait_ge(count.sem, count.n)


class Signals:

    def __init__(self, nc, ctx, batch=0):
        self.nc, self.ctx, self.batch, self.every = nc, ctx, batch, []
        (self.ln_centred, self.ln_copied, self.ln_squared, self.ln_var, self.ln_diag, self.ln_spread, self.ln_done,
         self.dve) = self.new("ln_centred ln_copied ln_squared ln_var ln_diag ln_spread ln_done dve")

    def new(self, names):
        counts = [Count(self.ctx.enter_context(self.nc.semaphore(f"{n}_{self.batch}"))) for n in names.split()]
        self.every += counts
        return counts


def clear(nc, signals):
    every = [count for s in signals for count in s.every]
    with nc.Block() as block:
        @block.gpsimd
        def _(pool):
            for count in every[0::5]:
                pool.sem_clear(count.sem)

        @block.vector
        def _(dve):
            for count in every[1::5]:
                dve.sem_clear(count.sem)

        @block.scalar
        def _(act):
            for count in every[2::5]:
                act.sem_clear(count.sem)

        @block.sync
        def _(sp):
            for count in every[3::5]:
                sp.sem_clear(count.sem)

        @block.tensor
        def _(pe):
            for count in every[4::5]:
                pe.sem_clear(count.sem)

    for s in signals:
        for count in s.every:
            count.n = 0


def in_turn(*programs):
    programs = list(programs)
    while programs:
        programs = [p for p in programs if next(p, "done") != "done"]


class Store:
    pass


def rsqrt_steps(dve, c, v, y, t):
    link(dve, c, dve.tensor_scalar(t.bitcast(I32), v.bitcast(I32), 1, None, ALU.arith_shift_right))
    link(dve, c, dve.tensor_scalar(y.bitcast(I32), t.bitcast(I32), -1.0, float(MAGIC), ALU.mult, ALU.add))
    for _ in range(3):
        link(dve, c, dve.tensor_tensor(t, y, y, ALU.mult))
        link(dve, c, dve.scalar_tensor_tensor(out=t, in0=t, scalar=-0.5, in1=v, op0=ALU.mult, op1=ALU.mult))
        link(dve, c, dve.scalar_tensor_tensor(out=y, in0=t, scalar=1.5, in1=y, op0=ALU.add, op1=ALU.mult))


def rsqrt_of_both(dve, signals, u, v, y, t):
    if u == 1:
        for s in signals:
            dve.wait_ge(s.dve.sem, s.dve.n)
        rsqrt_steps(dve, signals[1].dve, v, y, t)


class Norm:

    def __init__(self, m, signals, u):
        self.m, self.signals, self.s, self.u, b = m, signals, signals[u], u, m.norm_buffers[u]
        self.lnc, self.lnsq, self.diag = b.lnc, b.lnsq, b.diag
        self.var, self.rstd = (a[:, u * NT:(u + 1) * NT] for a in (m.var, m.rstd))

    def inverse_root(self, eps, src):
        m, s, dve = self.m, self.s, self.m.nc.vector
        up(s.dve, dve.tensor_scalar(self.var, src, 1.0, eps, ALU.mult, ALU.add))
        rsqrt_of_both(dve, self.signals, self.u, m.var[:], m.rstd[:], m.tmp[:])
        yield
        for t in range(NT):
            last = dve.tensor_scalar(self.diag[:, t * P:(t + 1) * P], m.ident[:], self.rstd[:, t:t + 1], None,
                                     ALU.mult)
            if t < NT - 1:
                up(s.dve, last)
        return last

    def pe(self, n, src, bank, other):
        m, s, pe, ps = self.m, self.s, self.m.nc.tensor, self.m.ps
        up(s.ln_centred, pe.matmul(ps[:, bank, :], m.centre[:], src, start=True, stop=True))
        yield
        pe.wait_ge(s.ln_squared.sem, n + 1)
        for t in range(NT):
            last = pe.matmul(ps[:, other, t:t + 1], self.lnsq[:, t * P:(t + 1) * P], m.mean_col[:, 0:1],
                             start=True, stop=True)
        up(s.ln_var, last)
        yield
        pe.wait_ge(s.ln_diag.sem, n + 1)
        up(s.ln_spread, pe.matmul(ps[:, other, :], m.ones[:], self.diag[:], start=True, stop=True))
        yield

    def act(self, n, bank):
        m, s, act, ps = self.m, self.s, self.m.nc.scalar, self.m.ps
        act.wait_ge(s.ln_centred.sem, n + 1)
        if n:
            act.wait_ge(s.ln_done.sem, n)
        act.activation(self.lnc[:], ps[:, bank, :], ACT.Copy).then_inc(s.ln_copied.sem, 1)
        act.activation(self.lnsq[:], ps[:, bank, :], ACT.Square).then_inc(s.ln_squared.sem, 1)
        yield

    def dve(self, n, other, out, eps=LN_EPS):
        m, s, dve, ps = self.m, self.s, self.m.nc.vector, self.m.ps
        dve.wait_ge(s.ln_var.sem, n + 1)
        up(s.ln_diag, (yield from self.inverse_root(eps, ps[:, other, 0:NT])))
        yield
        dve.wait_ge(s.dve.sem, s.dve.n)
        dve.wait_ge(s.ln_spread.sem, n + 1)
        dve.wait_ge(s.ln_copied.sem, n + 1)
        up(s.ln_done, dve.tensor_tensor(out, self.lnc[:], ps[:, other, :], ALU.mult))
        yield


def attention_block(m, ctx):
    nc = m.nc
    sb = lambda name, shape, dt=F32: ctx.enter_context(nc.sbuf_tensor(name, shape, dt))
    signals, buffers = [], []
    for u in range(2):
        s, own = Signals(nc, ctx, u), Store()
        (s.qk_proj, s.v_proj, s.qk_f32, s.v_done, s.parts, s.placed, s.q_stack, s.k_stack, s.s_ready, s.maxed,
         s.m_parts, s.m_turned, s.q_full, s.st_ready, s.exp_done, s.av_done, s.o_copied, s.o_turned, s.att_done,
         s.a_turned, s.a_copied, s.y_ready, s.y_copied) = s.new(
            "qk_proj v_proj qk_f32 v_done parts placed q_stack k_stack s_ready maxed m_parts m_turned q_full "
            "st_ready exp_done av_done o_copied o_turned att_done a_turned a_copied y_ready y_copied")
        own.xn, own.rest = (sb(f"a_{n}{u}", [P, S]) for n in ("xn", "rest"))
        own.qk = sb(f"a_qk{u}", [P, 2, S])
        own.parts = sb(f"a_parts{u}", [P, 2, 3, S], BF16)
        own.kst, own.qst = sb(f"a_kst{u}", [P, H0, S], BF16), sb(f"a_qst{u}", [P, NPAIR, S], BF16)
        own.va = sb(f"a_va{u}", [P, NT, H0, 32])
        own.negm, own.mrest = sb(f"a_negm{u}", [P, H0, NT]), sb(f"a_mrest{u}", [P, 2, NT, 2])
        own.mx = sb(f"a_mx{u}", [P, 2, NT, P], BF16)
        own.mxv = own.mx[:].rearrange("p r t (a c) -> p r t a c", a=2)
        own.prob = sb(f"a_prob{u}", [P, 4, 2, S])
        own.aT, own.y = own.qk[:, 0, :], own.qk[:, 1, :]
        own.osb, own.att = own.xn, own.rest[:].rearrange("p (t c) -> p t c", t=NT)
        own.rec = sb(f"a_rec{u}", [P, NT, 4])
        signals.append(s)
        buffers.append(own)

    FIRST = 4
    SCORES = 4 * NT

    def turned_bank(g, k2):
        return 1 if g == NGROUP - 1 and k2 else 2

    def scored_first(n):
        return max(0, (n + 1 - FIRST) * SCORES // (2 * NPAIR - FIRST))

    def scored(k):
        return min(SCORES * (NGROUP - 1), 2 * k + 4 if k else 0)

    with nc.Block() as block:
        m.start(block)

        @block.vector
        def _(dve):
            for s, o in zip(signals, buffers):
                link(dve, s.dve, dve.memset(o.va[:], 0.0))
                up(s.dve, dve.memset(o.va[:, :, :, HD0:HD0 + 1], 1.0))
                up(s.dve, dve.memset(o.mx[:], 0.0))
            dve.wait_ge(m.loaded, 16 * m.loads)
            link(dve, signals[0].dve, dve.tensor_scalar(m.bq_scaled[:], m.bq[:], HD0 ** -0.5, None, ALU.mult))

        @block.gpsimd
        def _(pool):
            for s, o in zip(signals, buffers):
                for a in range(2):
                    up(s.q_stack, pool.memset(o.kst[64 - 64 * a:P - 64 * a, a::2, :], 0.0))
    clear(nc, signals)

    with nc.Fori(0, B // 2, 1) as b:
        x_pair = m.x[:, bass.ts(b, 2 * S)]
        with nc.Block() as block:
            @block.tensor
            def _(pe):
                def program(u):
                    s, o, ps, norm, k0 = signals[u], buffers[u], m.ps, Norm(m, signals, u), 4 * u
                    yield from norm.pe(0, x_pair[:, u * S:(u + 1) * S], k0, k0 + 1)
                    pe.wait_ge(s.ln_done.sem, 1)
                    up(s.qk_proj, pe.matmul(ps[:, k0 + 2, :], m.wq[:], o.xn[:], start=True, stop=True))
                    up(s.qk_proj, pe.matmul(ps[:, k0 + 3, :], m.wk[:], o.xn[:], start=True, stop=True))
                    yield
                    for t in range(NT):
                        last = pe.matmul(ps[:, k0, t * P:(t + 1) * P], o.xn[:, t * P:(t + 1) * P], m.wv[:],
                                         start=True, stop=True)
                    up(s.v_proj, last)
                    yield
                    def place(n):
                        p, which = n // 2, n % 2
                        pe.wait_ge(s.parts.sem, which + 1)
                        if p:
                            pe.wait_ge((s.k_stack if which else s.q_stack).sem, p * (1 + which))
                        for part in range(3):
                            last = pe.matmul(ps[:, k0 + 2 + which, :], m.sel[:, which, p, part, :],
                                             o.parts[:, which, part, :], start=part == 0, stop=part == 2)
                        up(s.placed, last)
                        yield

                    def scores(g, i):
                        h, qt = 4 * g + i // 4, i % 4
                        n = 16 * g + i
                        pe.wait_ge(s.q_stack.sem, h // 2 + 1)
                        pe.wait_ge(s.k_stack.sem, h + 1)
                        if n >= 2:
                            pe.wait_ge(s.maxed.sem, n - 1)
                        elif n == 0:
                            pe.wait_ge(s.v_done.sem, 1)
                        if i == 0 and g:
                            pe.wait_ge(s.q_full.sem, 2 * g)
                        if i == 0 and g >= 3:
                            pe.wait_ge(s.att_done.sem, g - 2)
                        up(s.s_ready, pe.matmul(ps[:, k0 + n % 2, :], o.qst[:, h // 2, qt * P:(qt + 1) * P], o.kst[:, h, :],
                                                start=True, stop=True))
                        yield

                    def turn_max(g):
                        pe.wait_ge(s.m_parts.sem, g + 1)
                        for r in range(2):
                            for t in range(NT):
                                last = pe.matmul(ps[:, k0 + r, t * P:(t + 1) * P], o.mx[:, r, t, :], m.ident_bf[:],
                                                 start=True, stop=True)
                            up(s.m_turned, last)
                            yield

                    def scores_t(g, i, k2):
                        n = 2 * (8 * g + i) + k2
                        kp, h = i // 4, 4 * g + i % 4
                        pe.wait_ge(s.q_full.sem, h // 2 + 1)
                        if n == 0:
                            pe.wait_ge(s.q_stack.sem, NPAIR)
                            pe.wait_ge(s.k_stack.sem, H0)
                        else:
                            pe.wait_ge(s.exp_done.sem, n - (n > 16 * (NGROUP - 1)))
                        kt = 2 * kp + k2
                        up(s.st_ready, pe.matmul(ps[:, k0 + turned_bank(g, k2), :], o.kst[:, h, kt * P:(kt + 1) * P],
                                                 o.qst[:, h // 2, :], start=True, stop=True))
                        yield

                    def weigh(c):
                        g, kp = c // 2, c % 2
                        pe.wait_ge(s.exp_done.sem, 8 * (c + 1))
                        if kp == 0 and g:
                            pe.wait_ge(s.o_copied.sem, g)
                        for k2 in range(2):
                            for j in range(4):
                                last = pe.matmul(ps[32 * j:32 * j + 32, k0 + 3, :], o.va[:, 2 * kp + k2, 4 * g + j, :],
                                                 o.prob[:, j, k2, :], start=kp == 0 and k2 == 0,
                                                 stop=kp == 1 and k2 == 1)
                            if k2 == 1:
                                up(s.av_done, last)
                            yield

                    def products(g, i):
                        yield from scores_t(g, i, 0)
                        if i % 4 == 0 and 2 * g + i // 4 > 0:
                            yield from weigh(2 * g + i // 4 - 1)
                        yield from scores_t(g, i, 1)

                    def turn_out(g):
                        pe.wait_ge(s.o_copied.sem, g + 1)
                        pe.wait_ge(s.maxed.sem, SCORES * min(g + 3, NGROUP))
                        pe.wait_ge(s.q_full.sem, 2 * min(g + 3, NGROUP))
                        if g:
                            pe.wait_ge(s.att_done.sem, g)
                        for t in range(NT):
                            last = pe.transpose(ps[:, k0, t * P:(t + 1) * P], o.osb[:, t * P:(t + 1) * P], m.ident[:])
                        up(s.o_turned, last)
                        yield

                    for n in range(2 * NPAIR):
                        yield from place(n)
                        for i in range(scored_first(n - 1), scored_first(n)):
                            yield from scores(0, i)
                    yield from turn_max(0)
                    for g in range(NGROUP):
                        for i in range(8):
                            others = products(g, i)
                            before = scored(8 * g + i)
                            if before and before % SCORES == 0 and before > scored(8 * g + i - 1):
                                yield from others
                                yield from turn_max(before // SCORES)
                            if i == 6 and g:
                                yield from others
                                yield from turn_out(g - 1)
                            for n in range(before, scored(8 * g + i + 1)):
                                next(others, None)
                                yield
                                yield from scores(1 + n // SCORES, n % SCORES)
                            yield from others
                    yield from weigh(2 * NGROUP - 1)
                    yield from turn_out(NGROUP - 1)
                    pe.wait_ge(s.att_done.sem, NGROUP)
                    for t in range(NT):
                        last = pe.transpose(ps[:, k0, t * P:(t + 1) * P], o.att[:, t, :], m.ident[:])
                    up(s.a_turned, last)
                    yield
                    pe.wait_ge(s.a_copied.sem, 1)
                    up(s.y_ready, pe.matmul(ps[:, k0 + 1, :], m.wo[:], o.aT[:], start=True, stop=True))
                    yield
                    pe.wait_ge(s.y_copied.sem, 1)
                    yield from norm.pe(1, o.y[:], k0 + 2, k0 + 3)

                in_turn(program(0), program(1))

            @block.scalar
            def _(act):
                def program(u):
                    s, o, ps, norm, k0 = signals[u], buffers[u], m.ps, Norm(m, signals, u), 4 * u
                    yield from norm.act(0, k0)
                    act.wait_ge(s.qk_proj.sem, 1)
                    act.activation(o.qk[:, 0, :], ps[:, k0 + 2, :], ACT.Identity, bias=m.bq_scaled[:, 0:1],
                                   scale=HD0 ** -0.5).then_inc(s.qk_f32.sem, 1)
                    act.wait_ge(s.qk_proj.sem, 2)
                    act.activation(o.qk[:, 1, :], ps[:, k0 + 3, :], ACT.Identity,
                                   bias=m.bk[:, 0:1]).then_inc(s.qk_f32.sem, 1)
                    yield
                    for p in range(NPAIR):
                        act.wait_ge(s.placed.sem, 2 * p + 1)
                        act.activation(o.qst[:, p, :], ps[:, k0 + 2, :], ACT.Copy).then_inc(s.q_stack.sem, 1)
                        yield
                        act.wait_ge(s.placed.sem, 2 * p + 2)
                        for a in range(2):
                            rows = slice(64 * a, 64 * a + 64)
                            act.activation(o.kst[rows, 2 * p + a, :], ps[rows, k0 + 3, :], ACT.Identity,
                                           bias=m.ones_rows[rows, 0:1]).then_inc(s.k_stack.sem, 1)
                        yield
                    for c in range(2 * NGROUP):
                        for j in range(4):
                            if j == 0 and c:
                                act.wait_ge(s.av_done.sem, c)
                            for k2 in range(2):
                                act.wait_ge(s.st_ready.sem, 2 * (4 * c + j) + k2 + 1)
                                act.activation(o.prob[:, j, k2, :], ps[:, k0 + turned_bank(c // 2, k2), :],
                                               ACT.Exp).then_inc(s.exp_done.sem, 1)
                                yield
                        if c % 2 == 0 and c:
                            if c > 2:
                                act.wait_ge(s.o_turned.sem, c // 2 - 1)
                            act.activation(o.osb[:], ps[:, k0 + 3, :], ACT.Copy).then_inc(s.o_copied.sem, 1)
                            yield
                    act.wait_ge(s.av_done.sem, 2 * NGROUP)
                    act.wait_ge(s.o_turned.sem, NGROUP - 1)
                    act.activation(o.osb[:], ps[:, k0 + 3, :], ACT.Copy).then_inc(s.o_copied.sem, 1)
                    yield
                    act.wait_ge(s.a_turned.sem, 1)
                    act.activation(o.aT[:], ps[:, k0, :], ACT.Copy).then_inc(s.a_copied.sem, 1)
                    yield
                    act.wait_ge(s.y_ready.sem, 1)
                    act.activation(o.y[:], ps[:, k0 + 1, :], ACT.Identity, bias=m.bo[:, 0:1]).then_inc(s.y_copied.sem, 1)
                    yield
                    yield from norm.act(1, k0 + 2)

                in_turn(program(0), program(1))

            @block.vector
            def _(dve):
                def program(u):
                    s, o, ps, norm, k0 = signals[u], buffers[u], m.ps, Norm(m, signals, u), 4 * u
                    yield from norm.dve(0, k0 + 1, o.xn[:])
                    dve.wait_ge(s.v_proj.sem, 1)
                    for t in range(NT):
                        last = dve.tensor_tensor(o.va[:, t, :, 0:HD0],
                                                 ps[:, k0, t * P:(t + 1) * P].rearrange("p (h d) -> p h d", h=H0),
                                                 m.bv[:].rearrange("p (h d) -> p h d", h=H0), ALU.add)
                        if t < NT - 1:
                            up(s.dve, last)
                    up(s.v_done, last)
                    yield
                    for w in range(2):
                        dve.wait_ge(s.qk_f32.sem, w + 1)
                        if w:
                            dve.wait_ge(s.parts.sem, 1)
                        link(dve, s.dve, dve.tensor_copy(o.parts[:, w, 0, :], o.qk[:, w, :]))
                        link(dve, s.dve, dve.tensor_tensor(o.rest[:], o.qk[:, w, :], o.parts[:, w, 0, :], ALU.subtract))
                        link(dve, s.dve, dve.tensor_copy(o.parts[:, w, 1, :], o.rest[:]))
                        up(s.parts, dve.tensor_tensor(o.parts[:, w, 2, :], o.rest[:], o.parts[:, w, 1, :], ALU.subtract))
                        yield
                    def maxima(g, i):
                        n = 16 * g + i
                        dve.wait_ge(s.s_ready.sem, n + 1)
                        up(s.maxed, dve.tensor_reduce(o.negm[:, 4 * g + i // 4, i % 4:i % 4 + 1], ps[:, k0 + n % 2, :], AX.X,
                                                      ALU.max, negate=True))
                        yield

                    def max_parts(g):
                        dve.wait_ge(s.maxed.sem, 16 * (g + 1))
                        if g:
                            dve.wait_ge(s.m_turned.sem, 2 * g)
                        neg = o.negm[:, 4 * g:4 * g + 4, :].rearrange("p (r a) t -> p r t a", r=2)
                        row = lambda i: o.mxv[:, :, :, :, MAX_ROW + i]
                        link(dve, s.dve, dve.tensor_copy(row(0), neg))
                        link(dve, s.dve, dve.tensor_tensor(o.mrest[:], neg, row(0), ALU.subtract))
                        link(dve, s.dve, dve.tensor_copy(row(1), o.mrest[:]))
                        up(s.m_parts, dve.tensor_tensor(row(2), o.mrest[:], row(1), ALU.subtract))
                        yield

                    def full_q(g):
                        for r in range(2):
                            p = 2 * g + r
                            dve.wait_ge(s.m_turned.sem, p + 1)
                            up(s.q_full, dve.tensor_tensor(o.qst[:, p, :], o.qst[:, p, :], ps[:, k0 + r, :], ALU.add))
                            yield

                    def finish(g):
                        dve.wait_ge(s.o_turned.sem, g + 1)
                        out = ps[:, k0, :].rearrange("p (t j c) -> p t j c", t=NT, j=4)
                        link(dve, s.dve, dve.reciprocal(o.rec[:], out[:, :, :, HD0]))
                        up(s.att_done, dve.tensor_tensor(
                            o.att[:, :, 32 * g:32 * g + 32].rearrange("p t (j d) -> p t j d", j=4),
                            out[:, :, :, 0:HD0], o.rec[:].unsqueeze(3).to_broadcast([P, NT, 4, HD0]), ALU.mult))
                        yield

                    for n in range(2 * NPAIR):
                        for i in range(scored_first(n - 1), scored_first(n)):
                            yield from maxima(0, i)
                    yield from max_parts(0)
                    yield from full_q(0)
                    for g in range(NGROUP):
                        for i in range(8):
                            before, after = scored(8 * g + i), scored(8 * g + i + 1)
                            if before and before % SCORES == 0 and before > scored(8 * g + i - 1):
                                yield from full_q(before // SCORES)
                            if i == 6 and g:
                                yield from finish(g - 1)
                            for n in range(before, after):
                                yield from maxima(1 + n // SCORES, n % SCORES)
                            if after % SCORES == 0 and after > before:
                                yield from max_parts(after // SCORES)
                    yield from finish(NGROUP - 1)
                    yield from norm.dve(1, k0 + 3, o.y[:])
                    dve.wait_ge(s.ln_done.sem, 2)
                    x_b = x_pair[:, u * S:(u + 1) * S]
                    up(s.dve, dve.tensor_tensor(x_b, x_b, o.y[:], ALU.add))

                in_turn(program(0), program(1))
        clear(nc, signals)


def local_block(m, ctx):
    nc = m.nc
    sb = lambda name, shape, dt=F32: ctx.enter_context(nc.sbuf_tensor(name, shape, dt))
    ssq, rn, rn_t = (sb(f"b_{n}", [P, 2, NT, 2, H1]) for n in ("ssq", "rn", "rn_t"))
    signals, buffers = [], []
    for u in range(2):
        s, own = Signals(nc, ctx, u), Store()
        (s.act, s.shifted, s.qkv_ready, s.q_raw, s.k_raw, s.v_raw, s.squared, s.summed, s.factors, s.k_scaled,
         s.swapped, s.rotated, s.q_turned, s.k_turned, s.q_t, s.k_t, s.scores_ready, s.neg_max, s.exp_done,
         s.own_turned, s.past_turned, s.own_kept, s.past_kept, s.p_scaled, s.o_ready, s.o_t, s.res_ready,
         s.stream, s.ga_ready, s.gelu_done, s.h_done, s.down_ready) = s.new(
            "act shifted qkv_ready q_raw k_raw v_raw squared summed factors k_scaled swapped rotated q_turned k_turned "
            "q_t k_t scores_ready neg_max exp_done own_turned past_turned own_kept past_kept p_scaled "
            "o_ready o_t res_ready stream ga_ready gelu_done h_done down_ready")
        signals.append(s)
        own.y, own.hT, own.hn = (sb(f"b_{n}{u}", [P, S]) for n in ("y", "hT", "hn"))
        own.raw, own.v = sb(f"b_raw{u}", [P, NT, 2, INNER]), sb(f"b_v{u}", [P, NT, INNER])
        own.ssq, own.rn = (a[:, u, :, :, :] for a in (ssq, rn))
        own.rq = sb(f"b_rq{u}", [P, NT, H1])
        own.rot = sb(f"b_rot{u}", [P, 2, INNER])
        own.qT, own.kT = sb(f"b_qT{u}", [P, 4, P]), sb(f"b_kT{u}", [P, H1, S])
        own.prob, own.pT = sb(f"b_prob{u}", [P, H1, 2 * P]), sb(f"b_pT{u}", [P, 2, 8, P])
        own.nmax, own.rden = sb(f"b_nmax{u}", [P, H1]), sb(f"b_rden{u}", [P, H1])
        own.nbias, own.den = sb(f"b_nbias{u}", [P, 2, H1]), sb(f"b_den{u}", [P, 2, H1])
        n = m.norm_buffers[u]
        own.swap = n.both
        own.sq = own.pT[:].rearrange("p f c k -> p (f c k)")[:, 0:2 * INNER].rearrange("p (j c) -> p j c", j=2)
        own.gel = own.rot
        own.oT = own.raw[:].rearrange("p t j (c k) -> p t j c k", c=4)[:, :, 0, :, :]
        own.hm = own.v
        buffers.append(own)

    with nc.Block() as block:
        @block.gpsimd
        def _(pool):
            for s, o in zip(signals, buffers):
                for a in range(2):
                    up(s.k_t, pool.memset(o.kT[64 - 64 * a:P - 64 * a, a::2, :], 0.0))

        @block.vector
        def _(dve):
            for s, o in zip(signals, buffers):
                up(s.dve, dve.memset(o.prob[:, :, 0:WIN], 0.0))
                up(s.dve, dve.memset(o.hT[64:P, 0:1], 0.0))
            dve.wait_ge(m.loaded_b, 16 * m.loads_b)
            for w in m.layer:
                for j in range(2):
                    scale = w.qk_scale[:, j, :].unsqueeze(1).to_broadcast([P, NT, HD1])
                    up(s.dve, dve.tensor_tensor(w.tab_direct[:, :, j, :], w.tab_direct[:, :, j, :], scale, ALU.mult))
                    for half in range(2):
                        to, fro = slice(32 * half, 32 * half + 32), slice(32 - 32 * half, 64 - 32 * half)
                        part = w.tab_swap[:, :, j, to]
                        up(s.dve, dve.tensor_tensor(part, part, scale[:, :, fro], ALU.mult))
    clear(nc, signals)

    with nc.Fori(0, B // 2, 1) as b:
        x_pair = m.x[:, bass.ts(b, 2 * S)]
        with nc.Block() as block:
            @block.tensor
            def _(pe):
                def program(u):
                    s, o, ps, norm = signals[u], buffers[u], m.ps, Norm(m, signals, u)
                    k0 = 4 * u
                    sc = ps[:, k0:k0 + 2, :].rearrange("p b c -> p (b c)").rearrange("p (h c) -> p h c", h=4)
                    yield from norm.pe(0, x_pair[:, u * S:(u + 1) * S], k0, k0 + 1)
                    for l in range(L1):
                        w = m.layer[l]
                        pe.wait_ge(s.shifted.sem, 4 * l + 2)
                        pe.wait_ge(s.stream.sem, 2 * l + 1)
                        for n in range(3 * NT):
                            t, j = n // 3, n % 3
                            if n >= 4:
                                pe.wait_ge((s.q_raw, s.k_raw, s.v_raw)[(n - 4) % 3].sem, NT * l + (n - 4) // 3 + 1)
                            up(s.qkv_ready, pe.matmul(ps[:, k0 + n % 4, :], o.hT[:, t * P:(t + 1) * P],
                                                      w.wqkv[:, j * INNER:(j + 1) * INNER], start=True, stop=True))
                            yield
                        pe.wait_ge(s.q_raw.sem, NT * (l + 1))
                        pe.wait_ge(s.k_raw.sem, NT * (l + 1))
                        pe.wait_ge(s.v_raw.sem, NT * (l + 1))

                        def turn(t):
                            n = NT * l + t
                            pe.wait_ge(s.rotated.sem, n + 1)
                            for j, turned in enumerate((s.q_turned, s.k_turned)):
                                if j:
                                    pe.wait_ge(s.q_t.sem, n + 1)
                                elif n:
                                    pe.wait_ge(s.k_t.sem, 2 * n)
                                    if t != 1 or l:
                                        pe.wait_ge(s.own_kept.sem, 2 * (n - 1 if t else n))
                                for c in range(4):
                                    last = pe.transpose(ps[:, k0 + 2, c * P:(c + 1) * P],
                                                        o.rot[:, j, c * P:(c + 1) * P], m.ident[:])
                                up(turned, last)
                                yield

                        def scores(t, f):
                            n = NT * l + t
                            lo = P if t == 0 else WIN
                            pe.wait_ge(s.q_t.sem, n + 1)
                            pe.wait_ge(s.k_t.sem, 2 * n + 2)
                            if 2 * n + f:
                                pe.wait_ge(s.exp_done.sem, 4 * (2 * n + f))
                            for hh in range(4):
                                h = 4 * f + hh
                                dst = sc[:, hh, lo:2 * P]
                                pe.matmul(dst, o.qT[:, h // 2, :], o.kT[:, h, t * P + lo - P:(t + 1) * P],
                                          start=True, stop=False)
                                last = pe.matmul(dst, m.ident_bf[:], m.mask[:, lo - WIN:3 * WIN], start=False, stop=True)
                            up(s.scores_ready, last)

                        def turn_probs(t, f):
                            n = 2 * (NT * l + t) + f
                            past = 2 * (NT - 1) * l + 2 * (t - 1) + f
                            pe.wait_ge(s.p_scaled.sem, n + 1)
                            if n:
                                pe.wait_ge(s.own_kept.sem, n)
                            pe.wait_ge(s.k_t.sem, 2 * (NT * l + min(t + 2, NT)))
                            for hh in range(4):
                                last = pe.transpose(ps[:, k0 + 2, hh * P:(hh + 1) * P],
                                                    o.prob[:, 4 * f + hh, P:2 * P], m.ident[:])
                            up(s.own_turned, last)
                            if t:
                                if past:
                                    pe.wait_ge(s.past_kept.sem, past)
                                pe.wait_ge(s.o_t.sem, NT * l + t)
                                for hh in range(4):
                                    last = pe.transpose(ps[:, k0 + 3, hh * P:(hh + 1) * P],
                                                        o.prob[:, 4 * f + hh, 0:P], m.ident[:])
                                up(s.past_turned, last)

                        def weigh(t):
                            n = NT * l + t
                            if n:
                                pe.wait_ge(s.o_t.sem, n)
                            past = 2 * (NT - 1) * l + 2 * t
                            pe.wait_ge(s.own_kept.sem, 2 * n + 2)
                            if past:
                                pe.wait_ge(s.past_kept.sem, past)
                            for c in range(H1 // 2):
                                for past in range(2 if t else 1):
                                    for h in (2 * c, 2 * c + 1):
                                        rows = slice(HD1 * (h % 2), HD1 * (h % 2 + 1))
                                        last = pe.matmul(ps[rows, k0 + 3, c * P:(c + 1) * P],
                                                         o.v[:, t - past, h * HD1:(h + 1) * HD1],
                                                         o.pT[:, h // 4, 4 * (1 - past) + h % 4, :],
                                                         start=past == 0, stop=past == 1 or t == 0)
                            up(s.o_ready, last)

                        for t in range(NT + 1):
                            if t < NT:
                                yield from turn(t)
                            for f in range(2):
                                if t:
                                    turn_probs(t - 1, f)
                                    yield
                                if t < NT:
                                    scores(t, f)
                                    yield
                            if t:
                                weigh(t - 1)
                                yield
                        pe.wait_ge(s.o_t.sem, NT * (l + 1))
                        for c in range(4):
                            last = pe.matmul(ps[:, k0, :], w.wo[:, c, :], o.oT[:, :, c, :], start=c == 0, stop=c == 3)
                        up(s.res_ready, last)
                        yield
                        pe.wait_ge(s.shifted.sem, 4 * l + 4)
                        yield from norm.pe(1 + l, o.hT[:], k0 + 1, k0 + 2)
                        pe.wait_ge(s.act.sem, l + 1)
                        for c, (c0, rows) in enumerate(HCH):
                            if c == 2:
                                pe.wait_ge(s.h_done.sem, 3 * l + 1)
                            g_bank, a_bank = k0 + 2 * (c % 2), k0 + 2 * (c % 2) + 1
                            pe.matmul(ps[0:rows, g_bank, :], w.w1[:, HID1 + c0:HID1 + c0 + rows], o.hn[:],
                                      start=True, stop=True)
                            up(s.ga_ready, pe.matmul(ps[0:rows, a_bank, :], w.w1[:, c0:c0 + rows], o.hn[:],
                                                     start=True, stop=True))
                            yield
                        pe.wait_ge(s.h_done.sem, 3 * l + 2)
                        for c, (c0, rows) in enumerate(HCH):
                            if c == 2:
                                yield
                                pe.wait_ge(s.h_done.sem, 3 * l + c + 1)
                            last = pe.matmul(ps[:, k0 + 2, :], w.w2[0:rows, c, :], o.hm[0:rows, c, :],
                                             start=c == 0, stop=c == 2)
                        up(s.down_ready, last)
                        yield
                    pe.wait_ge(s.stream.sem, 1 + 2 * L1)
                    yield from norm.pe(1 + L1, o.y[:], k0, k0 + 1)

                in_turn(program(0), program(1))

            @block.scalar
            def _(act):
                def program(u):
                    s, o, ps, norm = signals[u], buffers[u], m.ps, Norm(m, signals, u)
                    k0 = 4 * u
                    sc = ps[:, k0:k0 + 2, :].rearrange("p b c -> p (b c)").rearrange("p (h c) -> p h c", h=4)
                    yield from norm.act(0, k0)

                    def shift(n):
                        act.wait_ge(s.stream.sem, n + 1)
                        act.activation(o.hT[0:64, :], o.y[0:64, :], ACT.Copy).then_inc(s.shifted.sem, 1)
                        act.activation(o.hT[64:P, 1:S], o.y[64:P, 0:S - 1], ACT.Copy).then_inc(s.shifted.sem, 1)

                    for l in range(L1):
                        w = m.layer[l]
                        shift(2 * l)
                        yield
                        for t in range(NT):
                            n = NT * l + t
                            act.wait_ge(s.qkv_ready.sem, 3 * n + 1)
                            act.activation(o.raw[:, t, 0, :], ps[:, k0 + (3 * t) % 4, :],
                                           ACT.Copy).then_inc(s.q_raw.sem, 1)
                            yield
                            act.wait_ge(s.k_raw.sem, n + 1)
                            act.wait_ge(s.q_raw.sem, n + 1)
                            if n:
                                act.wait_ge(s.summed.sem, n)
                            if l and t == 0:
                                act.wait_ge(s.o_ready.sem, NT * l)
                            act.activation(o.sq, o.raw[:, t, :, :], ACT.Square).then_inc(s.squared.sem, 1)
                            yield
                            act.wait_ge(s.qkv_ready.sem, 3 * n + 3)
                            act.activation(o.v[:, t, :], ps[:, k0 + (3 * t + 2) % 4, :],
                                           ACT.Copy).then_inc(s.v_raw.sem, 1)
                            yield
                        for t in range(NT + 1):
                            n = NT * l + t
                            if t < NT:
                                act.wait_ge(s.q_turned.sem, n + 1)
                                if n:
                                    act.wait_ge(s.scores_ready.sem, 2 * n)
                                act.activation(o.qT[:], ps[:, k0 + 2, :].rearrange("p (c k) -> p c k", c=4),
                                               ACT.Copy).then_inc(s.q_t.sem, 1)
                                yield
                                act.wait_ge(s.k_turned.sem, n + 1)
                                for a in range(2):
                                    rows = slice(64 * a, 64 * a + 64)
                                    act.activation(o.kT[rows, a::2, t * P:(t + 1) * P],
                                                   ps[rows, k0 + 2, :].rearrange("p (c k) -> p c k", c=4),
                                                   ACT.Copy).then_inc(s.k_t.sem, 1)
                                yield
                            for f in range(2):
                                if t:
                                    k = 2 * (n - 1) + f
                                    act.wait_ge(s.own_turned.sem, k + 1)
                                    if k >= 2:
                                        act.wait_ge(s.o_ready.sem, k // 2)
                                    act.activation(o.pT[:, f, 4:8, :],
                                                   ps[:, k0 + 2, :].rearrange("p (c k) -> p c k", c=4),
                                                   ACT.Copy).then_inc(s.own_kept.sem, 1)
                                    yield
                                if t < NT:
                                    lo = P if t == 0 else WIN
                                    act.wait_ge(s.neg_max.sem, 2 * n + f + 1)
                                    if n:
                                        act.wait_ge(s.own_turned.sem, 2 * n + f - 1)
                                        past = 2 * (NT - 1) * l + 2 * (t - 1) + f - 1
                                        if t and past > 0:
                                            act.wait_ge(s.past_turned.sem, past)
                                    for hh in range(4):
                                        h = 4 * f + hh
                                        act.activation(o.prob[:, h, lo:2 * P], sc[:, hh, lo:2 * P], ACT.Exp,
                                                       bias=o.nbias[:, t % 2, h:h + 1], scale=o.rq[:, t, h:h + 1],
                                                       accum_out=o.den[:, t % 2, h:h + 1]).then_inc(s.exp_done.sem, 1)
                                    yield
                            if t:
                                act.wait_ge(s.o_ready.sem, n)
                                act.activation(o.oT[:, t - 1, :, :], ps[:, k0 + 3, :].rearrange("p (c k) -> p c k", c=4),
                                               ACT.Copy).then_inc(s.o_t.sem, 1)
                                yield
                        shift(2 * l + 1)
                        yield
                        yield from norm.act(1 + l, k0 + 1)
                        act.wait_ge(s.ln_done.sem, 2 + l)
                        up(s.act, act.activation(o.hn[:], o.hn[:], ACT.Identity, bias=w.ln_b[:, 0:1],
                                                 scale=w.ln_g[:, 0:1]))
                        yield
                        for c, (c0, rows) in enumerate(HCH):
                            k = 3 * l + c
                            act.wait_ge(s.ga_ready.sem, k + 1)
                            if k >= 2:
                                act.wait_ge(s.h_done.sem, k - 1)
                            act.activation(o.gel[0:rows, c % 2, :], ps[0:rows, k0 + 2 * (c % 2), :], ACT.Gelu,
                                           bias=w.b1[0:rows, 3 + c:4 + c]).then_inc(s.gelu_done.sem, 1)
                            yield
                    yield from norm.act(1 + L1, k0)

                in_turn(program(0), program(1))

            @block.gpsimd
            def _(pool):
                def program(u):
                    s, o = signals[u], buffers[u]
                    for l in range(L1):
                        w = m.layer[l]
                        for t in range(NT):
                            n = NT * l + t
                            if t:
                                pool.wait_ge(s.factors.sem, 2 * l + 2)
                                kk = o.raw[:, t, 1, :].rearrange("p (h d) -> p h d", h=H1)
                                up(s.k_scaled, pool.tensor_tensor(
                                    kk, kk, o.rn[:, t, 1, :].unsqueeze(2).to_broadcast([P, H1, HD1]), ALU.mult))
                            pool.wait_ge(s.k_scaled.sem, n + 1)
                            if n:
                                pool.wait_ge(s.rotated.sem, n)
                            src = o.raw[:, t, :, :].rearrange("p j (h d) -> p j h d", h=H1)
                            dst = o.swap[:].rearrange("p j (h d) -> p j h d", h=H1)
                            for half in range(2):
                                to, fro = slice(32 * half, 32 * half + 32), slice(32 - 32 * half, 64 - 32 * half)
                                for j in range(2):
                                    up(s.swapped, pool.tensor_tensor(
                                        dst[:, j, :, to], src[:, j, :, fro],
                                        w.tab_swap[:, t, j, to].unsqueeze(1).to_broadcast([P, H1, 32]), ALU.mult))
                            yield

                in_turn(program(0), program(1))

            @block.vector
            def _(dve):
                def program(u):
                    s, o, ps, norm = signals[u], buffers[u], m.ps, Norm(m, signals, u)
                    k0 = 4 * u
                    sc = ps[:, k0:k0 + 2, :].rearrange("p b c -> p (b c)").rearrange("p (h c) -> p h c", h=4)
                    heads = lambda a: a.rearrange("p (h d) -> p h d", h=H1)
                    yield from norm.dve(0, k0 + 1, o.y[:])
                    dve.wait_ge(s.ln_done.sem, 1)
                    up(s.stream, dve.tensor_scalar(o.y[:], o.y[:], 1.0, None, ALU.mult))
                    yield
                    for l in range(L1):
                        w = m.layer[l]
                        def rotate(t):
                            n = NT * l + t
                            if t == 0:
                                kk = heads(o.raw[:, t, 1, :])
                                up(s.k_scaled, dve.tensor_tensor(
                                    kk, kk, o.rn[:, t, 1, :].unsqueeze(2).to_broadcast([P, H1, HD1]), ALU.mult))
                            dve.wait_ge(s.k_scaled.sem, n + 1)
                            if n:
                                dve.wait_ge(s.k_turned.sem, n)
                            for j in range(2):
                                up(s.dve, dve.tensor_tensor(
                                    heads(o.rot[:, j, :]), heads(o.raw[:, t, j, :]),
                                    w.tab_direct[:, t, j, :].unsqueeze(1).to_broadcast([P, H1, HD1]), ALU.mult))
                            yield
                            dve.wait_ge(s.dve.sem, s.dve.n)
                            dve.wait_ge(s.swapped.sem, 4 * (n + 1))
                            up(s.rotated, dve.tensor_tensor(o.rot[:], o.rot[:], o.swap[:], ALU.add))
                            dve.wait_ge(s.rotated.sem, n + 1)
                            yield

                        def norms(lo, hi):
                            dve.wait_ge(s.summed.sem, NT * l + hi)
                            own = o.ssq[:, lo:hi, :, :].rearrange("p t j h -> p (t j h)")
                            up(s.dve, dve.tensor_scalar(own, own, 1e-24, None, ALU.max))
                            tiles = lambda a: a[:, :, lo:hi, :, :].rearrange("p u t j h -> p u (t j h)")
                            rsqrt_of_both(dve, signals, u, tiles(ssq), tiles(rn), tiles(rn_t))
                            yield
                            link(dve, s.factors, dve.tensor_scalar(o.rq[:, lo:hi, :], o.rn[:, lo:hi, 0, :], 8.0, None,
                                                                   ALU.mult))

                        first = None
                        for t in range(NT):
                            n = NT * l + t
                            dve.wait_ge(s.qkv_ready.sem, 3 * n + 2)
                            up(s.k_raw, dve.tensor_copy(o.raw[:, t, 1, :], ps[:, k0 + (3 * t + 1) % 4, :]))
                            yield
                            if t:
                                dve.wait_ge(s.squared.sem, n)
                                up(s.summed, dve.tensor_reduce(o.ssq[:, t - 1, :, :],
                                                               o.sq.rearrange("p j (h d) -> p j h d", h=H1),
                                                               AX.X, ALU.add))
                            yield
                            if t == 1:
                                yield from norms(0, 1)
                                first = rotate(0)
                            if t >= 1:
                                next(first, None)
                        dve.wait_ge(s.squared.sem, NT * (l + 1))
                        up(s.summed, dve.tensor_reduce(o.ssq[:, NT - 1, :, :],
                                                       o.sq.rearrange("p j (h d) -> p j h d", h=H1), AX.X, ALU.add))
                        yield from norms(1, NT)
                        def scale(t, f):
                            n, hs, lo = NT * l + t, slice(4 * f, 4 * f + 4), P if t == 0 else WIN
                            dve.wait_ge(s.exp_done.sem, 4 * (2 * n + f + 1))
                            link(dve, s.dve, dve.reciprocal(o.rden[:, hs], o.den[:, t % 2, hs]))
                            part = o.prob[:, hs, lo:2 * P]
                            up(s.p_scaled, dve.tensor_tensor(
                                part, part, o.rden[:, hs].unsqueeze(2).to_broadcast([P, 4, 2 * P - lo]), ALU.mult))

                        for t in range(NT + 1):
                            n = NT * l + t
                            if t:
                                scale(t - 1, 1)
                                yield
                            if t + 1 < NT:
                                following = rotate(t + 1)
                                next(following)
                                yield
                            for f in range(2):
                                if t > 1:
                                    k = 2 * (n - 1) + f
                                    dve.wait_ge(s.past_turned.sem, 2 * (NT - 1) * l + 2 * (t - 2) + f + 1)
                                    dve.wait_ge(s.o_ready.sem, k // 2)
                                    up(s.past_kept, dve.tensor_copy(
                                        o.pT[:, f, 0:4, :], ps[:, k0 + 3, :].rearrange("p (c k) -> p c k", c=4)))
                                    yield
                                if t < NT:
                                    lo = P if t == 0 else WIN
                                    hs = slice(4 * f, 4 * f + 4)
                                    dve.wait_ge(s.scores_ready.sem, 2 * n + f + 1)
                                    link(dve, s.dve, dve.tensor_reduce(o.nmax[:, hs], sc[:, :, lo:2 * P], AX.X, ALU.max,
                                                                       negate=True))
                                    if n >= 2:
                                        dve.wait_ge(s.exp_done.sem, 8 * (n - 1))
                                    up(s.neg_max, dve.tensor_tensor(o.nbias[:, t % 2, hs], o.nmax[:, hs],
                                                                    o.rq[:, t, hs], ALU.mult))
                                    yield
                                if f == 0 and t + 1 < NT:
                                    next(following)
                                    yield
                            if t < NT:
                                scale(t, 0)
                                yield
                        dve.wait_ge(s.res_ready.sem, l + 1)
                        up(s.stream, dve.tensor_tensor(o.y[:], o.y[:], ps[:, k0, :], ALU.add))
                        yield
                        yield from norm.dve(1 + l, k0 + 2, o.hn[:])
                        for c, (c0, rows) in enumerate(HCH):
                            k = 3 * l + c
                            dve.wait_ge(s.gelu_done.sem, k + 1)
                            up(s.h_done, dve.scalar_tensor_tensor(
                                out=o.hm[0:rows, c, :], in0=ps[0:rows, k0 + 2 * (c % 2) + 1, :],
                                scalar=w.b1[0:rows, c:c + 1], in1=o.gel[0:rows, c % 2, :], op0=ALU.add, op1=ALU.mult))
                            yield
                        dve.wait_ge(s.down_ready.sem, l + 1)
                        up(s.stream, dve.scalar_tensor_tensor(out=o.y[:], in0=ps[:, k0 + 2, :], scalar=w.b2[:, 0:1],
                                                              in1=o.y[:], op0=ALU.add, op1=ALU.add))
                        yield
                    yield from norm.dve(1 + L1, k0 + 1, o.hn[:])
                    dve.wait_ge(s.ln_done.sem, 2 + L1)
                    x_b = x_pair[:, u * S:(u + 1) * S]
                    up(s.dve, dve.tensor_tensor(x_b, x_b, o.hn[:], ALU.add))

                in_turn(program(0), program(1))
        clear(nc, signals)


def delta_prepare(m, ctx, st):
    nc, ps = m.nc, m.ps
    sb = lambda name, shape, dt=F32: ctx.enter_context(nc.sbuf_tensor(name, shape, dt))
    tile_signals = Signals(nc, ctx, "tiles")
    s = tile_signals
    (s.n_ready, s.nt_ready, s.at_ready, s.nt_raw, s.level_masked, s.tt_ready, s.t_ready, s.att_ready, s.x_ready,
     s.x_copied, s.tx_ready, s.txt_ready, s.uw_ready, s.wt_ready, s.uw_copied, s.out_ready, s.out_copied, s.qp_done,
     s.u_kept) = s.new(
        "n_ready nt_ready at_ready nt_raw level_masked tt_ready t_ready att_ready x_ready x_copied tx_ready "
        "txt_ready uw_ready wt_ready uw_copied out_ready out_copied qp_done u_kept")
    signals, buffers = [], []
    UNITS = 10
    ssq, rn, rn_t = (sb(f"c_{n}", [P, 2, 2, NT * H2]) for n in ("ssq", "rn", "rn_t"))
    shared = sb("c_shared", [P, 2 * UNITS, S])
    for u in range(2):
        s, own = Signals(nc, ctx, u), Store()
        (s.act, s.conv_ready, s.gates_ready, s.sigmoid_done, s.silu_done, s.turned, s.tok_copied,
         s.half_done, s.base_done, s.rot_done, s.rot_squared, s.k_norm, s.q_norm, s.b_weighed, s.v_weighed,
         s.f_turned, s.q_t, s.kb_t, s.k_t, s.gamma_ready, s.gamma_wide, s.k_kept) = s.new(
            "act conv_ready gates_ready sigmoid_done silu_done turned tok_copied half_done base_done rot_done "
            "rot_squared k_norm q_norm b_weighed v_weighed f_turned q_t kb_t k_t gamma_ready gamma_wide k_kept")
        signals.append(s)
        mine = shared[:, u * UNITS:(u + 1) * UNITS, :]
        own.sg, own.act3, own.half_a, own.half_b = mine[:, 0, :], mine[:, 1:4, :], mine[:, 4:6, :], mine[:, 6:8, :]
        own.ktok, own.wide = (mine[:, i, :].rearrange("p (t c) -> p t c", t=NT) for i in (8, 9))
        own.tok = m.norm_buffers[u].both
        own.xp = sb(f"c_xp{u}", [P, TAPS - 1 + S])
        own.xn = own.xp[:, TAPS - 1:TAPS - 1 + S]
        own.bg = sb(f"c_bg{u}", [P, NT, 2, H2])
        own.ssq, own.rn = (a[:, u, :, :] for a in (ssq, rn))
        own.vk = sb(f"c_vk{u}", [P, NT, H2, 2, HD2])
        own.qT, own.kbT, own.kT = sb(f"c_qT{u}", [P, S]), sb(f"c_kbT{u}", [P, S]), sb(f"c_kT{u}", [P, H2, S])
        buffers.append(own)
    unit = lambda i: shared[:, i, :].rearrange("p (h c) -> p h c", h=H2)
    T, TT, X, NT_raw, att = ([unit(2 * i), unit(2 * i + 1)] for i in range(5))
    NTs = [[unit(10), unit(11)], [unit(12), unit(13)]]
    uw = [shared[:, 14, u * 2 * P:(u + 1) * 2 * P].rearrange("p (h a c) -> p h a c", h=H2, a=2) for u in range(2)]
    heads = lambda a: a.unsqueeze(1).to_broadcast([P, H2, P])
    bank = lambda k: ps[:, k, :].rearrange("p (h c) -> p h c", h=H2)
    g16 = lambda a: a.rearrange("p (g c) -> p g c", c=HD2)
    even_odd = lambda a: a.rearrange("p (g i two) -> p g two i", two=2, i=HD2 // 2)
    halves = lambda a: a.rearrange("p (g two i) -> p g two i", two=2, i=HD2 // 2)

    def summed(versions, t0, i, u):
        return versions * t0 + 2 * i + u + 1

    with nc.Block() as block:
        @block.vector
        def _(dve):
            for s, o in zip(signals, buffers):
                up(s.dve, dve.memset(o.kT[:], 0.0))
                up(s.dve, dve.memset(o.xp[:], 0.0))
    clear(nc, signals)

    with nc.Fori(0, B // 2, 1) as b:
        x_pair = m.x[:, bass.ts(b, 2 * S)]
        with nc.Block() as block:
            @block.tensor
            def _(pe):
                def program(u):
                    s, o, ps, norm, k0 = signals[u], buffers[u], m.ps, Norm(m, signals, u), 4 * u
                    yield from norm.pe(0, x_pair[:, u * S:(u + 1) * S], k0, k0 + 1)
                    pe.wait_ge(s.ln_done.sem, 1)
                    for j in range(3):
                        for tap in range(TAPS):
                            last = pe.matmul(ps[:, k0 + j, :], m.c_taps[:, j, tap, :], o.xp[:, tap:tap + S],
                                             start=tap == 0, stop=tap == TAPS - 1)
                        up(s.conv_ready, last)
                        yield
                    for t in range(NT):
                        last = pe.matmul(ps[:, k0 + 3, t * 8:t * 8 + 8], o.xn[:, t * P:(t + 1) * P], m.c_wbg[:],
                                         start=True, stop=True)
                    up(s.gates_ready, last)
                    yield
                    for j in range(3):
                        pe.wait_ge(s.silu_done.sem, j + 1)
                        for t in range(NT):
                            last = pe.transpose(ps[:, k0 + j, t * P:(t + 1) * P], o.act3[:, j, t * P:(t + 1) * P], m.ident[:])
                        up(s.turned, last)
                        yield
                    pe.wait_ge(s.gamma_wide.sem, NT)
                    for t in range(NT):
                        last = pe.matmul(ps[:, k0 + 3, 64 + t * 4:64 + t * 4 + 4], o.wide[:, t, :], m.c_chunk_mean[:], start=True, stop=True)
                    up(s.gamma_ready, last)
                    yield
                    pe.wait_ge(s.q_norm.sem, 1)
                    for t in range(NT):
                        last = pe.transpose(ps[:, k0, t * P:(t + 1) * P], o.half_a[:, 0, t * P:(t + 1) * P], m.ident[:])
                    up(s.f_turned, last)
                    yield
                    pe.wait_ge(s.k_norm.sem, 1)
                    for t in range(NT):
                        last = pe.transpose(ps[:, k0 + 1, t * P:(t + 1) * P], o.ktok[:, t, :], m.ident[:])
                    up(s.f_turned, last)
                    yield
                    pe.wait_ge(s.b_weighed.sem, NT)
                    pe.wait_ge(s.act.sem, 1)
                    for t in range(NT):
                        last = pe.transpose(ps[:, k0 + 3, t * P:(t + 1) * P], o.half_b[:, 0, t * P:(t + 1) * P], m.ident[:])
                    up(s.f_turned, last)
                    yield

                in_turn(program(0), program(1))

            @block.scalar
            def _(act):
                def program(u):
                    s, o, ps, norm, k0 = signals[u], buffers[u], m.ps, Norm(m, signals, u), 4 * u
                    yield from norm.act(0, k0)
                    for j in range(3):
                        act.wait_ge(s.conv_ready.sem, j + 1)
                        if j:
                            act.wait_ge(s.silu_done.sem, j)
                        act.activation(o.sg, ps[:, k0 + j, :], ACT.Sigmoid).then_inc(s.sigmoid_done.sem, 1)
                        yield
                    act.wait_ge(s.gates_ready.sem, 1)
                    act.activation(o.bg[:].rearrange("p t g h -> p (t g h)"), ps[:, k0 + 3, 0:8 * NT],
                                   ACT.Sigmoid).then_inc(s.sigmoid_done.sem, 1)
                    yield
                    for j in range(2):
                        act.wait_ge(s.turned.sem, j + 1)
                        act.activation(o.tok[:, j, :], ps[:, k0 + j, :], ACT.Copy).then_inc(s.tok_copied.sem, 1)
                        yield
                    act.wait_ge(s.sigmoid_done.sem, 4)
                    for t in range(NT):
                        act.activation(o.wide[:, t, :].rearrange("p (h c) -> p h c", h=H2),
                                       o.bg[:, t, 1, :].unsqueeze(2).to_broadcast([P, H2, HD2]),
                                       ACT.Copy).then_inc(s.gamma_wide.sem, 1)
                    yield
                    for j in range(2):
                        act.wait_ge(s.rot_done.sem, 2 * j + 2)
                        act.activation(o.half_b[:, j, :], o.half_a[:, j, :], ACT.Square).then_inc(s.rot_squared.sem, 1)
                        yield
                    act.wait_ge(s.gamma_ready.sem, 1)
                    act.activation(st.g[:, :, bass.ts(b, 2), :][:, :, u, :],
                                   ps[:, k0 + 3, 64:64 + 4 * NT].rearrange("p (t c) -> p t c", t=NT), ACT.Copy).then_inc(s.act.sem, 1)
                    yield
                    act.wait_ge(s.f_turned.sem, 1)
                    act.activation(o.qT[:], ps[:, k0, :], ACT.Copy).then_inc(s.q_t.sem, 1)
                    yield
                    act.wait_ge(s.f_turned.sem, 2)
                    for h in range(H2):
                        rows = slice(32 * h, 32 * h + 32)
                        act.activation(o.kT[rows, h, :], ps[rows, k0 + 1, :], ACT.Copy).then_inc(s.k_t.sem, 1)
                    yield
                    act.wait_ge(s.f_turned.sem, 3)
                    act.activation(o.kbT[:], ps[:, k0 + 3, :], ACT.Copy).then_inc(s.kb_t.sem, 1)
                    yield

                in_turn(program(0), program(1))

            @block.gpsimd
            def _(pool):
                def program(u):
                    s, o = signals[u], buffers[u]
                    for j in range(2):
                        yield
                        pool.wait_ge(s.tok_copied.sem, j + 1)
                        for half in range(2):
                            up(s.half_done, pool.tensor_tensor(halves(o.half_b[:, j, :])[:, :, half, :],
                                                               even_odd(o.tok[:, j, :])[:, :, 1 - half, :],
                                                               halves(m.c_sin[:])[:, :, half, :], ALU.mult))
                    yield
                    pool.wait_ge(s.k_norm.sem, 1)
                    pool.tensor_copy(st.k[:, :, bass.ts(b, 2), :][:, :, u, :],
                                     o.ktok[:]).then_inc(s.k_kept.sem, 1)

                in_turn(program(0), program(1))

            @block.vector
            def _(dve):
                def program(u):
                    s, o, ps, norm, k0 = signals[u], buffers[u], m.ps, Norm(m, signals, u), 4 * u
                    yield from norm.dve(0, k0 + 1, o.xn)
                    for j in range(3):
                        dve.wait_ge(s.sigmoid_done.sem, j + 1)
                        up(s.silu_done, dve.tensor_tensor(o.act3[:, j, :], ps[:, k0 + j, :], o.sg[:], ALU.mult))
                        yield
                    for j in range(2):
                        yield
                        dve.wait_ge(s.tok_copied.sem, j + 1)
                        link(dve, s.dve, dve.tensor_tensor(halves(o.half_a[:, j, :]), even_odd(o.tok[:, j, :]),
                                                           halves(m.c_cos[:]), ALU.mult))
                        up(s.base_done, dve.tensor_tensor(o.act3[:, j, :].rearrange("p (t h c) -> p t h c", t=NT, h=H2),
                                                           o.tok[:, j, :].rearrange("p (t h c) -> p t h c", t=NT, h=H2),
                                                           m.c_share[:].rearrange("p (t h c) -> p t h c", t=NT, h=H2),
                                                           ALU.mult))
                        yield
                        dve.wait_ge(s.half_done.sem, 2 * j + 2)
                        up(s.rot_done, dve.tensor_tensor(o.half_a[:, j, :], o.half_a[:, j, :], o.half_b[:, j, :], ALU.add))
                        dve.wait_ge(s.rot_done.sem, s.rot_done.n)
                        dve.wait_ge(s.base_done.sem, j + 1)
                        up(s.rot_done, dve.tensor_tensor(o.half_a[:, j, :], o.half_a[:, j, :], o.act3[:, j, :], ALU.add))
                    yield
                    dve.wait_ge(s.turned.sem, 3)
                    dve.wait_ge(s.sigmoid_done.sem, 4)
                    for t in range(NT):
                        up(s.v_weighed, dve.tensor_tensor(
                            o.vk[:, t, :, 0, :], ps[:, k0 + 2, t * P:(t + 1) * P].rearrange("p (h c) -> p h c", h=H2),
                            o.bg[:, t, 0, :].unsqueeze(2).to_broadcast([P, H2, HD2]), ALU.mult))
                    yield
                    for j in range(2):
                        dve.wait_ge(s.rot_squared.sem, j + 1)
                        link(dve, s.dve, dve.tensor_reduce(o.ssq[:, j, :], g16(o.half_b[:, j, :]), AX.X, ALU.add))
                    up(s.dve, dve.tensor_scalar(o.ssq, o.ssq, 1e-6, None, ALU.add))
                    flat = lambda a: a[:].rearrange("p u j g -> p (u j g)")
                    rsqrt_of_both(dve, signals, u, flat(ssq), flat(rn), flat(rn_t))
                    yield
                    wide_rn = lambda j: o.rn[:, j, :].unsqueeze(2).to_broadcast([P, NT * H2, HD2])
                    up(s.q_norm, dve.tensor_tensor(g16(o.half_a[:, 0, :]), g16(o.half_a[:, 0, :]), wide_rn(0), ALU.mult))
                    up(s.k_norm, dve.tensor_tensor(g16(o.ktok[:].rearrange("p t c -> p (t c)")), g16(o.half_a[:, 1, :]),
                                                   wide_rn(1), ALU.mult))
                    yield
                    dve.wait_ge(s.k_norm.sem, 1)
                    for t in range(NT):
                        link(dve, s.dve, dve.tensor_tensor(
                            o.half_b[:, 0, t * P:(t + 1) * P].rearrange("p (h c) -> p h c", h=H2),
                            o.ktok[:, t, :].rearrange("p (h c) -> p h c", h=H2),
                            o.bg[:, t, 0, :].unsqueeze(2).to_broadcast([P, H2, HD2]), ALU.mult))
                        up(s.b_weighed, dve.tensor_copy(
                            o.vk[:, t, :, 1, :], o.half_b[:, 0, t * P:(t + 1) * P].rearrange("p (h c) -> p h c", h=H2)))

                in_turn(program(0), program(1))

        mine = lambda a, t: a[:, t % NT, bass.ts(b, 2), :][:, t // NT, :]
        with nc.Block() as block:
            @block.tensor
            def _(pe):
                s = tile_signals
                for t0 in range(0, 2 * NT, 2):
                    for u in range(2):
                        t, o = t0 + u, buffers[t0 // NT]
                        tile = slice(t % NT * P, (t % NT + 1) * P)
                        if t0:
                            pe.wait_ge(s.qp_done.sem, t - 1)
                            pe.wait_ge(s.out_copied.sem, 2 * t0)
                            pe.wait_ge(s.uw_copied.sem, t - 1)
                        for h in range(H2):
                            last = pe.matmul(ps[:, 4 * u, h * P:(h + 1) * P], o.kbT[:, tile], o.kT[:, h, tile],
                                             start=True, stop=True)
                        up(s.n_ready, last)
                        for h in range(H2):
                            last = pe.matmul(ps[:, 4 * u + 1, h * P:(h + 1) * P], o.kT[:, h, tile], o.kbT[:, tile],
                                             start=True, stop=True)
                        up(s.nt_ready, last)
                        for h in range(H2):
                            last = pe.matmul(ps[:, 4 * u + 2, h * P:(h + 1) * P], o.kT[:, h, tile], o.qT[:, tile],
                                             start=True, stop=True)
                        up(s.at_ready, last)
                    for i in range(LEVELS):
                        for u in range(2):
                            k = LEVELS * t0 + 2 * i + u
                            pe.wait_ge(s.level_masked.sem, k + 1)
                            pe.wait_ge(s.t_ready.sem, summed(LEVELS, t0, i, u))
                            if i:
                                pe.wait_ge(s.x_copied.sem, k - 1)
                            for h in range(H2):
                                last = pe.matmul(ps[:, 4 * u, h * P:(h + 1) * P], NTs[u][i % 2][:, h, :], T[u][:, h, :],
                                                 start=True, stop=True)
                            up(s.x_ready, last)
                        for u in range(2):
                            k = LEVELS * t0 + 2 * i + u
                            pe.wait_ge(s.x_copied.sem, k + 1)
                            pe.wait_ge(s.tt_ready.sem, summed(LEVELS + 1, t0, i, u))
                            pe.wait_ge(s.att_ready.sem, t0 + u + 1)
                            if i < LEVELS - 1:
                                for h in range(H2):
                                    last = pe.matmul(ps[:, 4 * u + 1, h * P:(h + 1) * P], TT[u][:, h, :],
                                                     X[u][:, h, :], start=True, stop=True)
                                up(s.tx_ready, last)
                            for h in range(H2):
                                last = pe.matmul(ps[:, 4 * u + 2, h * P:(h + 1) * P], X[u][:, h, :], TT[u][:, h, :],
                                                 start=True, stop=True)
                            up(s.txt_ready, last)
                    for u in range(2):
                        t = t0 + u
                        pe.wait_ge(s.tt_ready.sem, summed(LEVELS + 1, t0, LEVELS, u))
                        for h in range(H2):
                            last = pe.matmul(ps[:, 4 * u, h * 64:(h + 1) * 64], TT[u][:, h, :],
                                             buffers[t // NT].vk[:, t % NT, h, :, :].rearrange("p a c -> p (a c)"), start=True, stop=True)
                        up(s.uw_ready, last)
                        for h in range(H2):
                            last = pe.matmul(ps[32 * h:32 * h + 32, 4 * u + 1, 0:P], buffers[t // NT].vk[:, t % NT, h, 1, :], TT[u][:, h, :],
                                             start=True, stop=True)
                        up(s.wt_ready, last)
                    for u in range(2):
                        t = t0 + u
                        pe.wait_ge(s.uw_copied.sem, t + 1)
                        for h in range(H2):
                            pe.matmul(ps[:, 4 * u + 3, h * HD2:(h + 1) * HD2], att[u][:, h, :], uw[u][:, h, 0, :],
                                      start=True, stop=True)
                        for h in range(H2):
                            last = pe.matmul(ps[32 * h:32 * h + 32, 4 * u + 3, P:2 * P], uw[u][:, h, 1, :],
                                             att[u][:, h, :], start=True, stop=True)
                        up(s.out_ready, last)

            @block.scalar
            def _(act):
                s = tile_signals
                for t0 in range(0, 2 * NT, 2):
                    for u in range(2):
                        act.wait_ge(s.nt_ready.sem, t0 + u + 1)
                        if t0:
                            act.wait_ge(s.level_masked.sem, 2 * LEVELS * (t0 // 2))
                        act.activation(NT_raw[u][:], bank(4 * u + 1), ACT.Copy).then_inc(s.nt_raw.sem, 1)
                    for i in range(LEVELS):
                        for u in range(2):
                            k = LEVELS * t0 + 2 * i + u
                            act.wait_ge(s.x_ready.sem, k + 1)
                            if k >= 2:
                                act.wait_ge(s.txt_ready.sem, k - 1)
                            act.activation(X[u][:], bank(4 * u), ACT.Copy).then_inc(s.x_copied.sem, 1)
                    for u in range(2):
                        t = t0 + u
                        act.wait_ge(s.uw_ready.sem, t + 1)
                        if t0:
                            act.wait_ge(s.out_ready.sem, t - 1)
                            act.wait_ge(s.u_kept.sem, t - 1)
                        act.activation(uw[u][:].rearrange("p h a c -> p (h a c)"), ps[:, 4 * u, 0:2 * P],
                                       ACT.Copy).then_inc(s.uw_copied.sem, 1)
                        act.wait_ge(s.wt_ready.sem, t + 1)
                        act.activation(mine(st.wT, t), ps[:, 4 * u + 1, 0:P], ACT.Copy).then_inc(s.out_copied.sem, 1)
                    for u in range(2):
                        t = t0 + u
                        act.wait_ge(s.out_ready.sem, t + 1)
                        act.activation(mine(st.o, t), ps[:, 4 * u + 3, 0:P], ACT.Copy).then_inc(s.out_copied.sem, 1)

            @block.gpsimd
            def _(pool):
                s = tile_signals
                for t0 in range(0, 2 * NT, 2):
                    for i in range(LEVELS):
                        for u in range(2):
                            k = LEVELS * t0 + 2 * i + u
                            if i == 0:
                                pool.wait_ge(s.nt_raw.sem, t0 + u + 1)
                            if k >= 4:
                                pool.wait_ge(s.x_ready.sem, k - 3)
                            up(s.level_masked, pool.tensor_tensor(NTs[u][i % 2][:], NT_raw[u][:],
                                                                  heads(m.c_level[:, i, :]), ALU.mult))
                    for u in range(2):
                        t = t0 + u
                        pool.wait_ge(s.uw_copied.sem, t + 1)
                        up(s.u_kept, pool.tensor_copy(mine(st.u, t).rearrange("p (h c) -> p h c", h=H2),
                                                      uw[u][:, :, 0, :]))

            @block.vector
            def _(dve):
                s = tile_signals
                for t0 in range(0, 2 * NT, 2):
                    for u in range(2):
                        t = t0 + u
                        dve.wait_ge(s.n_ready.sem, t + 1)
                        if t0:
                            dve.wait_ge(s.out_ready.sem, t - 1)
                        link(dve, s.dve, dve.tensor_tensor(T[u][:], bank(4 * u), heads(m.c_first[:, 0, :]), ALU.mult))
                        up(s.t_ready, dve.tensor_tensor(T[u][:], T[u][:], heads(m.ident[:]), ALU.add))
                        dve.wait_ge(s.nt_ready.sem, t + 1)
                        dve.wait_ge(s.nt_raw.sem, t + 1)
                        link(dve, s.dve, dve.tensor_tensor(TT[u][:], bank(4 * u + 1), heads(m.c_first[:, 1, :]),
                                                           ALU.mult))
                        up(s.tt_ready, dve.tensor_tensor(TT[u][:], TT[u][:], heads(m.ident[:]), ALU.add))
                        dve.wait_ge(s.at_ready.sem, t + 1)
                        up(s.att_ready, dve.tensor_tensor(att[u][:], bank(4 * u + 2), heads(m.c_causal[:]), ALU.mult))
                    for i in range(LEVELS):
                        for u in range(2):
                            k = LEVELS * t0 + 2 * i + u
                            dve.wait_ge(s.txt_ready.sem, k + 1)
                            if i < LEVELS - 1:
                                dve.wait_ge(s.tx_ready.sem, k - t0 + 1)
                                dve.wait_ge(s.t_ready.sem, s.t_ready.n)
                                up(s.t_ready, dve.tensor_tensor(T[u][:], T[u][:], bank(4 * u + 1), ALU.add))
                            dve.wait_ge(s.tt_ready.sem, s.tt_ready.n)
                            up(s.tt_ready, dve.tensor_tensor(TT[u][:], TT[u][:], bank(4 * u + 2), ALU.add))
                    for u in range(2):
                        t = t0 + u
                        dve.wait_ge(s.out_ready.sem, t + 1)
                        dve.wait_ge(s.out_copied.sem, 4 * (t0 // 2) + 3 + u)
                        up(s.qp_done, dve.tensor_tensor(mine(st.qT, t), buffers[t // NT].qT[:, t % NT * P:(t % NT + 1) * P],
                                                        ps[:, 4 * u + 3, P:2 * P], ALU.subtract))
        clear(nc, signals + [tile_signals])


def delta_scan(m, ctx, st):
    nc = m.nc
    sb = lambda name, shape, dt=F32: ctx.enter_context(nc.sbuf_tensor(name, shape, dt))
    HB = B // 2
    signals, buffers = [], []
    for u in range(2):
        s, own = Signals(nc, ctx, u), Store()
        (s.staged, s.staged_k, s.ws_ready, s.qs_ready, s.u_done, s.ku_ready, s.spread_dve, s.spread_act,
         s.stacked, s.o_done) = s.new(
            "staged staged_k ws_ready qs_ready u_done ku_ready spread_dve spread_act stacked o_done")
        own.w, own.q, own.k, own.u = (sb(f"s_{n}{u}", [P, HB, P]) for n in ("w", "q", "k", "u"))
        own.stack, own.decayed = sb(f"s_stack{u}", [P, HB, HD2]), sb(f"s_decayed{u}", [P, HB, HD2])
        own.diag = sb(f"s_diag{u}", [P, HB, P])
        signals.append(s)
        buffers.append(own)

    with nc.Block() as block:
        @block.vector
        def _(dve):
            for s, o in zip(signals, buffers):
                up(s.dve, dve.memset(o.stack[:], 0.0))
                up(s.dve, dve.memset(o.diag[:], 0.0))
    clear(nc, signals)

    with nc.Fori(0, NT, 1) as t:
        now = lambda a, u: a[:, bass.ds(t, 1), :, :].rearrange("p a b c -> p (a b) c")[:, u * HB:(u + 1) * HB, :]
        with nc.Block() as block:
            @block.tensor
            def _(pe):
                def program(u):
                    s, o, ps, k0 = signals[u], buffers[u], m.ps, 4 * u
                    pe.wait_ge(s.staged.sem, 2)
                    pe.wait_ge(s.staged_k.sem, 1)
                    for r in range(4):
                        rows = slice(32 * r, 32 * r + 32)
                        if r:
                            pe.wait_ge(s.spread_dve.sem, 2 * r)
                            pe.wait_ge(s.spread_act.sem, 2 * r)
                        for b in range(HB):
                            last = pe.matmul(ps[rows, k0, b * P:(b + 1) * P], o.w[:, b, rows], o.diag[:, b, :],
                                             start=True, stop=True)
                        up(s.ws_ready, last)
                        yield
                        if r:
                            pe.wait_ge(s.o_done.sem, r)
                        for b in range(HB):
                            last = pe.matmul(ps[rows, k0 + 1, b * P:(b + 1) * P], o.q[:, b, rows], o.diag[:, b, :],
                                             start=True, stop=True)
                        up(s.qs_ready, last)
                        yield
                        if r:
                            pe.wait_ge(s.stacked.sem, r)
                        pe.wait_ge(s.u_done.sem, r + 1)
                        for b in range(HB):
                            for h in range(H2):
                                cols = slice(32 * h, 32 * h + 32)
                                last = pe.matmul(ps[cols, k0 + 2, b * HD2:(b + 1) * HD2], o.k[rows, b, cols],
                                                 o.u[rows, b, cols], start=True, stop=True)
                        up(s.ku_ready, last)
                        yield

                in_turn(program(0), program(1))

            @block.scalar
            def _(act):
                def program(u):
                    s, o = signals[u], buffers[u]
                    act.activation(o.w[:], now(st.wT, u), ACT.Copy).then_inc(s.staged.sem, 1)
                    yield
                    act.activation(o.q[:], now(st.qT, u), ACT.Copy).then_inc(s.staged.sem, 1)
                    yield
                    for r in range(4):
                        act.wait_ge(s.stacked.sem, r + 1)
                        act.wait_ge(s.qs_ready.sem, r + 1)
                        for h in range(2):
                            blk = slice(32 * h, 32 * h + 32)
                            act.activation(o.diag[blk, :, blk], o.stack[blk, :, :],
                                           ACT.Copy).then_inc(s.spread_act.sem, 1)
                        yield

                in_turn(program(0), program(1))

            @block.vector
            def _(dve):
                def program(u):
                    s, o, ps, k0 = signals[u], buffers[u], m.ps, 4 * u
                    half = slice(u * HB, (u + 1) * HB)
                    bank = lambda i, rows: ps[rows, k0 + i, 0:HB * P].rearrange("p (b c) -> p b c", c=P)
                    up(s.staged_k, dve.tensor_copy(o.k[:], now(st.k, u)))
                    yield
                    for r in range(4):
                        rows = slice(32 * r, 32 * r + 32)
                        g = st.g[:, bass.ds(t, 1), half, r:r + 1].rearrange("p a b c -> p (a b c)")
                        if r:
                            dve.wait_ge(s.stacked.sem, r)
                            dve.wait_ge(s.spread_act.sem, 2 * r)
                        link(dve, s.dve, dve.tensor_tensor(o.decayed[:], o.stack[:],
                                                           g.unsqueeze(2).to_broadcast([P, HB, HD2]), ALU.mult))
                        dve.wait_ge(s.ws_ready.sem, r + 1)
                        up(s.u_done, dve.tensor_tensor(o.u[rows, :, :], now(st.u, u)[rows, :, :], bank(0, rows),
                                                       ALU.subtract))
                        yield
                        dve.wait_ge(s.ku_ready.sem, r + 1)
                        up(s.stacked, dve.tensor_tensor(o.stack[:], o.decayed[:],
                                                        ps[:, k0 + 2, 0:HB * HD2].rearrange("p (b c) -> p b c", c=HD2),
                                                        ALU.add))
                        dve.wait_ge(s.stacked.sem, r + 1)
                        dve.wait_ge(s.qs_ready.sem, r + 1)
                        for h in range(2, H2):
                            blk = slice(32 * h, 32 * h + 32)
                            up(s.spread_dve, dve.tensor_copy(o.diag[blk, :, blk], o.stack[blk, :, :]))
                        out = now(st.o, u)[rows, :, :]
                        up(s.o_done, dve.tensor_tensor(out, out, bank(1, rows), ALU.add))
                        yield

                in_turn(program(0), program(1))
        clear(nc, signals)


def delta_finish(m, ctx, st):
    nc = m.nc
    sb = lambda name, shape, dt=F32: ctx.enter_context(nc.sbuf_tensor(name, shape, dt))
    PAD = 2 ** (DILATIONS - 1)
    ssq, rn, rn_t = (sb(f"f_{n}", [P, 2 * NT * H2]) for n in ("ssq", "rn", "rn_t"))
    signals, buffers = [], []
    for u in range(2):
        s, own = Signals(nc, ctx, u), Store()
        (s.squared, s.o_norm, s.o_turned, s.o_t, s.core_ready, s.gate_ready, s.gate_done, s.frac,
         s.frac_squared, s.frac_var, s.frac_diag, s.frac_spread, s.y_ready) = s.new(
            "squared o_norm o_turned o_t core_ready gate_ready gate_done frac frac_squared frac_var "
            "frac_diag frac_spread y_ready")
        own.xp = sb(f"f_xp{u}", [P, PAD + S])
        own.xn = own.xp[:, PAD:PAD + S]
        own.osq, own.on, own.oT = sb(f"f_osq{u}", [P, NT, P]), sb(f"f_on{u}", [P, NT, P]), sb(f"f_oT{u}", [P, S])
        own.ssq, own.rn = (a[:, u * NT * H2:(u + 1) * NT * H2] for a in (ssq, rn))
        own.frac, own.fsq, own.gate, own.y = (sb(f"f_{n}{u}", [P, S]) for n in ("frac", "fsq", "gate", "y"))
        signals.append(s)
        buffers.append(own)

    with nc.Block() as block:
        @block.vector
        def _(dve):
            for s, o in zip(signals, buffers):
                up(s.dve, dve.memset(o.xp[:], 0.0))
    clear(nc, signals)

    with nc.Fori(0, B // 2, 1) as b:
        x_pair = m.x[:, bass.ts(b, 2 * S)]
        o_pair = st.o[:, :, bass.ts(b, 2), :]
        g16 = lambda a: a.rearrange("p t (h c) -> p (t h) c", h=H2)
        with nc.Block() as block:
            @block.tensor
            def _(pe):
                def program(u):
                    s, o, ps, norm, k0 = signals[u], buffers[u], m.ps, Norm(m, signals, u), 4 * u
                    yield from norm.pe(0, x_pair[:, u * S:(u + 1) * S], k0, k0 + 1)
                    pe.wait_ge(s.o_norm.sem, 1)
                    for t in range(NT):
                        last = pe.transpose(ps[:, k0 + 3, t * P:(t + 1) * P], o.on[:, t, :], m.ident[:])
                    up(s.o_turned, last)
                    yield
                    pe.wait_ge(s.ln_done.sem, 1)
                    up(s.gate_ready, pe.matmul(ps[:, k0 + 2, :], m.c_gate_w[:], o.xn, start=True, stop=True))
                    yield
                    pe.wait_ge(s.o_t.sem, 1)
                    up(s.core_ready, pe.matmul(ps[:, k0 + 3, :], m.c_wo[:], o.oT[:], start=True, stop=True))
                    yield
                    pe.wait_ge(s.frac_squared.sem, 1)
                    for t in range(NT):
                        last = pe.matmul(ps[:, k0, t:t + 1], o.fsq[:, t * P:(t + 1) * P], m.mean_col[:, 0:1],
                                         start=True, stop=True)
                    up(s.frac_var, last)
                    yield
                    pe.wait_ge(s.frac_diag.sem, 1)
                    up(s.frac_spread, pe.matmul(ps[:, k0 + 1, :], m.ones[:], norm.diag[:], start=True, stop=True))
                    yield
                    pe.wait_ge(s.y_ready.sem, 1)
                    yield from norm.pe(1, o.y[:], k0, k0 + 1)

                in_turn(program(0), program(1))

            @block.scalar
            def _(act):
                def program(u):
                    s, o, ps, norm, k0 = signals[u], buffers[u], m.ps, Norm(m, signals, u), 4 * u
                    act.activation(o.osq[:], o_pair[:, :, u, :], ACT.Square).then_inc(s.squared.sem, 1)
                    yield
                    yield from norm.act(0, k0)
                    act.wait_ge(s.o_turned.sem, 1)
                    act.activation(o.oT[:], ps[:, k0 + 3, :], ACT.Copy).then_inc(s.o_t.sem, 1)
                    yield
                    act.wait_ge(s.gate_ready.sem, 1)
                    act.activation(o.gate[:], ps[:, k0 + 2, :], ACT.Sigmoid,
                                   bias=m.c_gate_b[:, 0:1]).then_inc(s.gate_done.sem, 1)
                    yield
                    act.wait_ge(s.frac.sem, DILATIONS + 1)
                    act.activation(o.fsq[:], o.frac[:], ACT.Square).then_inc(s.frac_squared.sem, 1)
                    yield
                    yield from norm.act(1, k0)

                in_turn(program(0), program(1))

            @block.vector
            def _(dve):
                def program(u):
                    s, o, ps, norm, k0 = signals[u], buffers[u], m.ps, Norm(m, signals, u), 4 * u
                    o_b = o_pair[:, :, u, :]
                    dve.wait_ge(s.squared.sem, 1)
                    link(dve, s.dve, dve.tensor_reduce(o.ssq, g16(o.osq[:]), AX.X, ALU.add))
                    up(s.dve, dve.tensor_scalar(o.ssq, o.ssq, 1.0 / HD2, 1e-5, ALU.mult, ALU.add))
                    rsqrt_of_both(dve, signals, u, ssq[:], rn[:], rn_t[:])
                    yield
                    for t in range(NT):
                        last = dve.tensor_tensor(o.on[:, t, :].rearrange("p (h c) -> p h c", h=H2),
                                                 o_b[:, t, :].rearrange("p (h c) -> p h c", h=H2),
                                                 o.rn[:, t * H2:(t + 1) * H2].unsqueeze(2).to_broadcast([P, H2, HD2]),
                                                 ALU.mult)
                        if t < NT - 1:
                            up(s.dve, last)
                    up(s.o_norm, last)
                    yield
                    yield from norm.dve(0, k0 + 1, o.xn)
                    dve.wait_ge(s.ln_done.sem, 1)
                    up(s.frac, dve.tensor_scalar(o.frac[:], o.xn, m.c_frac_own[:, 0:1], None, ALU.mult))
                    for i in range(DILATIONS):
                        dve.wait_ge(s.frac.sem, i + 1)
                        up(s.frac, dve.scalar_tensor_tensor(out=o.frac[:], in0=o.xp[:, PAD - 2 ** i:PAD - 2 ** i + S],
                                                            scalar=m.c_frac_w[:, i, 0:1], in1=o.frac[:], op0=ALU.mult,
                                                            op1=ALU.add))
                    yield
                    dve.wait_ge(s.frac_var.sem, 1)
                    up(s.frac_diag, (yield from norm.inverse_root(1e-5, ps[:, k0, 0:NT])))
                    yield
                    dve.wait_ge(s.dve.sem, s.dve.n)
                    dve.wait_ge(s.frac_spread.sem, 1)
                    link(dve, s.dve, dve.scalar_tensor_tensor(out=o.frac[:], in0=o.frac[:], scalar=m.c_mix_w[:, 0:1],
                                                              in1=ps[:, k0 + 1, :], op0=ALU.mult, op1=ALU.mult))
                    dve.wait_ge(s.gate_done.sem, 1)
                    link(dve, s.dve, dve.tensor_tensor(o.frac[:], o.frac[:], o.gate[:], ALU.mult))
                    dve.wait_ge(s.core_ready.sem, 1)
                    up(s.y_ready, dve.tensor_tensor(o.y[:], o.frac[:], ps[:, k0 + 3, :], ALU.add))
                    yield
                    yield from norm.dve(1, k0 + 1, o.y[:])
                    dve.wait_ge(s.ln_done.sem, 2)
                    x_b = x_pair[:, u * S:(u + 1) * S]
                    up(s.dve, dve.tensor_tensor(x_b, x_b, o.y[:], ALU.add))

                in_turn(program(0), program(1))
        clear(nc, signals)


def gated_block(m, ctx):
    nc = m.nc
    sb = lambda name, shape, dt=F32: ctx.enter_context(nc.sbuf_tensor(name, shape, dt))
    signals, buffers = [], []
    for u in range(2):
        s, own = Signals(nc, ctx, u), Store()
        (s.gu_ready, s.gate_done, s.silu_done, s.h_done, s.y_ready, s.y_copied) = s.new(
            "gu_ready gate_done silu_done h_done y_ready y_copied")
        own.xn, own.y = sb(f"d_xn{u}", [P, S]), sb(f"d_y{u}", [P, S])
        own.sg, own.gated = sb(f"d_sg{u}", [P, 2, S]), sb(f"d_gated{u}", [P, 2, S])
        own.h = sb(f"d_h{u}", [P, HCH3, S])
        signals.append(s)
        buffers.append(own)

    with nc.Fori(0, B // 2, 1) as b:
        x_pair = m.x[:, bass.ts(b, 2 * S)]
        with nc.Block() as block:
            @block.tensor
            def _(pe):
                def program(u):
                    s, o, ps, norm, k0 = signals[u], buffers[u], m.ps, Norm(m, signals, u), 4 * u
                    yield from norm.pe(0, x_pair[:, u * S:(u + 1) * S], k0, k0 + 1)
                    pe.wait_ge(s.ln_done.sem, 1)
                    for c in range(HCH3):
                        if c == 2:
                            pe.wait_ge(s.h_done.sem, 1)
                        hid, bank = slice(c * P, (c + 1) * P), k0 + 2 * (c % 2)
                        pe.matmul(ps[:, bank, :], m.d_gate[:, hid], o.xn[:], start=True, stop=True)
                        up(s.gu_ready, pe.matmul(ps[:, bank + 1, :], m.d_up[:, hid], o.xn[:], start=True, stop=True))
                        yield
                    for c in range(HCH3):
                        pe.wait_ge(s.h_done.sem, max(c + 1, 2))
                        last = pe.matmul(ps[:, k0 + 2, :], m.d_down[:, c, :], o.h[:, c, :],
                                         start=c == 0, stop=c == HCH3 - 1)
                        yield
                    up(s.y_ready, last)
                    yield
                    pe.wait_ge(s.y_copied.sem, 1)
                    yield from norm.pe(1, o.y[:], k0, k0 + 1)

                in_turn(program(0), program(1))

            @block.scalar
            def _(act):
                def program(u):
                    s, o, ps, norm, k0 = signals[u], buffers[u], m.ps, Norm(m, signals, u), 4 * u
                    yield from norm.act(0, k0)
                    for c in range(HCH3):
                        act.wait_ge(s.gu_ready.sem, c + 1)
                        if c == 2:
                            act.wait_ge(s.silu_done.sem, 1)
                        act.activation(o.sg[:, c % 2, :], ps[:, k0 + 2 * (c % 2), :],
                                       ACT.Sigmoid).then_inc(s.gate_done.sem, 1)
                        yield
                    act.wait_ge(s.y_ready.sem, 1)
                    act.activation(o.y[:], ps[:, k0 + 2, :], ACT.Copy).then_inc(s.y_copied.sem, 1)
                    yield
                    yield from norm.act(1, k0)

                in_turn(program(0), program(1))

            @block.vector
            def _(dve):
                def program(u):
                    s, o, ps, norm, k0 = signals[u], buffers[u], m.ps, Norm(m, signals, u), 4 * u
                    yield from norm.dve(0, k0 + 1, o.xn[:])
                    for c in range(HCH3):
                        bank = k0 + 2 * (c % 2)
                        dve.wait_ge(s.gate_done.sem, c + 1)
                        if c == 2:
                            dve.wait_ge(s.h_done.sem, 1)
                        up(s.silu_done, dve.tensor_tensor(o.gated[:, c % 2, :], o.sg[:, c % 2, :], ps[:, bank, :],
                                                          ALU.mult))
                        dve.wait_ge(s.silu_done.sem, c + 1)
                        up(s.h_done, dve.tensor_tensor(o.h[:, c, :], o.gated[:, c % 2, :], ps[:, bank + 1, :], ALU.mult))
                        yield
                    yield from norm.dve(1, k0 + 1, o.y[:])
                    dve.wait_ge(s.ln_done.sem, 2)
                    x_b = x_pair[:, u * S:(u + 1) * S]
                    up(s.dve, dve.tensor_tensor(x_b, x_b, o.y[:], ALU.add))

                in_turn(program(0), program(1))
        clear(nc, signals)


def local_weights(m, ctx, ins):
    sa = lambda name, shape, dt=F32: ctx.enter_context(m.nc.sbuf_tensor(name, shape, dt))
    loads = []

    def load(dst, src):
        loads.append((dst[:], src))
        return dst

    m.layer = []
    for l in range(L1):
        w = Store()
        w.wqkv = load(sa(f"b_wqkv{l}", [P, 3 * INNER]), ins["b_wqkv"][l])
        w.wo = load(sa(f"b_wo{l}", [P, 4, P]), ins["b_wo"][l])
        w.w1 = load(sa(f"b_w1{l}", [P, 2 * HID1]), ins["b_w1"][l])
        w.w2 = load(sa(f"b_w2{l}", [P, 3, P]), ins["b_w2"][l])
        w.b1 = load(sa(f"b_b1{l}", [P, 6]), ins["b_b1"][l])
        w.b2, w.ln_g, w.ln_b = (load(sa(f"b_{n}{l}", [P, 1]), ins["b_" + n][l])
                                for n in ("b2", "ln_g", "ln_b"))
        w.tab_direct = load(sa(f"b_direct{l}", [P, NT, 2, HD1]), ins["b_direct"])
        w.tab_swap = load(sa(f"b_swap{l}", [P, NT, 2, HD1]), ins["b_swap"])
        w.qk_scale = sa(f"b_qk_scale{l}", [P, 2, HD1])
        for j, n in enumerate(("b_q_scale", "b_k_scale")):
            loads.append((w.qk_scale[:, j, :], ins[n][l].partition_broadcast(P)))
        m.layer.append(w)
    m.mask = load(sa("b_mask", [P, 3 * WIN], BF16), ins["b_mask"])
    return loads


def build(nc, ins, out, blocks=range(4)):
    with ExitStack() as ctx:
        m = Store()
        m.nc = nc
        sb = lambda name, shape, dt=F32: ctx.enter_context(nc.sbuf_tensor(name, shape, dt))
        m.ps = ctx.enter_context(nc.psum_tensor("ps", [P, 8, S], F32))
        m.x = sb("x", [P, B * S])
        m.var, m.rstd, m.tmp = (sb(f"ln_{name}", [P, 2 * NT]) for name in ("var", "rstd", "tmp"))
        m.norm_buffers = []
        for u in range(2):
            n = Store()
            n.both = sb(f"ln_both{u}", [P, 2, S])
            n.lnc, n.lnsq, n.diag = n.both[:, 0, :], n.both[:, 1, :], sb(f"ln_diag{u}", [P, S])
            m.norm_buffers.append(n)
        m.loaded = ctx.enter_context(nc.semaphore("loaded"))
        m.loaded_b = ctx.enter_context(nc.semaphore("loaded_b"))
        loaded_d = ctx.enter_context(nc.semaphore("loaded_d"))
        ready_d = ctx.enter_context(nc.semaphore("ready_d"))
        loaded_c = ctx.enter_context(nc.semaphore("loaded_c"))
        ready_c = ctx.enter_context(nc.semaphore("ready_c"))
        chain_c = ctx.enter_context(nc.semaphore("chain_c"))
        stored = ctx.enter_context(nc.semaphore("stored"))
        small = {"ident": [P, P], "centre": [P, P], "ones": [P, P], "mean_col": [P, 1], "ones_rows": [P, 1]}
        m.ident, m.centre, m.ones, m.mean_col, m.ones_rows = (sb(n, shape) for n, shape in small.items())
        m.ident_bf = sb("ident_bf", [P, P], BF16)
        loads = [(t[:], ins[n]) for n, t in zip(small, (m.ident, m.centre, m.ones, m.mean_col, m.ones_rows))] + [(m.ident_bf[:], ins["ident_bf"])]

        with ExitStack() as both:
            second = local_weights(m, both, ins)
            m.loads_b = len(second)
            with ExitStack() as own:
                sa = lambda name, shape, dt=F32: own.enter_context(nc.sbuf_tensor(name, shape, dt))

                def taken(n, shape):
                    dst = sa("a_" + n, shape)
                    loads.append((dst[:], ins["a_" + n]))
                    return dst

                m.wq, m.wk, m.wv, m.wo = (taken(n, [P, P]) for n in ("wq", "wk", "wv", "wo"))
                m.bq, m.bk, m.bo = (taken(n, [P, 1]) for n in ("bq", "bk", "bo"))
                m.bv = sa("a_bv", [P, P])
                loads.append((m.bv[:], ins["a_bv"].partition_broadcast(P)))
                m.bq_scaled = sa("a_bq_scaled", [P, 1])
                m.sel = sa("a_sel", [P, 2, NPAIR, 3, P], BF16)
                loads.append((m.sel[:], ins["a_sel"]))
                m.loads = len(loads) + 1

                def start(block):
                    @block.sync
                    def _(sp):
                        for dst, src in loads:
                            sp.dma_start(dst, src).then_inc(m.loaded, 16)
                        for dst, src in second:
                            sp.dma_start(dst, src).then_inc(m.loaded_b, 16)

                    @block.scalar
                    def _(act):
                        act.dma_start(m.x[:], ins["xT"]).then_inc(m.loaded, 16)

                m.start = start
                if 0 in blocks:
                    attention_block(m, own)
                else:
                    with nc.Block() as block:
                        start(block)

                        @block.vector
                        def _(dve):
                            dve.wait_ge(m.loaded, 16 * m.loads)
            if 1 in blocks:
                with ExitStack() as own:
                    local_block(m, own)
        if 2 in blocks:
            with ExitStack() as own:
                sa = lambda name, shape, dt=F32: own.enter_context(nc.sbuf_tensor(name, shape, dt))
                todo = []

                def load(name, shape, src=None):
                    dst = sa(name, shape)
                    todo.append((dst[:], ins[name] if src is None else src))
                    return dst

                m.c_wbg, m.c_chunk_mean = load("c_wbg", [P, 8]), load("c_chunk_mean", [P, 4])
                m.c_level, m.c_first = load("c_level", [P, LEVELS, P]), load("c_first", [P, 2, P])
                m.c_causal, m.c_cos, m.c_sin = load("c_causal", [P, P]), load("c_cos", [P, S]), load("c_sin", [P, S])
                m.c_wo, m.c_o_norm = load("c_wo", [P, P]), load("c_o_norm", [P, 1])
                m.c_gate_b = load("c_gate_b", [P, 1], ins["c_gate_b"].partition_broadcast(P))
                m.c_gate_col, m.c_mix_w = load("c_gate_col", [P, 1]), load("c_mix_w", [P, 1])
                m.c_frac_w = load("c_frac_w", [P, DILATIONS, 2])
                m.c_rot = load("c_rot", [P, H2], ins["c_rot"].partition_broadcast(P))
                m.c_taps, m.c_share, m.c_gate_w = sa("c_taps", [P, 3, TAPS, P]), sa("c_share", [P, S]), sa("c_gate_w", [P, P])
                m.c_frac_own = sa("c_frac_own", [P, 1])
                st = Store()
                st.wT, st.qT, st.k, st.u, st.o = (sa("st_" + n, [P, NT, B, P]) for n in ("wT", "qT", "k", "u", "o"))
                st.g = sa("st_g", [P, NT, B, 4])
                with ExitStack() as once:
                    so = lambda name, shape: once.enter_context(nc.sbuf_tensor(name, shape, F32))
                    w3, conv = so("c_w3", [P, 3, P]), so("c_conv", [P, 3, TAPS, P])
                    mix, share = so("c_mix", [P, H2]), so("c_share4", [P, H2])
                    todo += [(w3[:], ins["c_w3"]), (conv[:], ins["c_conv"].partition_broadcast(P))]
                    with nc.Block() as block:
                        @block.sync
                        def _(sp):
                            for dst, src in todo:
                                sp.dma_start(dst, src).then_inc(loaded_c, 16)

                        @block.scalar
                        def _(act):
                            act.wait_ge(loaded_c, 16 * len(todo))
                            act.activation(mix[:], m.c_rot[:], ACT.Sigmoid).then_inc(ready_c, 1)

                        @block.vector
                        def _(dve):
                            c = Count(chain_c)
                            dve.wait_ge(loaded_c, 16 * len(todo))
                            for j in range(3):
                                for tap in range(TAPS):
                                    up(c, dve.tensor_tensor(m.c_taps[:, j, tap, :], w3[:, j, :], conv[:, j, tap, :],
                                                            ALU.mult))
                            up(c, dve.tensor_scalar(m.c_gate_w[:], m.ones[:], m.c_gate_col[:, 0:1], None, ALU.mult))
                            up(c, dve.tensor_scalar(m.c_wo[:], m.c_wo[:], m.c_o_norm[:, 0:1], None, ALU.mult))
                            link(dve, c, dve.tensor_reduce(m.c_frac_own[:], m.c_frac_w[:, :, 1], AX.X, ALU.add))
                            up(c, dve.tensor_scalar(m.c_frac_own[:], m.c_frac_own[:], 2.0, None, ALU.add))
                            dve.wait_ge(ready_c, 1)
                            link(dve, c, dve.tensor_scalar(share[:], mix[:], -1.0, 1.0, ALU.mult, ALU.add))
                            link(dve, c, dve.memset(m.c_share[:], 1.0))
                            wide = lambda a: a[:].unsqueeze(2).to_broadcast([P, H2, HD2])
                            for tab, by in ((m.c_cos, mix), (m.c_sin, mix), (m.c_share, share)):
                                for t in range(NT):
                                    part = tab[:, t * P:(t + 1) * P].rearrange("p (h c) -> p h c", h=H2)
                                    up(c, dve.tensor_tensor(part, part, wide(by), ALU.mult))
                with ExitStack() as own1:
                    delta_prepare(m, own1, st)
                with ExitStack() as own2:
                    delta_scan(m, own2, st)
                with ExitStack() as own3:
                    delta_finish(m, own3, st)
        if 3 in blocks:
            with ExitStack() as own:
                sa = lambda name, shape, dt=F32: own.enter_context(nc.sbuf_tensor(name, shape, dt))
                ints = [(sa("d_gate_i", [P, HID3], I32), ins["d_gate"]), (sa("d_up_i", [P, HID3], I32), ins["d_up"]),
                        (sa("d_down_i", [P, HCH3, P], I32), ins["d_down"])]
                m.d_gate, m.d_up = sa("d_gate", [P, HID3]), sa("d_up", [P, HID3])
                m.d_down = sa("d_down", [P, HCH3, P])
                with nc.Block() as block:
                    @block.sync
                    def _(sp):
                        for dst, src in ints:
                            sp.dma_start(dst[:], src).then_inc(loaded_d, 16)

                    @block.vector
                    def _(dve):
                        dve.wait_ge(loaded_d, 16 * len(ints))
                        for dst, (src, _) in zip((m.d_gate, m.d_up, m.d_down), ints):
                            dve.tensor_scalar(dst[:], src[:], DEQUANT, None, ALU.mult).then_inc(ready_d, 1)
                gated_block(m, own)
        with nc.Block() as block:
            @block.sync
            def _(sp):
                sp.dma_start(out, m.x[:]).then_inc(stored, 16)
                sp.wait_ge(stored, 16)


def rotary_tables():
    f32 = np.float32
    half = np.arange(0, HD1, 2, dtype=f32)
    t = np.arange(S, dtype=f32)
    freqs = t[:, None] * (f32(1.0) / f32(10000.0) ** (half / f32(HD1)))[None, :]
    base = (half + f32(0.4 * HD1)) / f32(1.4 * HD1)
    scale = base[None, :] ** ((t - S // 2) / f32(WIN // 2))[:, None]
    direct, swap = np.zeros((S, 2, HD1), f32), np.zeros((S, 2, HD1), f32)
    for j, sc in enumerate((scale, 1.0 / scale)):
        direct[:, j] = np.concatenate([np.cos(freqs) * sc] * 2, axis=1)
        swap[:, j] = np.concatenate([-np.sin(freqs) * sc, np.sin(freqs) * sc], axis=1)
    tiles = lambda a: a.reshape(NT, P, 2, HD1).transpose(1, 0, 2, 3)
    return tiles(direct), tiles(swap)


def layout(inputs):
    f = {n: np.asarray(a) for n, a in inputs.items()}
    col = lambda a: np.ascontiguousarray(a).reshape(-1, 1)
    eye = np.eye(P, dtype=np.float32)
    bf16 = mybir.dt.np(BF16)
    d = {"xT": f["L0_attn_hidden_states"].reshape(B * S, P).T,
         "ident": eye, "centre": eye - np.float32(1.0 / P), "ones": np.ones((P, P), np.float32),
         "mean_col": np.full((P, 1), 1.0 / P, np.float32), "ident_bf": eye.astype(bf16)}
    for n in ("q", "k", "v", "o"):
        d["a_w" + n] = f["L0_attn_W" + n].T
    for n in ("q", "k", "o"):
        d["a_b" + n] = col(f["L0_attn_b" + n])
    d["a_bv"] = f["L0_attn_bv"]
    sel = np.zeros((P, 2, NPAIR, 3, P), np.float32)
    for w, slots in enumerate((Q_PARTS, K_PARTS)):
        for p in range(NPAIR):
            for a in range(2):
                for slot, part in enumerate(slots):
                    for e in range(HD0):
                        sel[(2 * p + a) * HD0 + e, w, p, part, 64 * a + slot * HD0 + e] = 1.0
    d["a_sel"] = sel.astype(bf16)
    rows = np.zeros((P, 1), np.float32)
    for a in range(2):
        rows[64 * a + MAX_ROW:64 * a + MAX_ROW + 3] = 1.0
    d["ones_rows"] = rows
    d["b_wqkv"] = f["L0_ffn_wqkv"]
    d["b_wo"] = f["L0_ffn_wo"].reshape(L1, 4, P, P).transpose(0, 2, 1, 3)
    d["b_w1"] = f["L0_ffn_w1"]
    w2 = np.zeros((L1, P, 3, P), np.float32)
    b1 = np.zeros((L1, P, 6), np.float32)
    for c, (c0, rows) in enumerate(HCH):
        w2[:, 0:rows, c, :] = f["L0_ffn_w2"][:, c0:c0 + rows, :]
        b1[:, 0:rows, c] = f["L0_ffn_b1"][:, c0:c0 + rows]
        b1[:, 0:rows, 3 + c] = f["L0_ffn_b1"][:, HID1 + c0:HID1 + c0 + rows]
    d["b_w2"], d["b_b1"] = w2, b1
    for n in ("b2", "ln_g", "ln_b"):
        d["b_" + n] = f["L0_ffn_" + n].reshape(L1, P, 1)
    d["b_q_scale"], d["b_k_scale"] = f["L0_ffn_q_scale"], f["L0_ffn_k_scale"]
    direct, swap = rotary_tables()
    d["b_direct"], d["b_swap"] = direct, swap
    q, k = np.arange(P)[:, None], np.arange(3 * WIN)[None, :] - WIN
    d["b_mask"] = np.where((k <= q) & (k >= q - WIN), 0.0, MASKED).astype(bf16)
    d["c_wbg"] = np.concatenate([f["L1_attn_Wb"], f["L1_attn_Wgamma"]], axis=1)
    i, j = np.arange(P)[:, None], np.arange(P)[None, :]
    same = i // CHUNK == j // CHUNK
    d["c_chunk_mean"] = (i // CHUNK == np.arange(4)[None, :]) / np.float32(CHUNK)
    below = lambda half: (i // (2 * half) == j // (2 * half)) & (i % (2 * half) >= half) & (j % (2 * half) < half)
    d["c_level"] = np.stack([-below(2 ** (1 + n)).T.astype(np.float32) for n in range(LEVELS)], axis=1)
    d["c_first"] = np.stack([-below(1).astype(np.float32), -below(1).T.astype(np.float32)], axis=1)
    d["c_causal"] = (same & (i <= j)).astype(np.float32)
    inv = np.float32(1.0) / np.float32(10000.0) ** (np.arange(0, HD2, 2, dtype=np.float32) / np.float32(HD2))
    ang = np.arange(S, dtype=np.float32)[:, None] * inv[None, :]
    for n, halves in (("c_cos", (np.cos(ang), np.cos(ang))), ("c_sin", (-np.sin(ang), np.sin(ang)))):
        one = np.concatenate(halves, axis=1).reshape(NT, P, 1, HD2)
        d[n] = np.broadcast_to(one, (NT, P, H2, HD2)).transpose(1, 0, 2, 3).reshape(P, S)
    d["c_wo"], d["c_o_norm"] = f["L1_attn_Wo"], col(np.tile(f["L1_attn_o_norm_w"], H2))
    d["c_gate_b"], d["c_gate_col"] = f["L1_attn_frac_gate_b"], col(f["L1_attn_frac_gate_w"])
    d["c_frac_w"] = f["L1_attn_frac_conv_w"].transpose(1, 0, 2)
    d["c_mix_w"], d["c_rot"] = col(f["L1_attn_mixer_norm_w"]), f["L1_attn_rot_logit"]
    d["c_w3"] = np.stack([f["L1_attn_W" + n] for n in "qkv"], axis=1)
    d["c_conv"] = np.stack([f["L1_attn_conv_" + n].T for n in "qkv"], axis=0)
    for n in d:
        if n.startswith("c_"):
            d[n] = d[n].astype(np.float32)
    d["d_gate"], d["d_up"] = f["L1_ffn_w_gate"].T, f["L1_ffn_w_up"].T
    d["d_down"] = f["L1_ffn_w_down"].T.reshape(HCH3, P, P).transpose(1, 0, 2)
    return {n: np.ascontiguousarray(a) for n, a in d.items()}


def kernel(**inputs):
    import concourse.bacc as bacc
    from concourse.bass_utils import run_bass_kernel_spmd

    arrays = layout(inputs)
    nc = bacc.Bacc("TRN2", target_bir_lowering=False, num_devices=1)
    ins = {n: nc.dram_tensor("in_" + n, a.shape, mybir.dt.from_np(a.dtype), kind="ExternalInput").ap()
           for n, a in arrays.items()}
    out = nc.dram_tensor("out_xT", (P, B * S), F32, kind="ExternalOutput").ap()
    build(nc, ins, out)
    r = run_bass_kernel_spmd(nc, [{"in_" + n: a for n, a in arrays.items()}], core_ids=[0])
    xT = np.asarray(r.results[0]["out_xT"])
    return np.ascontiguousarray(xT.T).reshape(B, S, P)
```
